# Optimizing a Trainium2 kernel written in Bass

```python
import numpy as np
import jax
import jax.numpy as jnp

def _softmax(x, axis=-1):
    return jax.nn.softmax(x, axis=axis)

def _gelu(x):
    return jax.nn.gelu(x, approximate=True)

def _silu(x):
    return jax.nn.silu(x)

def _sigmoid(x):
    return jax.nn.sigmoid(x)

def _layernorm(x, axis=-1, eps=1e-05):
    m = jnp.mean(x, axis=axis, keepdims=True)
    v = jnp.var(x, axis=axis, keepdims=True)
    return (x - m) / jnp.sqrt(v + eps)

def _scatter_add(tgt, idx, src, axis=0):
    return tgt.at[idx].add(src)

def _segment_sum(src, seg, n):
    return jax.ops.segment_sum(src, seg, n)
kernel_name = 'mk_xattn_seq_d1_seqx_r2_6139e0'

def setup_inputs(seed: int=0):
    np.random.seed(seed)
    _w = jnp.asarray

    def _rec_inputs():
        import jax
        import jax.numpy as jnp
        _rk = jax.random.key(seed)
        x = -0.0002928 + 1 * jax.random.normal(jax.random.fold_in(_rk, 1), (4, 1024, 512), jnp.float32)
        _lenS = 1024 - jax.random.randint(jax.random.fold_in(_rk, 7), (4,), 0, max(1, 1024 // 4) + 1, jnp.int32)
        _lenS2 = 1024 - jax.random.randint(jax.random.fold_in(_rk, 8), (4,), 0, max(1, 1024 // 4) + 1, jnp.int32)
        _ctx_1024P = jax.random.normal(jax.random.fold_in(_rk, 11), (4, 16, 512), jnp.float32)
        _ctx_1024c = jax.random.dirichlet(jax.random.fold_in(_rk, 511), 0.3 * jnp.ones((16,), jnp.float32), (4, 1024))
        _ctx_1024t = jnp.einsum('bsk,bkd->bsd', _ctx_1024c, _ctx_1024P)
        _ctx_1024t = _ctx_1024t * jax.lax.rsqrt(jnp.mean(jnp.square(_ctx_1024t)) + 1e-12) * 0.953939
        ctx_1024 = -0.000514642 + 1.00011 * (_ctx_1024t + 0.3 * jax.random.normal(jax.random.fold_in(_rk, 611), (4, 1024, 512), jnp.float32))
        return (x, ctx_1024)
    x, ctx_1024 = _rec_inputs()

    def _L0_xattn_setup():
        import jax, jax.numpy as jnp
        import numpy as np
        D_MODEL = 512
        N_HEADS = 16
        D_FF = 2048
        BLOCK = 64
        ROUTER_H = 128
        NEG = -1000000000.0

        def _layernorm(x, g, b, eps=1e-05):
            mu = x.mean(-1, keepdims=True)
            var = ((x - mu) ** 2).mean(-1, keepdims=True)
            return (x - mu) * jax.lax.rsqrt(var + eps) * g + b

        def _block_sparse_self_attn(x, qkv_w, sa_out_w, sa_out_b, r_w1, r_b1, r_w2, r_b2):
            B, S, D = x.shape
            H, Dh = (N_HEADS, D // N_HEADS)
            nb = S // BLOCK
            qkv = x @ qkv_w.T
            q, k, v = jnp.split(qkv, 3, axis=-1)
            q = q.reshape(B, S, H, Dh).transpose(0, 2, 1, 3)
            kh = k.reshape(B, S, H, Dh).transpose(0, 2, 1, 3)
            vh = v.reshape(B, S, H, Dh).transpose(0, 2, 1, 3)
            scores = jnp.einsum('bhqd,bhkd->bhqk', q, kh) / jnp.sqrt(jnp.float32(D))
            block_repr = k.reshape(B, nb, BLOCK, D).mean(axis=2)
            r = jax.nn.relu(block_repr @ r_w1.T + r_b1) @ r_w2.T + r_b2
            keep0 = jax.nn.sigmoid(r[0, :, 0]) > 0.5
            allowed = keep0[:, None] & keep0[None, :]
            allowed_pos = jnp.repeat(jnp.repeat(allowed, BLOCK, 0), BLOCK, 1)
            scores = jnp.where(allowed_pos[None, None], scores, NEG)
            causal = jnp.triu(jnp.ones((S, S), bool), k=1)
            scores = jnp.where(causal[None, None], -jnp.inf, scores)
            p = jax.nn.softmax(scores, axis=-1)
            out = jnp.einsum('bhqk,bhkd->bhqd', p, vh)
            out = out.transpose(0, 2, 1, 3).reshape(B, S, D)
            return out @ sa_out_w.T + sa_out_b

        def _mha_cross(q_in, kv_in, in_w, in_b, out_w, out_b):
            B, S, D = q_in.shape
            M = kv_in.shape[1]
            H, Dh = (N_HEADS, D // N_HEADS)
            wq, wk, wv = jnp.split(in_w, 3, axis=0)
            bq, bk, bv = jnp.split(in_b, 3, axis=0)
            q = (q_in @ wq.T + bq).reshape(B, S, H, Dh).transpose(0, 2, 1, 3)
            k = (kv_in @ wk.T + bk).reshape(B, M, H, Dh).transpose(0, 2, 1, 3)
            v = (kv_in @ wv.T + bv).reshape(B, M, H, Dh).transpose(0, 2, 1, 3)
            scores = jnp.einsum('bhqd,bhkd->bhqk', q, k) / jnp.sqrt(jnp.float32(Dh))
            p = jax.nn.softmax(scores, axis=-1)
            out = jnp.einsum('bhqk,bhkd->bhqd', p, v).transpose(0, 2, 1, 3).reshape(B, S, D)
            return out @ out_w.T + out_b
        key = jax.random.key(seed)
        ks = jax.random.split(key, 24)
        B, S, M, D = (2, 1024, 512, D_MODEL)
        s = lambda k, shape, fan: jax.random.normal(k, shape, jnp.float32) * (1.0 / np.sqrt(fan))
        return {'tgt': jax.random.normal(ks[0], (B, S, D), jnp.float32), 'memory': jax.random.normal(ks[1], (B, M, D), jnp.float32), 'qkv_w': s(ks[2], (3 * D, D), D), 'sa_out_w': s(ks[3], (D, D), D), 'sa_out_b': jnp.zeros((D,), jnp.float32), 'r_w1': s(ks[4], (ROUTER_H, D), D), 'r_b1': jnp.zeros((ROUTER_H,), jnp.float32), 'r_w2': s(ks[5], (1, ROUTER_H), ROUTER_H), 'r_b2': jnp.zeros((1,), jnp.float32), 'ca_in_w': s(ks[6], (3 * D, D), D), 'ca_in_b': jnp.zeros((3 * D,), jnp.float32), 'ca_out_w': s(ks[7], (D, D), D), 'ca_out_b': jnp.zeros((D,), jnp.float32), 'ff_w1': s(ks[8], (D_FF, D), D), 'ff_b1': jnp.zeros((D_FF,), jnp.float32), 'ff_w2': s(ks[9], (D, D_FF), D_FF), 'ff_b2': jnp.zeros((D,), jnp.float32), 'n1_g': jnp.ones((D,), jnp.float32), 'n1_b': jnp.zeros((D,), jnp.float32), 'n2_g': jnp.ones((D,), jnp.float32), 'n2_b': jnp.zeros((D,), jnp.float32), 'n3_g': jnp.ones((D,), jnp.float32), 'n3_b': jnp.zeros((D,), jnp.float32)}
    _L0_xattn_all = _L0_xattn_setup()
    _L0_xattn_in = {k: v for k, v in _L0_xattn_all.items() if k in ('qkv_w', 'sa_out_w', 'sa_out_b', 'r_w1', 'r_b1', 'r_w2', 'r_b2', 'ca_in_w', 'ca_in_b', 'ca_out_w', 'ca_out_b', 'ff_w1', 'ff_b1', 'ff_w2', 'ff_b2', 'n1_g', 'n1_b', 'n2_g', 'n2_b', 'n3_g', 'n3_b')}
    del _L0_xattn_all
    return {'x': x, 'ctx_1024': ctx_1024, 'L0_xattn_qkv_w': _L0_xattn_in['qkv_w'], 'L0_xattn_sa_out_w': _L0_xattn_in['sa_out_w'], 'L0_xattn_sa_out_b': _L0_xattn_in['sa_out_b'], 'L0_xattn_r_w1': _L0_xattn_in['r_w1'], 'L0_xattn_r_b1': _L0_xattn_in['r_b1'], 'L0_xattn_r_w2': _L0_xattn_in['r_w2'], 'L0_xattn_r_b2': _L0_xattn_in['r_b2'], 'L0_xattn_ca_in_w': _L0_xattn_in['ca_in_w'], 'L0_xattn_ca_in_b': _L0_xattn_in['ca_in_b'], 'L0_xattn_ca_out_w': _L0_xattn_in['ca_out_w'], 'L0_xattn_ca_out_b': _L0_xattn_in['ca_out_b'], 'L0_xattn_ff_w1': _L0_xattn_in['ff_w1'], 'L0_xattn_ff_b1': _L0_xattn_in['ff_b1'], 'L0_xattn_ff_w2': _L0_xattn_in['ff_w2'], 'L0_xattn_ff_b2': _L0_xattn_in['ff_b2'], 'L0_xattn_n1_g': _L0_xattn_in['n1_g'], 'L0_xattn_n1_b': _L0_xattn_in['n1_b'], 'L0_xattn_n2_g': _L0_xattn_in['n2_g'], 'L0_xattn_n2_b': _L0_xattn_in['n2_b'], 'L0_xattn_n3_g': _L0_xattn_in['n3_g'], 'L0_xattn_n3_b': _L0_xattn_in['n3_b']}

def reference(x, ctx_1024, L0_xattn_qkv_w, L0_xattn_sa_out_w, L0_xattn_sa_out_b, L0_xattn_r_w1, L0_xattn_r_b1, L0_xattn_r_w2, L0_xattn_r_b2, L0_xattn_ca_in_w, L0_xattn_ca_in_b, L0_xattn_ca_out_w, L0_xattn_ca_out_b, L0_xattn_ff_w1, L0_xattn_ff_b1, L0_xattn_ff_w2, L0_xattn_ff_b2, L0_xattn_n1_g, L0_xattn_n1_b, L0_xattn_n2_g, L0_xattn_n2_b, L0_xattn_n3_g, L0_xattn_n3_b):
    import jax
    import jax.numpy as jnp

    def _L0_xattn_ref(tgt, memory, qkv_w, sa_out_w, sa_out_b, r_w1, r_b1, r_w2, r_b2, ca_in_w, ca_in_b, ca_out_w, ca_out_b, ff_w1, ff_b1, ff_w2, ff_b2, n1_g, n1_b, n2_g, n2_b, n3_g, n3_b):
        import jax, jax.numpy as jnp
        import numpy as np
        D_MODEL = 512
        N_HEADS = 16
        D_FF = 2048
        BLOCK = 64
        ROUTER_H = 128
        NEG = -1000000000.0

        def _layernorm(x, g, b, eps=1e-05):
            mu = x.mean(-1, keepdims=True)
            var = ((x - mu) ** 2).mean(-1, keepdims=True)
            return (x - mu) * jax.lax.rsqrt(var + eps) * g + b

        def _block_sparse_self_attn(x, qkv_w, sa_out_w, sa_out_b, r_w1, r_b1, r_w2, r_b2):
            B, S, D = x.shape
            H, Dh = (N_HEADS, D // N_HEADS)
            nb = S // BLOCK
            qkv = x @ qkv_w.T
            q, k, v = jnp.split(qkv, 3, axis=-1)
            q = q.reshape(B, S, H, Dh).transpose(0, 2, 1, 3)
            kh = k.reshape(B, S, H, Dh).transpose(0, 2, 1, 3)
            vh = v.reshape(B, S, H, Dh).transpose(0, 2, 1, 3)
            scores = jnp.einsum('bhqd,bhkd->bhqk', q, kh) / jnp.sqrt(jnp.float32(D))
            block_repr = k.reshape(B, nb, BLOCK, D).mean(axis=2)
            r = jax.nn.relu(block_repr @ r_w1.T + r_b1) @ r_w2.T + r_b2
            keep0 = jax.nn.sigmoid(r[0, :, 0]) > 0.5
            allowed = keep0[:, None] & keep0[None, :]
            allowed_pos = jnp.repeat(jnp.repeat(allowed, BLOCK, 0), BLOCK, 1)
            scores = jnp.where(allowed_pos[None, None], scores, NEG)
            causal = jnp.triu(jnp.ones((S, S), bool), k=1)
            scores = jnp.where(causal[None, None], -jnp.inf, scores)
            p = jax.nn.softmax(scores, axis=-1)
            out = jnp.einsum('bhqk,bhkd->bhqd', p, vh)
            out = out.transpose(0, 2, 1, 3).reshape(B, S, D)
            return out @ sa_out_w.T + sa_out_b

        def _mha_cross(q_in, kv_in, in_w, in_b, out_w, out_b):
            B, S, D = q_in.shape
            M = kv_in.shape[1]
            H, Dh = (N_HEADS, D // N_HEADS)
            wq, wk, wv = jnp.split(in_w, 3, axis=0)
            bq, bk, bv = jnp.split(in_b, 3, axis=0)
            q = (q_in @ wq.T + bq).reshape(B, S, H, Dh).transpose(0, 2, 1, 3)
            k = (kv_in @ wk.T + bk).reshape(B, M, H, Dh).transpose(0, 2, 1, 3)
            v = (kv_in @ wv.T + bv).reshape(B, M, H, Dh).transpose(0, 2, 1, 3)
            scores = jnp.einsum('bhqd,bhkd->bhqk', q, k) / jnp.sqrt(jnp.float32(Dh))
            p = jax.nn.softmax(scores, axis=-1)
            out = jnp.einsum('bhqk,bhkd->bhqd', p, v).transpose(0, 2, 1, 3).reshape(B, S, D)
            return out @ out_w.T + out_b
        x = _layernorm(tgt, n1_g, n1_b)
        tgt = tgt + _block_sparse_self_attn(x, qkv_w, sa_out_w, sa_out_b, r_w1, r_b1, r_w2, r_b2)
        x = _layernorm(tgt, n2_g, n2_b)
        tgt = tgt + _mha_cross(x, memory, ca_in_w, ca_in_b, ca_out_w, ca_out_b)
        x = _layernorm(tgt, n3_g, n3_b)
        ff = jax.nn.relu(x @ ff_w1.T + ff_b1) @ ff_w2.T + ff_b2
        return tgt + ff
    x = _L0_xattn_ref(x, ctx_1024, L0_xattn_qkv_w, L0_xattn_sa_out_w, L0_xattn_sa_out_b, L0_xattn_r_w1, L0_xattn_r_b1, L0_xattn_r_w2, L0_xattn_r_b2, L0_xattn_ca_in_w, L0_xattn_ca_in_b, L0_xattn_ca_out_w, L0_xattn_ca_out_b, L0_xattn_ff_w1, L0_xattn_ff_b1, L0_xattn_ff_w2, L0_xattn_ff_b2, L0_xattn_n1_g, L0_xattn_n1_b, L0_xattn_n2_g, L0_xattn_n2_b, L0_xattn_n3_g, L0_xattn_n3_b)
    return x

_drawn_inputs = setup_inputs


def setup_inputs(seed=0):
    import zlib

    import numpy as np

    out = dict(_drawn_inputs(seed))
    spreads = {'L0_xattn_sa_out_b': (0.0, 0.1),
     'L0_xattn_r_b1': (0.0, 0.8),
     'L0_xattn_ca_in_b': (0.0, 0.1),
     'L0_xattn_ca_out_b': (0.0, 0.1),
     'L0_xattn_ff_b1': (0.0, 0.1),
     'L0_xattn_ff_b2': (0.0, 0.1),
     'L0_xattn_n1_g': (1.0, 0.6),
     'L0_xattn_n1_b': (0.0, 0.1),
     'L0_xattn_n2_g': (1.0, 0.2),
     'L0_xattn_n2_b': (0.0, 0.464),
     'L0_xattn_n3_g': (1.0, 0.2),
     'L0_xattn_n3_b': (0.0, 0.1)}
    factors = {'L0_xattn_r_w1': 2.759, 'L0_xattn_r_w2': 5.697}
    for name, (base, spread) in spreads.items():
        noise = np.random.default_rng([zlib.crc32(name.encode()), seed]).standard_normal(out[name].shape)
        drawn = base * np.exp(spread * noise) if base else spread * noise
        out[name] = jnp.asarray(drawn.astype(out[name].dtype))
    for name, factor in factors.items():
        out[name] = (out[name] * factor).astype(out[name].dtype)
    return out
```

```python
from contextlib import ExitStack

import concourse.bass as bass
from concourse import mybir

ALU = mybir.AluOpType
ACT = mybir.ActivationFunctionType
AX = mybir.AxisListType
F32 = mybir.dt.float32
F32R = mybir.dt.float32r
BF16 = mybir.dt.bfloat16

P = 128
B, S, D = 4, 1024, 512
H, DH = 16, 32
HG = P // DH
NG = H // HG
FF = 2048
BLOCK = 64
NBLK = S // BLOCK
TOK = 512
SUB = TOK // P
HALVES = S // TOK
TILES = B * HALVES
KC = D // P
KT = S // P
NEG = -1.0e9
CAUSAL = -1.0e30
EPS = 1e-5
AUG = 3 * DH
MASK_ROW, MAX_HI_ROW, MAX_LO_ROW = AUG, AUG + 1, AUG + 2
ROWS = AUG + 3


def on_tiles(eng, body):
    body(0, 0, 0)
    with eng.Fori(0, B - 2) as j:
        body(j * 2 + 1, j, 1)
        body(j * 2 + 2, j + 1, 0)
    for i in range(TILES - 3, TILES):
        body(i, i // HALVES, i % HALVES)


def nxt(i, b, s):
    return (i + 1, b, 1) if s == 0 else (i + 1, b + 1, 0)


def at_least(i, n):
    return i >= n if isinstance(i, int) else True


def wait_alone(eng, sem, value, passed):
    eng.wait_ge(sem, value)
    eng.sem_inc(passed, 1)


class Semaphores:

    def __init__(self, nc, ctx, tag):
        self.nc, self.ctx, self.tag, self.all = nc, ctx, tag, []

    def __call__(self, name):
        self.all.append(self.ctx.enter_context(self.nc.semaphore(self.tag + name)))
        return self.all[-1]

    def clear(self):
        numbers = sorted(s.num for s in self.all)
        starts = [n for n in numbers if n - 1 not in numbers]
        with self.nc.Block() as block:
            @block.sync
            def _(sp):
                for start in starts:
                    end = start
                    while end in numbers:
                        end += 1
                    sp.sem_clear(range(start, end))


def three(pe, out, pairs, start, stop):
    last = None
    for n, (wh, wl, xh, xl) in enumerate(pairs):
        for m, (w, x) in enumerate(((wh, xh), (wh, xl), (wl, xh))):
            last = pe.matmul(out, w, x, start=(start and n == 0 and m == 0),
                             stop=(stop and n == len(pairs) - 1 and m == 2))
    return last


def router_stage(nc, keep, x_tiles, ln_g, ln_b, wk, r_w1, r_b1, r_w2, r_b2):
    with ExitStack() as ctx:
        sb = lambda name, shape, dt=F32: ctx.enter_context(nc.sbuf_tensor("r_" + name, shape, dt))
        sem = Semaphores(nc, ctx, "r_")
        x = sb("x", [P, HALVES * SUB, D])
        xn = sb("xn", [P, HALVES * SUB, D])
        wk_sb = sb("wk", [P, KC, D])
        w1 = sb("w1", [P, KC, P])
        w2 = sb("w2", [P, 1])
        w2_all = sb("w2_all", [P, P])
        gb = sb("gb", [P, 2, KC])
        b1 = sb("b1", [P, 1])
        b2 = sb("b2", [P, 1])
        stats = sb("stats", [P, KT, 6])
        mv = sb("mv", [P, KT, 2])
        var = sb("var", [P, KT])
        rstd = sb("rstd", [P, KT])
        power = sb("power", [P, KT])
        averager = sb("averager", [P, 2])
        means = sb("means", [P, KC, NBLK])
        key_means = sb("key_means", [P, KC, NBLK])
        hidden = sb("hidden", [P, NBLK])
        kept = sb("kept", [P, NBLK])
        ps = ctx.enter_context(nc.psum_tensor("r_ps", [P, 4, 512], F32))
        loaded_x, loaded_w, consts = sem("loaded_x"), sem("loaded_w"), sem("consts")
        v_step, rstd_ready = sem("v_step"), sem("rstd_ready")
        normed, meaned, scaled, keyed = sem("normed"), sem("meaned"), sem("scaled"), sem("keyed")
        keys_copied, hid_ready, relu_done, logits = (sem("keys_copied"), sem("hid_ready"),
                                                     sem("relu_done"), sem("logits"))
        with nc.Block() as block:
            @block.sync
            def _(sp):
                for s in range(HALVES):
                    sp.dma_start(x[:, s * SUB:(s + 1) * SUB, :], x_tiles[0, s]).then_inc(loaded_x, 16)
                sp.dma_start(wk_sb[:], wk.rearrange("(c p) n -> p c n", p=P)).then_inc(loaded_w, 16)
                sp.dma_start(w1[:], r_w1.rearrange("(c p) n -> p c n", p=P)).then_inc(loaded_w, 16)
                sp.dma_start(w2[:], r_w2).then_inc(loaded_w, 16)
                sp.dma_start(gb[:, 0, :], ln_g).then_inc(loaded_w, 16)
                sp.dma_start(gb[:, 1, :], ln_b).then_inc(loaded_w, 16)
                sp.dma_start(b1[:], r_b1).then_inc(loaded_w, 16)
                sp.dma_start(b2[:], r_b2.partition_broadcast(P)).then_inc(loaded_w, 16)

            @block.gpsimd
            def _(pool):
                pool.memset(averager[:], 0.0).then_inc(consts, 1)
                pool.memset(power[:], -0.5).then_inc(consts, 1)
                pool.wait_ge(consts, 2)
                for h in range(2):
                    pool.memset(averager[h * BLOCK:(h + 1) * BLOCK, h:h + 1], 1.0 / BLOCK).then_inc(consts, 1)
                pool.wait_ge(consts, 4)
                pool.wait_ge(v_step, 2)
                pool.tensor_tensor(rstd[:], var[:], power[:], ALU.pow).then_inc(rstd_ready, 1)

            @block.vector
            def _(dve):
                dve.wait_ge(loaded_x, 16 * HALVES)
                for t in range(KT):
                    last = dve.bn_stats(stats[:, t, :], x[:, t, :])
                last.then_inc(v_step, 1)
                dve.wait_ge(v_step, 1)
                for t in range(KT):
                    last = dve.bn_aggr(mv[:, t, :], stats[:, t, :])
                last.then_inc(normed, 1)
                dve.wait_ge(normed, 1)
                dve.tensor_scalar_add(var[:], mv[:, :, 1], EPS).then_inc(v_step, 1)
                dve.wait_ge(rstd_ready, 1)
                for t in range(KT):
                    dve.tensor_scalar(xn[:, t, :], x[:, t, :], mv[:, t, 0:1], rstd[:, t:t + 1],
                                      ALU.subtract, ALU.mult).then_inc(normed, 1)
                dve.wait_ge(loaded_w, 16 * 7)
                dve.tensor_copy(w2_all[:], w2[:, 0:1].to_broadcast([P, P])).then_inc(v_step, 1)
                dve.wait_ge(meaned, 1)
                for c in range(KC):
                    last = dve.tensor_scalar(means[:, c, :], ps[:, 0, c * NBLK:(c + 1) * NBLK],
                                             gb[:, 0, c:c + 1], gb[:, 1, c:c + 1], ALU.mult, ALU.add)
                last.then_inc(scaled, 1)
                dve.wait_ge(keyed, 1)
                dve.tensor_copy(key_means[:].rearrange("p c n -> p (c n)"),
                                ps[:, 1, 0:KC * NBLK]).then_inc(keys_copied, 1)
                dve.wait_ge(hid_ready, 1)
                dve.tensor_scalar(hidden[:], ps[:, 2, 0:NBLK], b1[:, 0:1], 0.0, ALU.add,
                                  ALU.max).then_inc(relu_done, 1)
                dve.wait_ge(logits, 1)
                dve.tensor_scalar(kept[:], ps[:, 3, 0:NBLK], b2[:, 0:1], 0.0, ALU.add,
                                  ALU.is_gt).then_inc(v_step, 1)
                dve.wait_ge(v_step, 4)
                dve.tensor_copy(keep[:].rearrange("p (n t) -> p n t", t=BLOCK),
                                kept[:].unsqueeze(2).to_broadcast([P, NBLK, BLOCK])).then_inc(v_step, 1)
                dve.wait_ge(v_step, 5)

            @block.tensor
            def _(pe):
                pe.wait_ge(consts, 4)
                for t in range(KT):
                    pe.wait_ge(normed, t + 2)
                    for c in range(KC):
                        last = pe.matmul(ps[:, 0, c * NBLK + 2 * t:c * NBLK + 2 * t + 2],
                                         xn[:, t, c * P:(c + 1) * P], averager[:], start=True, stop=True)
                last.then_inc(meaned, 1)
                pe.wait_ge(loaded_w, 16 * 7)
                pe.wait_ge(scaled, 1)
                for m in range(KC):
                    for c in range(KC):
                        last = pe.matmul(ps[:, 1, m * NBLK:(m + 1) * NBLK], wk_sb[:, c, m * P:(m + 1) * P],
                                         means[:, c, :], start=(c == 0), stop=(c == KC - 1))
                last.then_inc(keyed, 1)
                pe.wait_ge(keys_copied, 1)
                for c in range(KC):
                    last = pe.matmul(ps[:, 2, 0:NBLK], w1[:, c, :], key_means[:, c, :],
                                     start=(c == 0), stop=(c == KC - 1))
                last.then_inc(hid_ready, 1)
                pe.wait_ge(v_step, 3)
                pe.wait_ge(relu_done, 1)
                pe.matmul(ps[:, 3, 0:NBLK], w2_all[:], hidden[:], start=True, stop=True).then_inc(logits, 1)
        sem.clear()


def projection_stage(nc, tag, ident, src, mix=None, norm=None, weights=(), chans=(), toks=None,
                     keep_xt=None):
    RING = 4
    has_mix = mix is not None
    n_mix, n_chan, n_tok = (SUB if has_mix else 0), len(chans), (SUB if toks else 0)
    per_tile = n_mix + n_chan + n_tok
    work = [("chan", k) for k in range(n_chan)] + [("tok", k) for k in range(n_tok)]
    halves = (work[:len(work) // 2], work[len(work) // 2:])
    assert n_chan % RING == 0 and n_tok % RING == 0

    def mix_seq(i, k):
        return k if isinstance(i, int) and i == 0 else (i - 1) * per_tile + n_mix + k

    def work_seq(i, k):
        ahead = 0 if isinstance(i, int) and i == TILES - 1 else n_mix
        return i * per_tile + n_mix + ahead + k

    with ExitStack() as ctx:
        sb = lambda name, shape, dt=F32: ctx.enter_context(nc.sbuf_tensor(tag + name, shape, dt))
        sem = Semaphores(nc, ctx, tag)
        n_w = len(weights)
        w_hi = sb("w_hi", [P, max(n_w, 1), KC, D], F32R) if n_w else None
        w_lo = sb("w_lo", [P, max(n_w, 1), KC, D], F32R) if n_w else None
        raw = sb("raw", [P, 4, D])
        x = sb("x", [P, 2, SUB, D])
        x_hi = sb("x_hi", [P, 2, KC, TOK], F32R)
        x_lo = sb("x_lo", [P, 2, KC, TOK], F32R)
        xt = sb("xt", [P, KC, TOK])
        tr = ctx.enter_context(nc.psum_tensor(tag + "tr", [P, 2, TOK], F32))
        ring = ctx.enter_context(nc.psum_tensor(tag + "ring", [P, RING, 512], F32))
        if norm:
            xn = sb("xn", [P, SUB, D])
            stats = sb("stats", [P, SUB, 6])
            mv = sb("mv", [P, SUB, 2])
            var = sb("var", [P, SUB])
            rstd = sb("rstd", [P, SUB])
            power = sb("power", [P, SUB])
            gb = sb("gb", [P, 2, KC])
        if has_mix:
            o = sb("o", [P, KC, TOK])
            o_hi = sb("o_hi", [P, KC, TOK], F32R)
            o_lo = sb("o_lo", [P, KC, TOK], F32R)
            o_bias = sb("o_bias", [P, D])
            ow_hi = sb("ow_hi", [P, KC, D], F32R)
            ow_lo = sb("ow_lo", [P, KC, D], F32R)
        if n_chan:
            full = sb("full", [P, 4, TOK])
            part_hi = sb("part_hi", [P, 4, TOK], F32R)
            part_lo = sb("part_lo", [P, 4, TOK], F32R)
        if toks:
            tok_out = sb("tok_out", [P, 2, SUB, D])
            tok_bias = sb("tok_bias", [P, D])

        sp_passed, dve_passed = sem("sp_passed"), sem("dve_passed")
        raw_loaded = [sem(f"raw_loaded{k}") for k in range(4)]
        w_hi_done, w_lo_done, small_loaded = sem("w_hi_done"), sem("w_lo_done"), sem("small_loaded")
        x_loaded = [sem(f"x_loaded{k}") for k in range(2)]
        o_loaded, o_hi_done, o_lo_done = sem("o_loaded"), sem("o_hi_done"), sem("o_lo_done")
        biased, x_stored = sem("biased"), [sem(f"x_stored{k}") for k in range(2)]
        stat_step, aggregated, var_ready, rstd_ready, normed = (sem("stat_step"), sem("aggregated"),
                                                               sem("var_ready"), sem("rstd_ready"), sem("normed"))
        power_set = sem("power_set")
        turned, turned_out, x_hi_done, x_lo_done = sem("turned"), sem("turned_out"), sem("x_hi_done"), sem("x_lo_done")
        xt_stored = [sem(f"xt_stored{k}") for k in range(2)]
        filled, emptied = sem("filled"), sem("emptied")
        hi_ready, lo_ready = sem("hi_ready"), sem("lo_ready")
        hi_stored = [sem(f"hi_stored{k}") for k in range(4)]
        lo_stored = [sem(f"lo_stored{k}") for k in range(4)]
        tok_stored = [sem(f"tok_stored{k}") for k in range(2)]

        pieces = []
        if has_mix:
            pieces += [(mix[1][c * P:(c + 1) * P, :], ow_hi[:, c, :], ow_lo[:, c, :]) for c in range(KC)]
        n_mix_pieces = len(pieces)
        for n, w in enumerate(weights):
            pieces += [(w[c * P:(c + 1) * P, :], w_hi[:, n, c, :], w_lo[:, n, c, :]) for c in range(KC)]
        small = []
        if norm:
            small += [(gb[:, 0, :], norm[0]), (gb[:, 1, :], norm[1])]
        if has_mix:
            small += [(o_bias[:], mix[2].partition_broadcast(P))]
        if toks and toks[1] is not None:
            small += [(tok_bias[:], toks[1].partition_broadcast(P))]

        with nc.Block() as block:
            @block.sync
            def _(sp):
                def load_x(i, b, s):
                    if at_least(i, 2):
                        if norm:
                            wait_alone(sp, normed, (i - 1) * SUB, sp_passed)
                        else:
                            wait_alone(sp, turned, (i - 1) * KC, sp_passed)
                        if has_mix:
                            wait_alone(sp, x_stored[s], b * 16, sp_passed)
                    sp.dma_start(x[:, s], src[b, s]).then_inc(x_loaded[s], 16)

                def load_o(i, b, s):
                    if at_least(i, 1):
                        wait_alone(sp, o_lo_done, i * KC, sp_passed)
                    sp.dma_start(o[:], mix[0][b, s]).then_inc(o_loaded, 16)

                if has_mix:
                    load_o(0, 0, 0)
                load_x(0, 0, 0)
                for dst, row in small:
                    sp.dma_start(dst, row).then_inc(small_loaded, 16)
                for u, (w, _, _) in enumerate(pieces):
                    if u >= 4:
                        sp.wait_ge(w_lo_done, u - 3)
                    sp.dma_start(raw[:, u % 4, :], w).then_inc(raw_loaded[u % 4], 16)
                if has_mix:
                    load_o(1, 0, 1)
                load_x(1, 0, 1)

                def body(i, b, s):
                    last = isinstance(i, int) and i == TILES - 1
                    one = nxt(i, b, s)
                    if has_mix and not last:
                        wait_alone(sp, emptied, mix_seq(one[0], SUB - 1) + 1, sp_passed)
                        sp.dma_start(mix[3][one[1], one[2]], x[:, one[2]]).then_inc(x_stored[one[2]], 16)
                    if not (isinstance(i, int) and i >= TILES - 2):
                        two = (i + 2, b + 1, s)
                        if has_mix:
                            load_o(*two)
                        load_x(*two)
                    else:
                        two = None
                    if keep_xt and not last:
                        wait_alone(sp, x_lo_done, (one[0] + 1) * KC, sp_passed)
                        for part, home in ((x_hi, keep_xt[0]), (x_lo, keep_xt[1])):
                            sp.dma_start(home[one[1], one[2]], part[:, one[2]].bitcast(F32)).then_inc(xt_stored[one[2]], 16)
                    for kind, k in work:
                        if kind == "chan":
                            c = i * n_chan + k
                            wait_alone(sp, hi_ready, c + 1, sp_passed)
                            sp.dma_start(chans[k][2][b, s], part_hi[:, k % 4, :].bitcast(F32)).then_inc(hi_stored[k % 4], 16)
                            wait_alone(sp, lo_ready, c + 1, sp_passed)
                            sp.dma_start(chans[k][3][b, s], part_lo[:, k % 4, :].bitcast(F32)).then_inc(lo_stored[k % 4], 16)
                        elif k == SUB - 1:
                            wait_alone(sp, emptied, work_seq(i, n_chan + k) + 1, sp_passed)
                            for g in range(NG):
                                sp.dma_start(toks[2][b, s, g], tok_out[:, s, :, g * P:(g + 1) * P]).then_inc(tok_stored[s], 16)

                if has_mix:
                    sp.wait_ge(emptied, mix_seq(0, SUB - 1) + 1)
                    sp.dma_start(mix[3][0, 0], x[:, 0]).then_inc(x_stored[0], 16)
                if keep_xt:
                    sp.wait_ge(x_lo_done, KC)
                    for part, home in ((x_hi, keep_xt[0]), (x_lo, keep_xt[1])):
                        sp.dma_start(home[0, 0], part[:, 0].bitcast(F32)).then_inc(xt_stored[0], 16)
                on_tiles(sp, body)
                for s in range(2):
                    if has_mix:
                        sp.wait_ge(x_stored[s], 16 * TILES // 2)
                    if keep_xt:
                        sp.wait_ge(xt_stored[s], 32 * TILES // 2)
                    if toks:
                        sp.wait_ge(tok_stored[s], 16 * NG * TILES // 2)
                for k in range(4 if n_chan else 0):
                    sp.wait_ge(hi_stored[k], 16 * TILES * n_chan // 4)
                    sp.wait_ge(lo_stored[k], 16 * TILES * n_chan // 4)

            def schedule(eng, split, mixing, turning, working):
                if has_mix:
                    split(0, 0, 0)
                    mixing(0, 0, 0)
                    split(1, 0, 1)
                else:
                    mixing(0, 0, 0)
                turning(0, 0, 0)

                def body(i, b, s):
                    last = isinstance(i, int) and i == TILES - 1
                    one = nxt(i, b, s)
                    if not last:
                        mixing(*one)
                    working(i, b, s, 0)
                    if not last:
                        turning(*one)
                    if has_mix and not (isinstance(i, int) and i >= TILES - 2):
                        split(i + 2, b + 1, s)
                    working(i, b, s, 1)
                on_tiles(eng, body)

            @block.scalar
            def _(act):
                for u, (_, hi, _) in enumerate(pieces):
                    act.wait_ge(raw_loaded[u % 4], 16 * (u // 4 + 1))
                    act.copy(hi, raw[:, u % 4, :]).then_inc(w_hi_done, 1)
                if small:
                    act.wait_ge(small_loaded, 16 * len(small))

                def split(i, b, s):
                    act.wait_ge(o_loaded, (i + 1) * 16)
                    if at_least(i, 1):
                        act.wait_ge(filled, mix_seq(i - 1, SUB - 1) + 1)
                    for c in range(KC):
                        act.copy(o_hi[:, c, :], o[:, c, :]).then_inc(o_hi_done, 1)

                def mixing(i, b, s):
                    pass

                def turning(i, b, s):
                    for c in range(KC):
                        act.wait_ge(turned, i * KC + c + 1)
                        if at_least(i, 1):
                            act.wait_ge(x_lo_done, (i - 1) * KC + c + 1)
                        if norm:
                            act.activation(xt[:, c, :], tr[:, c % 2, :], ACT.Identity, bias=gb[:, 1, c:c + 1],
                                           scale=gb[:, 0, c:c + 1]).then_inc(turned_out, 1)
                        else:
                            act.copy(xt[:, c, :], tr[:, c % 2, :]).then_inc(turned_out, 1)

                def working(i, b, s, half):
                    for kind, k in halves[half]:
                        if kind == "chan":
                            uses = i * (n_chan // 4) + k // 4
                            act.wait_ge(emptied, work_seq(i, k) + 1)
                            if k >= 4 or at_least(i, 1):
                                act.wait_ge(hi_stored[k % 4], uses * 16)
                                act.wait_ge(lo_ready, i * n_chan + k - 3)
                            act.copy(part_hi[:, k % 4, :], full[:, k % 4, :]).then_inc(hi_ready, 1)

                schedule(act, split, mixing, turning, working)

            @block.gpsimd
            def _(pool):
                if norm:
                    pool.memset(power[:], -0.5).then_inc(power_set, 1)
                    pool.wait_ge(power_set, 1)
                for u, (_, hi, lo) in enumerate(pieces):
                    pool.wait_ge(w_hi_done, u + 1)
                    pool.tensor_tensor(lo, raw[:, u % 4, :], hi.bitcast(F32), ALU.subtract).then_inc(w_lo_done, 1)
                if small:
                    pool.wait_ge(small_loaded, 16 * len(small))

                def split(i, b, s):
                    for c in range(KC):
                        pool.wait_ge(o_hi_done, i * KC + c + 1)
                        if at_least(i, 1) and c == 0:
                            pool.wait_ge(filled, mix_seq(i - 1, SUB - 1) + 1)
                        pool.tensor_tensor(o_lo[:, c, :], o[:, c, :], o_hi[:, c, :].bitcast(F32),
                                           ALU.subtract).then_inc(o_lo_done, 1)

                def mixing(i, b, s):
                    if has_mix:
                        pool.wait_ge(x_loaded[s], (b + 1) * 16)
                        for u in range(SUB):
                            pool.tensor_tensor(x[:, s, u, :], x[:, s, u, :], o_bias[:], ALU.add).then_inc(biased, 1)
                    if norm:
                        pool.wait_ge(var_ready, i + 1)
                        pool.tensor_tensor(rstd[:], var[:], power[:], ALU.pow).then_inc(rstd_ready, 1)

                def turning(i, b, s):
                    for c in range(KC):
                        pool.wait_ge(x_hi_done, i * KC + c + 1)
                        if c == 0 and keep_xt and at_least(i, 2):
                            pool.wait_ge(xt_stored[s], b * 32)
                        pool.tensor_tensor(x_lo[:, s, c, :], xt[:, c, :], x_hi[:, s, c, :].bitcast(F32),
                                           ALU.subtract).then_inc(x_lo_done, 1)

                def working(i, b, s, half):
                    for kind, k in halves[half]:
                        if kind == "chan":
                            uses = i * (n_chan // 4) + k // 4
                            pool.wait_ge(hi_ready, i * n_chan + k + 1)
                            if k >= 4 or at_least(i, 1):
                                pool.wait_ge(lo_stored[k % 4], uses * 16)
                            pool.tensor_tensor(part_lo[:, k % 4, :], full[:, k % 4, :],
                                               part_hi[:, k % 4, :].bitcast(F32), ALU.subtract).then_inc(lo_ready, 1)

                schedule(pool, split, mixing, turning, working)

            @block.vector
            def _(dve):
                if small:
                    dve.wait_ge(small_loaded, 16 * len(small))

                def split(i, b, s):
                    pass

                def mixing(i, b, s):
                    dve.wait_ge(x_loaded[s], (b + 1) * 16)
                    if has_mix:
                        for u in range(SUB):
                            dve.wait_ge(biased, i * SUB + u + 1)
                            dve.wait_ge(filled, mix_seq(i, u) + 1)
                            dve.tensor_tensor(x[:, s, u, :], ring[:, u % RING, :], x[:, s, u, :],
                                              ALU.add).then_inc(emptied, 1)
                        dve.wait_ge(emptied, mix_seq(i, SUB - 1) + 1)
                    if not norm:
                        return
                    for u in range(SUB):
                        last = dve.bn_stats(stats[:, u, :], x[:, s, u, :])
                    last.then_inc(stat_step, 1)
                    wait_alone(dve, stat_step, i + 1, dve_passed)
                    for u in range(SUB):
                        last = dve.bn_aggr(mv[:, u, :], stats[:, u, :])
                    last.then_inc(aggregated, 1)
                    dve.wait_ge(aggregated, i + 1)
                    dve.tensor_scalar_add(var[:], mv[:, :, 1], EPS).then_inc(var_ready, 1)
                    dve.wait_ge(rstd_ready, i + 1)
                    if at_least(i, 1):
                        dve.wait_ge(turned, i * KC)
                    for u in range(SUB):
                        dve.tensor_scalar(xn[:, u, :], x[:, s, u, :], mv[:, u, 0:1], rstd[:, u:u + 1],
                                          ALU.subtract, ALU.mult).then_inc(normed, 1)

                def turning(i, b, s):
                    for c in range(KC):
                        dve.wait_ge(turned_out, i * KC + c + 1)
                        if c == 0 and at_least(i, 2):
                            if work:
                                dve.wait_ge(filled, work_seq(i - 2, len(work) - 1) + 1)
                            if keep_xt:
                                dve.wait_ge(xt_stored[s], b * 32)
                            dve.wait_ge(x_lo_done, (i - 1) * KC)
                        dve.tensor_copy(x_hi[:, s, c, :], xt[:, c, :]).then_inc(x_hi_done, 1)

                def working(i, b, s, half):
                    for n, (kind, k) in enumerate(halves[half]):
                        q = half * len(halves[0]) + n
                        dve.wait_ge(filled, work_seq(i, q) + 1)
                        bank = ring[:, q % RING, :]
                        if kind == "chan":
                            if k >= 4 or at_least(i, 1):
                                dve.wait_ge(lo_ready, i * n_chan + k - 3)
                            chans[k][1](dve, full[:, k % 4, :], bank, s).then_inc(emptied, 1)
                        else:
                            if k == 0 and at_least(i, 2):
                                dve.wait_ge(tok_stored[s], b * 16 * NG)
                            out = tok_out[:, s, k, :]
                            ins = (dve.tensor_tensor(out, bank, tok_bias[:], ALU.add) if toks[1] is not None
                                   else dve.tensor_copy(out, bank))
                            ins.then_inc(emptied, 1)

                schedule(dve, split, mixing, turning, working)

            @block.tensor
            def _(pe):
                def bank_free(seq, q, i):
                    if not (isinstance(seq, int) and seq < RING):
                        pe.wait_ge(emptied, seq - RING + 1)

                def split(i, b, s):
                    pass

                def mixing(i, b, s):
                    if not has_mix:
                        return
                    if isinstance(i, int) and i == 0:
                        pe.wait_ge(w_lo_done, n_mix_pieces)
                    pe.wait_ge(o_lo_done, (i + 1) * KC)
                    for u in range(SUB):
                        bank_free(mix_seq(i, u), u, i)
                        cols = slice(u * P, (u + 1) * P)
                        three(pe, ring[:, u % RING, :],
                                     [(o_hi[:, c, cols], o_lo[:, c, cols], ow_hi[:, c, :], ow_lo[:, c, :])
                                      for c in range(KC)], True, True).then_inc(filled, 1)

                def turning(i, b, s):
                    if norm:
                        pe.wait_ge(normed, (i + 1) * SUB)
                    else:
                        pe.wait_ge(x_loaded[s], (b + 1) * 16)
                    tokens = xn if norm else x[:, s]
                    for c in range(KC):
                        if c >= 2 or at_least(i, 1):
                            pe.wait_ge(turned_out, i * KC + c - 1)
                        for u in range(SUB):
                            last = pe.transpose(tr[:, c % 2, u * P:(u + 1) * P],
                                                tokens[:, u, c * P:(c + 1) * P], ident[:])
                        last.then_inc(turned, 1)

                def working(i, b, s, half):
                    if not work:
                        return
                    if half == 0:
                        if isinstance(i, int) and i == 0:
                            pe.wait_ge(w_lo_done, len(pieces))
                        pe.wait_ge(x_lo_done, (i + 1) * KC)
                    for n, (kind, k) in enumerate(halves[half]):
                        q = half * len(halves[0]) + n
                        bank_free(work_seq(i, q), q, i)
                        bank = ring[:, q % RING, :]
                        if kind == "chan":
                            w, m = divmod(chans[k][0], KC)
                            cols = slice(m * P, (m + 1) * P)
                            pairs = [(w_hi[:, w, c, cols], w_lo[:, w, c, cols], x_hi[:, s, c, :], x_lo[:, s, c, :])
                                     for c in range(KC)]
                        else:
                            cols = slice(k * P, (k + 1) * P)
                            pairs = [(x_hi[:, s, c, cols], x_lo[:, s, c, cols], w_hi[:, toks[0], c, :],
                                      w_lo[:, toks[0], c, :]) for c in range(KC)]
                        three(pe, bank, pairs, True, True).then_inc(filled, 1)

                schedule(pe, split, mixing, turning, working)
        sem.clear()


def attention_stage(nc, tag, ident, q_hi, q_lo, k_hi, k_lo, v, out, keep=None, mask_qk=None,
                    mask_kq=None, ident_bf=None):
    causal = keep is not None
    N = B * NG
    steps = [(h, t, max(0, t * P - h * TOK) if causal else 0) for h in range(HALVES)
             for t in range((h + 1) * TOK // P if causal else KT)]
    last_step = {h: max(n for n, st in enumerate(steps) if st[0] == h) for h in range(HALVES)}
    NS, NBLOCKS = len(steps), len(steps) * HG
    UNITS = HG * KT
    PR = 4
    assert NS % PR == 0
    lead = 2
    weight = [0.3 + ((u % KT) + 1 if causal else KT) for u in range(UNITS)]
    unit_step, acc = [], 0.0
    for u in range(UNITS):
        unit_step.append(lead + int(acc / sum(weight) * (NS - 1 - lead)))
        acc += weight[u]

    with ExitStack() as ctx:
        sb = lambda name, shape, dt=F32: ctx.enter_context(nc.sbuf_tensor(tag + name, shape, dt))
        sem = Semaphores(nc, ctx, tag)
        qs = [sb(f"qs{p}", [P, HG, S], F32R) for p in range(2)]
        ks = [sb(f"ks{p}", [P, HG, S], F32R) for p in range(2)]
        vs = [sb(f"vs{p}", [P, KT, P]) for p in range(2)]
        probs = sb("probs", [P, PR, HG, TOK])
        ones = sb("ones", [P, DH])
        neg_max = sb("neg_max", [P, UNITS])
        max_hi = sb("max_hi", [UNITS, P], F32R)
        max_lo = sb("max_lo", [UNITS, P], F32R)
        recip = sb("recip", [P, TOK])
        outs = sb("outs", [P, 2, TOK])
        nat = ctx.enter_context(nc.psum_tensor(tag + "nat", [P, 2, 2, 512], F32))
        st_ps = ctx.enter_context(nc.psum_tensor(tag + "st", [P, 2, 512], F32))
        pv_ps = ctx.enter_context(nc.psum_tensor(tag + "pv", [P, 512], F32))
        sum_ps = ctx.enter_context(nc.psum_tensor(tag + "sum", [P, 512], F32))

        consts_set, ones_set, sp_passed = sem("consts_set"), sem("ones_set"), sem("sp_passed")
        loaded = [sem(f"loaded{p}") for p in range(2)]
        rows_loaded = [sem(f"rows_loaded{p}") for p in range(2)]
        nat_ready, maxed, max_turned, max_split = sem("nat_ready"), sem("maxed"), sem("max_turned"), sem("max_split")
        st_ready, exped, pv_done = sem("st_ready"), sem("exped"), sem("pv_done")
        recip_done, out_ready = sem("recip_done"), sem("out_ready")
        out_stored = [sem(f"out_stored{h}") for h in range(HALVES)]
        LOADS = 7

        def schedule(eng, body):
            body(0, 0, 0)
            with eng.Fori(0, (N - 2) // 2) as j:
                body(j * 2 + 1, j, 1)
                body(j * 2 + 2, j + 1, 0)
            body(N - 1, (N - 1) // 2, 1)

        def is_last(n):
            return isinstance(n, int) and n == N - 1

        with nc.Block() as block:
            @block.sync
            def _(sp):
                def load(n, m, p):
                    if at_least(n, 2):
                        wait_alone(sp, pv_done, (n - 1) * NS, sp_passed)
                    heads = "(h r) t -> r h t"
                    for row, part in ((0, q_hi), (1, q_hi), (2, q_lo)):
                        sp.dma_start(qs[p][row * DH:(row + 1) * DH].bitcast(F32),
                                     part[n].rearrange(heads, r=DH)).then_inc(loaded[p], 16)
                    for row, part in ((0, k_hi), (1, k_lo), (2, k_hi)):
                        sp.dma_start(ks[p][row * DH:(row + 1) * DH].bitcast(F32),
                                     part[n].rearrange(heads, r=DH)).then_inc(loaded[p], 16)
                    sp.dma_start(vs[p][:], v[n].rearrange("k p c -> p k c")).then_inc(loaded[p], 16)

                def rows(n, m, p):
                    wait_alone(sp, max_split, (n + 1) * 2, sp_passed)
                    sp.wait_ge(consts_set, 8)
                    for row, part in ((MAX_HI_ROW, max_hi), (MAX_LO_ROW, max_lo)):
                        sp.dma_start(qs[p][row:row + 1].bitcast(F32), part[:].bitcast(F32)).then_inc(rows_loaded[p], 16)

                load(0, 0, 0)
                load(1, 0, 1)
                rows(0, 0, 0)

                def body(n, m, p):
                    if not is_last(n):
                        nn = (n + 1, m, 1) if p == 0 else (n + 1, m + 1, 0)
                        if not (isinstance(n, int) and n == 0):
                            load(*nn)
                    for h in range(HALVES):
                        if h == 1 and not is_last(n):
                            rows(*nn)
                        wait_alone(sp, out_ready, n * 2 + h + 1, sp_passed)
                        sp.dma_start(out[n][:, h * TOK:(h + 1) * TOK], outs[:, h, :]).then_inc(out_stored[h], 16)
                schedule(sp, body)
                for h in range(HALVES):
                    sp.wait_ge(out_stored[h], 16 * N)

            @block.gpsimd
            def _(pool):
                pool.memset(ones[:], 1.0).then_inc(ones_set, 1)
                pool.wait_ge(ones_set, 1)
                for p in range(2):
                    pool.memset(ks[p][AUG:ROWS].bitcast(F32), 1.0).then_inc(consts_set, 1)
                    pool.memset(qs[p][AUG:ROWS].bitcast(F32), 0.0).then_inc(consts_set, 1)

            @block.vector
            def _(dve):
                dve.wait_ge(consts_set, 4)
                if causal:
                    for p in range(2):
                        row = keep[AUG:AUG + 1, :].unsqueeze(1).to_broadcast([1, HG, S])
                        dve.tensor_copy(qs[p][AUG:AUG + 1], row).then_inc(consts_set, 1)
                        dve.tensor_scalar(ks[p][AUG:AUG + 1], row, -NEG, NEG, ALU.mult, ALU.add).then_inc(consts_set, 1)
                else:
                    for p in range(2):
                        dve.memset(ks[p][AUG:AUG + 1].bitcast(F32), 0.0).then_inc(consts_set, 2)

                def maximum(n, u):
                    keys = ((u % KT) + 1) * P if causal else S
                    banks = 2 if keys > 512 else 1
                    dve.wait_ge(nat_ready, n * UNITS + u + 1)
                    if u == 0 and at_least(n, 1):
                        dve.wait_ge(max_turned, n)
                    dve.tensor_reduce(neg_max[:, u:u + 1], nat[:, u % 2, 0:banks, 0:keys // banks], AX.XY,
                                      ALU.max, negate=True).then_inc(maxed, 1)

                def split_max(n, m, p):
                    dve.wait_ge(max_turned, n + 1)
                    if at_least(n, 1):
                        dve.wait_ge(rows_loaded[1 - p], (m + 1 if p else m) * 32)
                    turned = nat[0:UNITS, 0, 0, 0:P]
                    dve.tensor_copy(max_hi[:], turned).then_inc(max_split, 1)
                    dve.wait_ge(max_split, n * 2 + 1)
                    dve.tensor_tensor(max_lo[:], turned, max_hi[:].bitcast(F32), ALU.subtract).then_inc(max_split, 1)

                for u in range(UNITS):
                    maximum(0, u)
                split_max(0, 0, 0)

                def body(n, m, p):
                    nn = (n + 1, m, 1) if p == 0 else (n + 1, m + 1, 0)
                    for k, (h, t, _) in enumerate(steps):
                        if not is_last(n):
                            for u in range(UNITS):
                                if unit_step[u] == k:
                                    maximum(n + 1, u)
                            if k == NS - 1:
                                split_max(*nn)
                        if k == last_step[h]:
                            dve.wait_ge(pv_done, n * NS + k + 1)
                            dve.reciprocal(recip[:], sum_ps[:]).then_inc(recip_done, 1)
                            dve.wait_ge(recip_done, n * 2 + h + 1)
                            if at_least(n, 1):
                                dve.wait_ge(out_stored[h], n * 16)
                            dve.tensor_tensor(outs[:, h, :], pv_ps[:], recip[:], ALU.mult).then_inc(out_ready, 1)
                schedule(dve, body)

            @block.scalar
            def _(act):
                def body(n, m, p):
                    for k, (h, t, first) in enumerate(steps):
                        for j in range(HG):
                            blk = k * HG + j
                            act.wait_ge(st_ready, n * NBLOCKS + blk + 1)
                            if j == 0 and (k >= PR or at_least(n, 1)):
                                act.wait_ge(pv_done, n * NS + k - PR + 1)
                            act.activation(probs[:, k % PR, j, first:TOK], st_ps[:, blk % 2, first:TOK],
                                           ACT.Exp).then_inc(exped, 1)
                schedule(act, body)

            @block.tensor
            def _(pe):
                def max_scores(n, m, p, u):
                    j, t = divmod(u, KT)
                    keys = (t + 1) * P if causal else S
                    banks = 2 if keys > 512 else 1
                    width = keys // banks
                    rows = AUG + 1 if causal else AUG
                    if u == 0:
                        pe.wait_ge(loaded[p], (m + 1) * LOADS * 16)
                        pe.wait_ge(consts_set, 8)
                        if at_least(n, 1):
                            pe.wait_ge(max_split, n * 2)
                    if u >= 2 or at_least(n, 1):
                        pe.wait_ge(maxed, n * UNITS + u - 1)
                    for bank in range(banks):
                        cols = max(width, 256)
                        diagonal = causal and bank == banks - 1
                        last = pe.matmul(nat[:, u % 2, bank, 0:cols], qs[p][0:rows, j, t * P:(t + 1) * P],
                                         ks[p][0:rows, j, bank * width:bank * width + cols], start=True,
                                         stop=not diagonal)
                        if diagonal:
                            last = pe.matmul(nat[:, u % 2, bank, width - P:width], ident_bf[:], mask_qk[:],
                                             start=False, stop=True)
                    last.then_inc(nat_ready, 1)

                def turn_max(n):
                    pe.wait_ge(maxed, (n + 1) * UNITS)
                    pe.transpose(nat[0:UNITS, 0, 0, 0:P], neg_max[:], ident[:]).then_inc(max_turned, 1)

                def scores(n, p, k):
                    h, t, first = steps[k]
                    for j in range(HG):
                        blk = k * HG + j
                        if blk >= 2 or at_least(n, 1):
                            pe.wait_ge(exped, n * NBLOCKS + blk - 1)
                        lo = min(first, TOK - 256)
                        diagonal = causal and t * P >= h * TOK
                        last = pe.matmul(st_ps[:, blk % 2, lo:TOK], ks[p][0:ROWS, j, t * P:(t + 1) * P],
                                         qs[p][0:ROWS, j, h * TOK + lo:(h + 1) * TOK], start=True,
                                         stop=not diagonal)
                        if diagonal:
                            last = pe.matmul(st_ps[:, blk % 2, first:first + P], ident_bf[:], mask_kq[:],
                                             start=False, stop=True)
                        last.then_inc(st_ready, 1)

                def weigh(n, p, k):
                    h, t, first = steps[k]
                    begins = t == 0
                    pe.wait_ge(exped, n * NBLOCKS + (k + 1) * HG)
                    if begins and (h or at_least(n, 1)):
                        pe.wait_ge(out_ready, n * 2 + h)
                    for lhs, bank in ((vs[p], pv_ps), (None, sum_ps)):
                        for j in range(HG):
                            w = ones[:] if lhs is None else lhs[:, t, j * DH:(j + 1) * DH]
                            last = pe.matmul(bank[j * DH:(j + 1) * DH, first:TOK], w, probs[:, k % PR, j, first:TOK],
                                             start=begins, stop=(k == last_step[h]), skip_group_check=True)
                    last.then_inc(pv_done, 1)

                pe.wait_ge(ones_set, 1)
                for u in range(UNITS):
                    max_scores(0, 0, 0, u)
                turn_max(0)

                def body(n, m, p):
                    nn = (n + 1, m, 1) if p == 0 else (n + 1, m + 1, 0)
                    pe.wait_ge(rows_loaded[p], (m + 1) * 32)
                    scores(n, p, 0)
                    for k in range(NS):
                        if k + 1 < NS:
                            scores(n, p, k + 1)
                        if not is_last(n):
                            for u in range(UNITS):
                                if unit_step[u] == k:
                                    max_scores(*nn, u)
                            if k == NS - 1:
                                turn_max(n + 1)
                        weigh(n, p, k)
                schedule(pe, body)
        sem.clear()


def mlp_stage(nc, xt_hi, xt_lo, x_src, w1, b1, w2, b2, out):
    NC = FF // P
    LAG, RING = 2, 4
    with ExitStack() as ctx:
        sb = lambda name, shape, dt=F32: ctx.enter_context(nc.sbuf_tensor("m_" + name, shape, dt))
        sem = Semaphores(nc, ctx, "m_")
        w1_hi = sb("w1_hi", [P, NC, KC, P], F32R)
        w1_lo = sb("w1_lo", [P, NC, KC, P], F32R)
        w2_hi = sb("w2_hi", [P, NC, D], F32R)
        w2_lo = sb("w2_lo", [P, NC, D], F32R)
        raw = sb("raw", [P, 4, D])
        x_hi = sb("x_hi", [P, KC, TOK], F32R)
        x_lo = sb("x_lo", [P, KC, TOK], F32R)
        x = sb("x", [P, SUB, D])
        b1_sb = sb("b1", [P, NC])
        b2_sb = sb("b2", [P, D])
        hid = sb("hid", [P, RING, TOK])
        hid_hi = sb("hid_hi", [P, RING, TOK], F32R)
        hid_lo = sb("hid_lo", [P, RING, TOK], F32R)
        h_ps = ctx.enter_context(nc.psum_tensor("m_h_ps", [P, RING, 512], F32))
        o_ps = ctx.enter_context(nc.psum_tensor("m_o_ps", [P, SUB, 512], F32))
        sp_passed = sem("sp_passed")
        raw_loaded = [sem(f"raw_loaded{k}") for k in range(4)]
        small_loaded, w_hi_done, w_lo_done = sem("small_loaded"), sem("w_hi_done"), sem("w_lo_done")
        xt_loaded, x_loaded, biased = sem("xt_loaded"), sem("x_loaded"), sem("biased")
        h_filled, relu_done, hid_hi_done, hid_lo_done = (sem("h_filled"), sem("relu_done"), sem("hid_hi_done"),
                                                         sem("hid_lo_done"))
        multiplied, summed, stored = sem("multiplied"), sem("summed"), sem("stored")
        pieces = []
        for c in range(NC):
            pieces.append((w1.rearrange("(k p) f -> p k f", p=P)[:, :, c * P:(c + 1) * P],
                           w1_hi[:, c].rearrange("p k f -> p (k f)"), w1_lo[:, c].rearrange("p k f -> p (k f)")))
            pieces.append((w2[c * P:(c + 1) * P, :], w2_hi[:, c, :], w2_lo[:, c, :]))
        AHEAD = 3

        with nc.Block() as block:
            @block.sync
            def _(sp):
                def load(u):
                    if u >= 4:
                        sp.wait_ge(w_lo_done, u - 3)
                    dst = raw[:, u % 4, :]
                    if u % 2 == 0:
                        dst = dst.rearrange("p (k f) -> p k f", k=KC)
                    sp.dma_start(dst, pieces[u][0]).then_inc(raw_loaded[u % 4], 16)

                def load_xt(i, b, s):
                    if at_least(i, 1):
                        wait_alone(sp, h_filled, i * NC, sp_passed)
                    sp.dma_start(x_hi[:].bitcast(F32), xt_hi[b, s]).then_inc(xt_loaded, 16)
                    sp.dma_start(x_lo[:].bitcast(F32), xt_lo[b, s]).then_inc(xt_loaded, 16)

                def load_x(i, b, s):
                    if at_least(i, 1):
                        wait_alone(sp, stored, i * 16, sp_passed)
                    sp.dma_start(x[:], x_src[b, s]).then_inc(x_loaded, 16)

                def store(i, b, s):
                    wait_alone(sp, summed, (i + 1) * SUB, sp_passed)
                    sp.dma_start(out[b, s], x[:]).then_inc(stored, 16)

                load_xt(0, 0, 0)
                sp.dma_start(b1_sb[:], b1).then_inc(small_loaded, 16)
                for u in range(4):
                    load(u)
                sp.dma_start(b2_sb[:], b2.partition_broadcast(P)).then_inc(small_loaded, 16)
                load_x(0, 0, 0)
                for u in range(4, len(pieces)):
                    load(u)

                def body(i, b, s):
                    if isinstance(i, int) and i == TILES - 1:
                        return
                    load_xt(*nxt(i, b, s))
                    store(i, b, s)
                    load_x(*nxt(i, b, s))
                on_tiles(sp, body)
                store(TILES - 1, B - 1, 1)
                sp.wait_ge(stored, 16 * TILES)

            @block.scalar
            def _(act):
                def split(u):
                    act.wait_ge(raw_loaded[u % 4], 16 * (u // 4 + 1))
                    act.copy(pieces[u][1], raw[:, u % 4, :]).then_inc(w_hi_done, 1)

                for u in range(2 * AHEAD):
                    split(u)
                act.wait_ge(small_loaded, 32)

                def body(i, b, s):
                    for c in range(NC):
                        if isinstance(i, int) and i == 0 and c + AHEAD < NC:
                            split(2 * (c + AHEAD))
                            split(2 * (c + AHEAD) + 1)
                        act.wait_ge(h_filled, i * NC + c + 1)
                        if c >= RING or at_least(i, 1):
                            act.wait_ge(hid_lo_done, i * NC + c - RING + 1)
                        act.activation(hid[:, c % RING, :], h_ps[:, c % RING, :], ACT.Relu,
                                       bias=b1_sb[:, c:c + 1]).then_inc(relu_done, 1)
                on_tiles(act, body)

            @block.gpsimd
            def _(pool):
                def split(u):
                    pool.wait_ge(w_hi_done, u + 1)
                    pool.tensor_tensor(pieces[u][2], raw[:, u % 4, :], pieces[u][1].bitcast(F32),
                                       ALU.subtract).then_inc(w_lo_done, 1)

                for u in range(2 * AHEAD):
                    split(u)
                pool.wait_ge(small_loaded, 32)

                def body(i, b, s):
                    for c in range(NC):
                        if isinstance(i, int) and i == 0 and c + AHEAD < NC:
                            split(2 * (c + AHEAD))
                            split(2 * (c + AHEAD) + 1)
                        if 8 <= c < 8 + SUB:
                            u = c - 8
                            pool.wait_ge(x_loaded, (i + 1) * 16)
                            pool.tensor_tensor(x[:, u, :], x[:, u, :], b2_sb[:], ALU.add).then_inc(biased, 1)
                        pool.wait_ge(hid_hi_done, i * NC + c + 1)
                        if c >= RING or at_least(i, 1):
                            pool.wait_ge(multiplied, i * NC + c - RING + 1)
                        pool.tensor_tensor(hid_lo[:, c % RING, :], hid[:, c % RING, :],
                                           hid_hi[:, c % RING, :].bitcast(F32), ALU.subtract).then_inc(hid_lo_done, 1)
                on_tiles(pool, body)

            @block.vector
            def _(dve):
                def finish(i):
                    dve.wait_ge(multiplied, (i + 1) * NC)
                    dve.wait_ge(biased, (i + 1) * SUB)
                    for u in range(SUB):
                        dve.tensor_tensor(x[:, u, :], o_ps[:, u, :], x[:, u, :], ALU.add).then_inc(summed, 1)

                def body(i, b, s):
                    for c in range(NC):
                        dve.wait_ge(relu_done, i * NC + c + 1)
                        if c >= RING or at_least(i, 1):
                            dve.wait_ge(multiplied, i * NC + c - RING + 1)
                            dve.wait_ge(hid_lo_done, i * NC + c - RING + 1)
                        dve.tensor_copy(hid_hi[:, c % RING, :], hid[:, c % RING, :]).then_inc(hid_hi_done, 1)
                        if c == LAG - 1 and at_least(i, 1):
                            finish(i - 1)
                on_tiles(dve, body)
                finish(TILES - 1)

            @block.tensor
            def _(pe):
                def hidden(i, c):
                    if isinstance(i, int) and i == 0:
                        pe.wait_ge(w_lo_done, 2 * c + 1)
                    if c == 0:
                        pe.wait_ge(xt_loaded, (i + 1) * 32)
                    if c >= RING or at_least(i, 1):
                        pe.wait_ge(relu_done, i * NC + c - RING + 1)
                    three(pe, h_ps[:, c % RING, :],
                          [(w1_hi[:, c, k, :], w1_lo[:, c, k, :], x_hi[:, k, :], x_lo[:, k, :])
                           for k in range(KC)], True, True).then_inc(h_filled, 1)

                def multiply(i, c):
                    if isinstance(i, int) and i == 0:
                        pe.wait_ge(w_lo_done, 2 * c + 2)
                    pe.wait_ge(hid_lo_done, i * NC + c + 1)
                    if c == 0 and at_least(i, 1):
                        pe.wait_ge(summed, i * SUB)
                    for u in range(SUB):
                        cols = slice(u * P, (u + 1) * P)
                        last = three(pe, o_ps[:, u, :],
                                     [(hid_hi[:, c % RING, cols], hid_lo[:, c % RING, cols], w2_hi[:, c, :],
                                       w2_lo[:, c, :])], c == 0, c == NC - 1)
                    last.then_inc(multiplied, 1)

                def body(i, b, s):
                    for c in range(NC):
                        hidden(i, c)
                        if c >= LAG:
                            multiply(i, c - LAG)
                        elif at_least(i, 1):
                            multiply(i - 1, NC - LAG + c)
                on_tiles(pe, body)
                for c in range(NC - LAG, NC):
                    multiply(TILES - 1, c)
        sem.clear()


def layer(nc, a, y):
    def dram(name, shape):
        return nc.dram_tensor(name, shape, F32, kind="Internal").ap()

    def tokens(t):
        return t.rearrange("b (s u p) d -> b s p u d", s=HALVES, p=P)

    qk = {n: dram(n, [B, D, S]) for n in ("sq_hi", "sq_lo", "sk_hi", "sk_lo", "cq_hi", "cq_lo", "ck_hi", "ck_lo")}
    vals = {n: dram(n, [B, NG, KT, P, P]) for n in ("sv", "cv")}
    att = {n: dram(n, [B, D, S]) for n in ("s_att", "c_att")}
    x1, x2 = dram("x1", [B, S, D]), dram("x2", [B, S, D])
    xt_hi, xt_lo = dram("xt_hi", [B, HALVES, P, KC, TOK]), dram("xt_lo", [B, HALVES, P, KC, TOK])

    def chan_home(t, m):
        return t.rearrange("b (c p) (s t) -> c b s p t", p=P, s=HALVES)[m]

    def by_group(t):
        return t.rearrange("b (g p) t -> (b g) p t", p=P)

    def tok_home(t):
        return t.rearrange("b g (s u) p c -> b s g p u c", s=HALVES)

    def att_home(t):
        return t.rearrange("b (c p) (s t) -> b s p c t", p=P, s=HALVES)

    with ExitStack() as ctx:
        sb = lambda name, shape, dt=F32: ctx.enter_context(nc.sbuf_tensor(name, shape, dt))
        ident, ident_bf = sb("ident", [P, P]), sb("ident_bf", [P, P], BF16)
        mask_qk, mask_kq = sb("mask_qk", [P, P], BF16), sb("mask_kq", [P, P], BF16)
        keep = sb("keep", [P, S])
        q_bias, k_bias = sb("q_bias", [P, KC]), sb("k_bias", [P, KC])
        made, biases_loaded = (ctx.enter_context(nc.semaphore(n)) for n in ("made", "biases_loaded"))
        with nc.Block() as block:
            @block.gpsimd
            def _(pool):
                tiles = ((ident, 0.0, ALU.not_equal, 1.0, 1, -1), (ident_bf, 0.0, ALU.not_equal, 1.0, 1, -1),
                         (mask_qk, 0.0, ALU.is_ge, CAUSAL, 1, -1), (mask_kq, 0.0, ALU.is_ge, CAUSAL, -1, 1))
                for t, value, *_ in tiles:
                    pool.memset(t[:], value).then_inc(made, 1)
                pool.wait_ge(made, len(tiles))
                for t, _, op, fill, row, col in tiles:
                    pool.affine_select(out=t[:], in_=t[:], compare_op=op, fill=fill, base=0,
                                       pattern=[[col, P]], channel_multiplier=row).then_inc(made, 1)
                pool.wait_ge(made, 2 * len(tiles))

            @block.sync
            def _(sp):
                sp.dma_start(q_bias[:], a["ca_q_b"]).then_inc(biases_loaded, 16)
                sp.dma_start(k_bias[:], a["ca_k_b"]).then_inc(biases_loaded, 16)
                sp.wait_ge(biases_loaded, 32)

        router_stage(nc, keep, tokens(a["x"]), a["n1_g"], a["n1_b"], a["qkv_w"][:, D:2 * D], a["r_w1"],
                     a["r_b1"], a["r_w2"], a["r_b2"])

        self_scale, cross_scale = float(D) ** -0.5, float(DH) ** -0.5

        def self_q(dve, out, psum, s):
            return dve.scalar_tensor_tensor(out=out, in0=psum, scalar=self_scale, in1=keep[:, s * TOK:(s + 1) * TOK],
                                            op0=ALU.mult, op1=ALU.mult)

        def self_k(dve, out, psum, s):
            return dve.tensor_tensor(out, psum, keep[:, s * TOK:(s + 1) * TOK], ALU.mult)

        def cross_q(m):
            return lambda dve, out, psum, s: dve.tensor_scalar(out, psum, q_bias[:, m:m + 1], cross_scale,
                                                               ALU.add, ALU.mult)

        def cross_k(m):
            return lambda dve, out, psum, s: dve.tensor_scalar(out, psum, k_bias[:, m:m + 1], None, ALU.add)

        third = lambda w, n: w[:, n * D:(n + 1) * D]
        projection_stage(
            nc, "a_", ident, tokens(a["x"]), norm=(a["n1_g"], a["n1_b"]),
            weights=[third(a["qkv_w"], n) for n in range(3)],
            chans=[(m, self_q, chan_home(qk["sq_hi"], m), chan_home(qk["sq_lo"], m)) for m in range(KC)]
            + [(KC + m, self_k, chan_home(qk["sk_hi"], m), chan_home(qk["sk_lo"], m)) for m in range(KC)],
            toks=(2, None, tok_home(vals["sv"])))
        attention_stage(nc, "b_", ident, *(by_group(qk[n]) for n in ("sq_hi", "sq_lo", "sk_hi", "sk_lo")),
                        vals["sv"].rearrange("b g k p c -> (b g) k p c"), by_group(att["s_att"]),
                        keep, mask_qk, mask_kq, ident_bf)
        projection_stage(
            nc, "d_", ident, tokens(a["ctx"]), weights=[third(a["ca_in_w"], n) for n in (1, 2)],
            chans=[(m, cross_k(m), chan_home(qk["ck_hi"], m), chan_home(qk["ck_lo"], m)) for m in range(KC)],
            toks=(1, a["ca_v_b"], tok_home(vals["cv"])))
        projection_stage(
            nc, "c_", ident, tokens(a["x"]), mix=(att_home(att["s_att"]), a["sa_out_w"], a["sa_out_b"], tokens(x1)),
            norm=(a["n2_g"], a["n2_b"]), weights=[third(a["ca_in_w"], 0)],
            chans=[(m, cross_q(m), chan_home(qk["cq_hi"], m), chan_home(qk["cq_lo"], m)) for m in range(KC)])
        attention_stage(nc, "e_", ident, *(by_group(qk[n]) for n in ("cq_hi", "cq_lo", "ck_hi", "ck_lo")),
                        vals["cv"].rearrange("b g k p c -> (b g) k p c"), by_group(att["c_att"]))
        projection_stage(
            nc, "f_", ident, tokens(x1), mix=(att_home(att["c_att"]), a["ca_out_w"], a["ca_out_b"], tokens(x2)),
            norm=(a["n3_g"], a["n3_b"]), keep_xt=(xt_hi, xt_lo))
        mlp_stage(nc, xt_hi, xt_lo, tokens(x2), a["ff_w1"], a["ff_b1"], a["ff_w2"], a["ff_b2"], tokens(y))


def kernel(**inputs):
    import numpy as np
    from concourse import bacc
    from concourse.bass_utils import run_bass_kernel_spmd

    given = {n.removeprefix("L0_xattn_"): np.asarray(v) for n, v in inputs.items()}
    columns = lambda v: np.ascontiguousarray(v.reshape(-1, P).T)
    turned = lambda w: np.ascontiguousarray(w.T)
    ca_b = given["ca_in_b"]
    arrays = {
        "x": given["x"], "ctx": given["ctx_1024"],
        "qkv_w": turned(given["qkv_w"]), "sa_out_w": turned(given["sa_out_w"]), "sa_out_b": given["sa_out_b"],
        "r_w1": turned(given["r_w1"]), "r_b1": columns(given["r_b1"]), "r_w2": turned(given["r_w2"]),
        "r_b2": given["r_b2"],
        "ca_in_w": turned(given["ca_in_w"]), "ca_q_b": columns(ca_b[0:D]), "ca_k_b": columns(ca_b[D:2 * D]),
        "ca_v_b": np.ascontiguousarray(ca_b[2 * D:]), "ca_out_w": turned(given["ca_out_w"]),
        "ca_out_b": given["ca_out_b"],
        "ff_w1": turned(given["ff_w1"]), "ff_b1": columns(given["ff_b1"]), "ff_w2": turned(given["ff_w2"]),
        "ff_b2": given["ff_b2"],
        **{f"n{n}_{c}": columns(given[f"n{n}_{c}"]) for n in (1, 2, 3) for c in "gb"},
    }
    nc = bacc.Bacc("TRN2", target_bir_lowering=False, num_devices=1)
    feeds, aps = {}, {}
    for name, v in arrays.items():
        v = np.ascontiguousarray(v)
        feeds[f"in_{name}"] = v
        aps[name] = nc.dram_tensor(f"in_{name}", v.shape, mybir.dt.from_np(v.dtype), kind="ExternalInput").ap()
    y = nc.dram_tensor("out_y", (B, S, D), F32, kind="ExternalOutput").ap()
    layer(nc, aps, y)
    r = run_bass_kernel_spmd(nc, [feeds], core_ids=[0])
    return r.results[0]["out_y"]
```

```python
from contextlib import ExitStack

import concourse.bass as bass
from concourse import mybir

ALU = mybir.AluOpType
ACT = mybir.ActivationFunctionType
AX = mybir.AxisListType
F32 = mybir.dt.float32
F32R = mybir.dt.float32r
BF16 = mybir.dt.bfloat16

P = 128
B, S, D = 4, 1024, 512
H, DH = 16, 32
HG = P // DH
NG = H // HG
FF = 2048
BLOCK = 64
NBLK = S // BLOCK
TOK = 512
SUB = TOK // P
HALVES = S // TOK
TILES = B * HALVES
KC = D // P
KT = S // P
NEG = -1.0e9
CAUSAL = -1.0e30
EPS = 1e-5
AUG = 3 * DH
MASK_ROW, MAX_HI_ROW, MAX_LO_ROW = AUG, AUG + 1, AUG + 2
ROWS = AUG + 3


def on_tiles(eng, body):
    body(0, 0, 0)
    with eng.Fori(0, B - 2) as j:
        body(j * 2 + 1, j, 1)
        body(j * 2 + 2, j + 1, 0)
    for i in range(TILES - 3, TILES):
        body(i, i // HALVES, i % HALVES)


def nxt(i, b, s):
    return (i + 1, b, 1) if s == 0 else (i + 1, b + 1, 0)


def at_least(i, n):
    return i >= n if isinstance(i, int) else True


def wait_alone(eng, sem, value, passed):
    eng.wait_ge(sem, value)
    eng.sem_inc(passed, 1)


class Semaphores:

    def __init__(self, nc, ctx, tag):
        self.nc, self.ctx, self.tag, self.all = nc, ctx, tag, []

    def __call__(self, name):
        self.all.append(self.ctx.enter_context(self.nc.semaphore(self.tag + name)))
        return self.all[-1]

    def clear(self):
        numbers = sorted(s.num for s in self.all)
        starts = [n for n in numbers if n - 1 not in numbers]
        with self.nc.Block() as block:
            @block.sync
            def _(sp):
                for start in starts:
                    end = start
                    while end in numbers:
                        end += 1
                    sp.sem_clear(range(start, end))


def three(pe, out, pairs, start, stop):
    last = None
    for n, (wh, wl, xh, xl) in enumerate(pairs):
        for m, (w, x) in enumerate(((wh, xh), (wh, xl), (wl, xh))):
            last = pe.matmul(out, w, x, start=(start and n == 0 and m == 0),
                             stop=(stop and n == len(pairs) - 1 and m == 2))
    return last


def router_stage(nc, keep, x_tiles, ln_g, ln_b, wk, r_w1, r_b1, r_w2, r_b2):
    with ExitStack() as ctx:
        sb = lambda name, shape, dt=F32: ctx.enter_context(nc.sbuf_tensor("r_" + name, shape, dt))
        sem = Semaphores(nc, ctx, "r_")
        x = sb("x", [P, HALVES * SUB, D])
        xn = sb("xn", [P, HALVES * SUB, D])
        wk_sb = sb("wk", [P, KC, D])
        w1 = sb("w1", [P, KC, P])
        w2 = sb("w2", [P, 1])
        w2_all = sb("w2_all", [P, P])
        gb = sb("gb", [P, 2, KC])
        b1 = sb("b1", [P, 1])
        b2 = sb("b2", [P, 1])
        stats = sb("stats", [P, KT, 6])
        mv = sb("mv", [P, KT, 2])
        var = sb("var", [P, KT])
        rstd = sb("rstd", [P, KT])
        power = sb("power", [P, KT])
        averager = sb("averager", [P, 2])
        means = sb("means", [P, KC, NBLK])
        key_means = sb("key_means", [P, KC, NBLK])
        hidden = sb("hidden", [P, NBLK])
        kept = sb("kept", [P, NBLK])
        ps = ctx.enter_context(nc.psum_tensor("r_ps", [P, 4, 512], F32))
        loaded_x, loaded_w, consts = sem("loaded_x"), sem("loaded_w"), sem("consts")
        v_step, rstd_ready = sem("v_step"), sem("rstd_ready")
        normed, meaned, scaled, keyed = sem("normed"), sem("meaned"), sem("scaled"), sem("keyed")
        keys_copied, hid_ready, relu_done, logits = (sem("keys_copied"), sem("hid_ready"),
                                                     sem("relu_done"), sem("logits"))
        with nc.Block() as block:
            @block.sync
            def _(sp):
                for s in range(HALVES):
                    sp.dma_start(x[:, s * SUB:(s + 1) * SUB, :], x_tiles[0, s]).then_inc(loaded_x, 16)
                sp.dma_start(wk_sb[:], wk.rearrange("(c p) n -> p c n", p=P)).then_inc(loaded_w, 16)
                sp.dma_start(w1[:], r_w1.rearrange("(c p) n -> p c n", p=P)).then_inc(loaded_w, 16)
                sp.dma_start(w2[:], r_w2).then_inc(loaded_w, 16)
                sp.dma_start(gb[:, 0, :], ln_g).then_inc(loaded_w, 16)
                sp.dma_start(gb[:, 1, :], ln_b).then_inc(loaded_w, 16)
                sp.dma_start(b1[:], r_b1).then_inc(loaded_w, 16)
                sp.dma_start(b2[:], r_b2.partition_broadcast(P)).then_inc(loaded_w, 16)

            @block.gpsimd
            def _(pool):
                pool.memset(averager[:], 0.0).then_inc(consts, 1)
                pool.memset(power[:], -0.5).then_inc(consts, 1)
                pool.wait_ge(consts, 2)
                for h in range(2):
                    pool.memset(averager[h * BLOCK:(h + 1) * BLOCK, h:h + 1], 1.0 / BLOCK).then_inc(consts, 1)
                pool.wait_ge(consts, 4)
                pool.wait_ge(v_step, 2)
                pool.tensor_tensor(rstd[:], var[:], power[:], ALU.pow).then_inc(rstd_ready, 1)

            @block.vector
            def _(dve):
                dve.wait_ge(loaded_x, 16 * HALVES)
                for t in range(KT):
                    last = dve.bn_stats(stats[:, t, :], x[:, t, :])
                last.then_inc(v_step, 1)
                dve.wait_ge(v_step, 1)
                for t in range(KT):
                    last = dve.bn_aggr(mv[:, t, :], stats[:, t, :])
                last.then_inc(normed, 1)
                dve.wait_ge(normed, 1)
                dve.tensor_scalar_add(var[:], mv[:, :, 1], EPS).then_inc(v_step, 1)
                dve.wait_ge(rstd_ready, 1)
                for t in range(KT):
                    dve.tensor_scalar(xn[:, t, :], x[:, t, :], mv[:, t, 0:1], rstd[:, t:t + 1],
                                      ALU.subtract, ALU.mult).then_inc(normed, 1)
                dve.wait_ge(loaded_w, 16 * 7)
                dve.tensor_copy(w2_all[:], w2[:, 0:1].to_broadcast([P, P])).then_inc(v_step, 1)
                dve.wait_ge(meaned, 1)
                for c in range(KC):
                    last = dve.tensor_scalar(means[:, c, :], ps[:, 0, c * NBLK:(c + 1) * NBLK],
                                             gb[:, 0, c:c + 1], gb[:, 1, c:c + 1], ALU.mult, ALU.add)
                last.then_inc(scaled, 1)
                dve.wait_ge(keyed, 1)
                dve.tensor_copy(key_means[:].rearrange("p c n -> p (c n)"),
                                ps[:, 1, 0:KC * NBLK]).then_inc(keys_copied, 1)
                dve.wait_ge(hid_ready, 1)
                dve.tensor_scalar(hidden[:], ps[:, 2, 0:NBLK], b1[:, 0:1], 0.0, ALU.add,
                                  ALU.max).then_inc(relu_done, 1)
                dve.wait_ge(logits, 1)
                dve.tensor_scalar(kept[:], ps[:, 3, 0:NBLK], b2[:, 0:1], 0.0, ALU.add,
                                  ALU.is_gt).then_inc(v_step, 1)
                dve.wait_ge(v_step, 4)
                dve.tensor_copy(keep[:].rearrange("p (n t) -> p n t", t=BLOCK),
                                kept[:].unsqueeze(2).to_broadcast([P, NBLK, BLOCK])).then_inc(v_step, 1)
                dve.wait_ge(v_step, 5)

            @block.tensor
            def _(pe):
                pe.wait_ge(consts, 4)
                for t in range(KT):
                    pe.wait_ge(normed, t + 2)
                    for c in range(KC):
                        last = pe.matmul(ps[:, 0, c * NBLK + 2 * t:c * NBLK + 2 * t + 2],
                                         xn[:, t, c * P:(c + 1) * P], averager[:], start=True, stop=True)
                last.then_inc(meaned, 1)
                pe.wait_ge(loaded_w, 16 * 7)
                pe.wait_ge(scaled, 1)
                for m in range(KC):
                    for c in range(KC):
                        last = pe.matmul(ps[:, 1, m * NBLK:(m + 1) * NBLK], wk_sb[:, c, m * P:(m + 1) * P],
                                         means[:, c, :], start=(c == 0), stop=(c == KC - 1))
                last.then_inc(keyed, 1)
                pe.wait_ge(keys_copied, 1)
                for c in range(KC):
                    last = pe.matmul(ps[:, 2, 0:NBLK], w1[:, c, :], key_means[:, c, :],
                                     start=(c == 0), stop=(c == KC - 1))
                last.then_inc(hid_ready, 1)
                pe.wait_ge(v_step, 3)
                pe.wait_ge(relu_done, 1)
                pe.matmul(ps[:, 3, 0:NBLK], w2_all[:], hidden[:], start=True, stop=True).then_inc(logits, 1)
        sem.clear()


def projection_stage(nc, tag, ident, src, mix=None, norm=None, weights=(), chans=(), toks=None,
                     keep_xt=None):
    RING = 4
    has_mix = mix is not None
    n_mix, n_chan, n_tok = (SUB if has_mix else 0), len(chans), (SUB if toks else 0)
    per_tile = n_mix + n_chan + n_tok
    work = [("chan", k) for k in range(n_chan)] + [("tok", k) for k in range(n_tok)]
    halves = (work[:len(work) // 2], work[len(work) // 2:])
    assert n_chan % RING == 0 and n_tok % RING == 0

    def mix_seq(i, k):
        if isinstance(i, int) and i < 2:
            return i * n_mix + k
        return 2 * n_mix + (i - 2) * per_tile + k

    def work_seq(i, k):
        if isinstance(i, int) and i >= TILES - 2:
            return 2 * n_mix + (TILES - 2) * per_tile + (i - TILES + 2) * len(work) + k
        return 2 * n_mix + i * per_tile + n_mix + k

    with ExitStack() as ctx:
        sb = lambda name, shape, dt=F32: ctx.enter_context(nc.sbuf_tensor(tag + name, shape, dt))
        sem = Semaphores(nc, ctx, tag)
        n_w = len(weights)
        w_hi = sb("w_hi", [P, max(n_w, 1), KC, D], F32R) if n_w else None
        w_lo = sb("w_lo", [P, max(n_w, 1), KC, D], F32R) if n_w else None
        raw = sb("raw", [P, 4, D])
        x = sb("x", [P, 2, SUB, D])
        x_hi = sb("x_hi", [P, 2, KC, TOK], F32R)
        x_lo = sb("x_lo", [P, 2, KC, TOK], F32R)
        xt = sb("xt", [P, KC, TOK])
        tr = ctx.enter_context(nc.psum_tensor(tag + "tr", [P, 2, TOK], F32))
        ring = ctx.enter_context(nc.psum_tensor(tag + "ring", [P, RING, 512], F32))
        if norm:
            xn = sb("xn", [P, 2, SUB, D])
            stats = sb("stats", [P, SUB, 6])
            mv = sb("mv", [P, SUB, 2])
            var = sb("var", [P, SUB])
            rstd = sb("rstd", [P, SUB])
            power = sb("power", [P, SUB])
            gb = sb("gb", [P, 2, KC])
        if has_mix:
            o = sb("o", [P, KC, TOK])
            o_hi = sb("o_hi", [P, KC, TOK], F32R)
            o_lo = sb("o_lo", [P, KC, TOK], F32R)
            o_bias = sb("o_bias", [P, D])
            ow_hi = sb("ow_hi", [P, KC, D], F32R)
            ow_lo = sb("ow_lo", [P, KC, D], F32R)
        if n_chan:
            full = sb("full", [P, 4, TOK])
            part_hi = sb("part_hi", [P, 4, TOK], F32R)
            part_lo = sb("part_lo", [P, 4, TOK], F32R)
        if toks:
            tok_out = sb("tok_out", [P, 2, SUB, D])
            tok_bias = sb("tok_bias", [P, D])

        sp_passed, dve_passed = sem("sp_passed"), sem("dve_passed")
        raw_loaded = [sem(f"raw_loaded{k}") for k in range(4)]
        w_hi_done, w_lo_done, small_loaded = sem("w_hi_done"), sem("w_lo_done"), sem("small_loaded")
        x_loaded = [sem(f"x_loaded{k}") for k in range(2)]
        o_loaded, o_hi_done, o_lo_done = sem("o_loaded"), sem("o_hi_done"), sem("o_lo_done")
        biased, x_stored = sem("biased"), [sem(f"x_stored{k}") for k in range(2)]
        stat_step, aggregated, var_ready, rstd_ready, normed = (sem("stat_step"), sem("aggregated"),
                                                               sem("var_ready"), sem("rstd_ready"), sem("normed"))
        power_set = sem("power_set")
        turned, turned_out, x_hi_done, x_lo_done = sem("turned"), sem("turned_out"), sem("x_hi_done"), sem("x_lo_done")
        xt_stored = [sem(f"xt_stored{k}") for k in range(2)]
        filled, emptied = sem("filled"), sem("emptied")
        hi_ready, lo_ready = sem("hi_ready"), sem("lo_ready")
        hi_stored = [sem(f"hi_stored{k}") for k in range(4)]
        lo_stored = [sem(f"lo_stored{k}") for k in range(4)]
        tok_stored = [sem(f"tok_stored{k}") for k in range(2)]

        pieces = []
        if has_mix:
            pieces += [(mix[1][c * P:(c + 1) * P, :], ow_hi[:, c, :], ow_lo[:, c, :]) for c in range(KC)]
        n_mix_pieces = len(pieces)
        n_first = n_mix_pieces + (KC if n_w else 0)
        for n, w in enumerate(weights):
            pieces += [(w[c * P:(c + 1) * P, :], w_hi[:, n, c, :], w_lo[:, n, c, :]) for c in range(KC)]
        small = []
        if norm:
            small += [(gb[:, 0, :], norm[0]), (gb[:, 1, :], norm[1])]
        if has_mix:
            small += [(o_bias[:], mix[2].partition_broadcast(P))]
        if toks and toks[1] is not None:
            small += [(tok_bias[:], toks[1].partition_broadcast(P))]

        with nc.Block() as block:
            @block.sync
            def _(sp):
                def load_x(i, b, s):
                    if at_least(i, 2):
                        if norm:
                            wait_alone(sp, normed, (i - 1) * SUB, sp_passed)
                        else:
                            wait_alone(sp, turned, (i - 1) * KC, sp_passed)
                        if has_mix:
                            wait_alone(sp, x_stored[s], b * 16, sp_passed)
                    sp.dma_start(x[:, s], src[b, s]).then_inc(x_loaded[s], 16)

                def load_o(i, b, s):
                    if at_least(i, 1):
                        wait_alone(sp, o_lo_done, i * KC, sp_passed)
                    sp.dma_start(o[:], mix[0][b, s]).then_inc(o_loaded, 16)

                def load_pieces(numbers):
                    for u in numbers:
                        if u >= 4:
                            sp.wait_ge(w_lo_done, u - 3)
                        sp.dma_start(raw[:, u % 4, :], pieces[u][0]).then_inc(raw_loaded[u % 4], 16)

                def store_x(i, b, s):
                    wait_alone(sp, emptied, mix_seq(i, SUB - 1) + 1, sp_passed)
                    sp.dma_start(mix[3][b, s], x[:, s]).then_inc(x_stored[s], 16)

                load_x(0, 0, 0)
                for dst, row in small:
                    sp.dma_start(dst, row).then_inc(small_loaded, 16)
                if has_mix:
                    load_o(0, 0, 0)
                load_pieces(range(n_first))
                load_x(1, 0, 1)
                if has_mix:
                    load_o(1, 0, 1)
                    store_x(0, 0, 0)
                load_pieces(range(n_first, len(pieces)))
                if has_mix:
                    store_x(1, 0, 1)
                    load_o(2, 1, 0)
                load_x(2, 1, 0)

                def body(i, b, s):
                    last = isinstance(i, int) and i == TILES - 1
                    one = nxt(i, b, s)
                    ahead = TILES - 1 - i if isinstance(i, int) else 3
                    if has_mix and ahead >= 2:
                        store_x(i + 2, b + 1, s)
                    if ahead >= 3:
                        three_on = nxt(i + 2, b + 1, s)
                        if has_mix:
                            load_o(*three_on)
                        load_x(*three_on)
                    if keep_xt and not last:
                        wait_alone(sp, x_lo_done, (one[0] + 1) * KC, sp_passed)
                        for part, home in ((x_hi, keep_xt[0]), (x_lo, keep_xt[1])):
                            sp.dma_start(home[one[1], one[2]], part[:, one[2]].bitcast(F32)).then_inc(xt_stored[one[2]], 16)
                    for kind, k in work:
                        if kind == "chan":
                            c = i * n_chan + k
                            wait_alone(sp, hi_ready, c + 1, sp_passed)
                            sp.dma_start(chans[k][2][b, s], part_hi[:, k % 4, :].bitcast(F32)).then_inc(hi_stored[k % 4], 16)
                            wait_alone(sp, lo_ready, c + 1, sp_passed)
                            sp.dma_start(chans[k][3][b, s], part_lo[:, k % 4, :].bitcast(F32)).then_inc(lo_stored[k % 4], 16)
                        elif k == SUB - 1:
                            wait_alone(sp, emptied, work_seq(i, n_chan + k) + 1, sp_passed)
                            for g in range(NG):
                                sp.dma_start(toks[2][b, s, g], tok_out[:, s, :, g * P:(g + 1) * P]).then_inc(tok_stored[s], 16)

                if keep_xt:
                    sp.wait_ge(x_lo_done, KC)
                    for part, home in ((x_hi, keep_xt[0]), (x_lo, keep_xt[1])):
                        sp.dma_start(home[0, 0], part[:, 0].bitcast(F32)).then_inc(xt_stored[0], 16)
                on_tiles(sp, body)
                for s in range(2):
                    if has_mix:
                        sp.wait_ge(x_stored[s], 16 * TILES // 2)
                    if keep_xt:
                        sp.wait_ge(xt_stored[s], 32 * TILES // 2)
                    if toks:
                        sp.wait_ge(tok_stored[s], 16 * NG * TILES // 2)
                for k in range(4 if n_chan else 0):
                    sp.wait_ge(hi_stored[k], 16 * TILES * n_chan // 4)
                    sp.wait_ge(lo_stored[k], 16 * TILES * n_chan // 4)

            def schedule(eng, prepare, split, mixing, turning, working):
                prepare(range(n_first))
                if has_mix:
                    split(0, 0, 0)
                mixing(0, 0, 0)
                if has_mix:
                    split(1, 0, 1)
                mixing(1, 0, 1)
                turning(0, 0, 0)
                prepare(range(n_first, len(pieces)))
                if has_mix:
                    split(2, 1, 0)

                def body(i, b, s):
                    ahead = TILES - 1 - i if isinstance(i, int) else 3
                    if ahead >= 2:
                        mixing(i + 2, b + 1, s)
                    working(i, b, s, 0)
                    if ahead >= 1:
                        turning(*nxt(i, b, s))
                    if has_mix and ahead >= 3:
                        split(*nxt(i + 2, b + 1, s))
                    working(i, b, s, 1)
                on_tiles(eng, body)

            @block.scalar
            def _(act):
                if small:
                    act.wait_ge(small_loaded, 16 * len(small))

                def prepare(numbers):
                    for u in numbers:
                        act.wait_ge(raw_loaded[u % 4], 16 * (u // 4 + 1))
                        act.copy(pieces[u][1], raw[:, u % 4, :]).then_inc(w_hi_done, 1)

                def split(i, b, s):
                    act.wait_ge(o_loaded, (i + 1) * 16)
                    if at_least(i, 1):
                        act.wait_ge(filled, mix_seq(i - 1, SUB - 1) + 1)
                    for c in range(KC):
                        act.copy(o_hi[:, c, :], o[:, c, :]).then_inc(o_hi_done, 1)

                def mixing(i, b, s):
                    pass

                def turning(i, b, s):
                    for c in range(KC):
                        act.wait_ge(turned, i * KC + c + 1)
                        if at_least(i, 1):
                            act.wait_ge(x_lo_done, (i - 1) * KC + c + 1)
                        if norm:
                            act.activation(xt[:, c, :], tr[:, c % 2, :], ACT.Identity, bias=gb[:, 1, c:c + 1],
                                           scale=gb[:, 0, c:c + 1]).then_inc(turned_out, 1)
                        else:
                            act.copy(xt[:, c, :], tr[:, c % 2, :]).then_inc(turned_out, 1)

                def working(i, b, s, half):
                    for kind, k in halves[half]:
                        if kind == "chan":
                            uses = i * (n_chan // 4) + k // 4
                            act.wait_ge(emptied, work_seq(i, k) + 1)
                            if k >= 4 or at_least(i, 1):
                                act.wait_ge(hi_stored[k % 4], uses * 16)
                                act.wait_ge(lo_ready, i * n_chan + k - 3)
                            act.copy(part_hi[:, k % 4, :], full[:, k % 4, :]).then_inc(hi_ready, 1)

                schedule(act, prepare, split, mixing, turning, working)

            @block.gpsimd
            def _(pool):
                if norm:
                    pool.memset(power[:], -0.5).then_inc(power_set, 1)
                    pool.wait_ge(power_set, 1)
                if small:
                    pool.wait_ge(small_loaded, 16 * len(small))

                def prepare(numbers):
                    for u in numbers:
                        pool.wait_ge(w_hi_done, u + 1)
                        pool.tensor_tensor(pieces[u][2], raw[:, u % 4, :], pieces[u][1].bitcast(F32),
                                           ALU.subtract).then_inc(w_lo_done, 1)

                def split(i, b, s):
                    for c in range(KC):
                        pool.wait_ge(o_hi_done, i * KC + c + 1)
                        if at_least(i, 1) and c == 0:
                            pool.wait_ge(filled, mix_seq(i - 1, SUB - 1) + 1)
                        pool.tensor_tensor(o_lo[:, c, :], o[:, c, :], o_hi[:, c, :].bitcast(F32),
                                           ALU.subtract).then_inc(o_lo_done, 1)

                def mixing(i, b, s):
                    if has_mix:
                        pool.wait_ge(x_loaded[s], (b + 1) * 16)
                        for u in range(SUB):
                            pool.tensor_tensor(x[:, s, u, :], x[:, s, u, :], o_bias[:], ALU.add).then_inc(biased, 1)
                    if norm:
                        pool.wait_ge(var_ready, i + 1)
                        pool.tensor_tensor(rstd[:], var[:], power[:], ALU.pow).then_inc(rstd_ready, 1)

                def turning(i, b, s):
                    for c in range(KC):
                        pool.wait_ge(x_hi_done, i * KC + c + 1)
                        if c == 0 and keep_xt and at_least(i, 2):
                            pool.wait_ge(xt_stored[s], b * 32)
                        pool.tensor_tensor(x_lo[:, s, c, :], xt[:, c, :], x_hi[:, s, c, :].bitcast(F32),
                                           ALU.subtract).then_inc(x_lo_done, 1)

                def working(i, b, s, half):
                    for kind, k in halves[half]:
                        if kind == "chan":
                            uses = i * (n_chan // 4) + k // 4
                            pool.wait_ge(hi_ready, i * n_chan + k + 1)
                            if k >= 4 or at_least(i, 1):
                                pool.wait_ge(lo_stored[k % 4], uses * 16)
                            pool.tensor_tensor(part_lo[:, k % 4, :], full[:, k % 4, :],
                                               part_hi[:, k % 4, :].bitcast(F32), ALU.subtract).then_inc(lo_ready, 1)

                schedule(pool, prepare, split, mixing, turning, working)

            @block.vector
            def _(dve):
                def prepare(numbers):
                    pass

                def split(i, b, s):
                    pass

                def mixing(i, b, s):
                    dve.wait_ge(x_loaded[s], (b + 1) * 16)
                    if has_mix:
                        for u in range(SUB):
                            dve.wait_ge(biased, i * SUB + u + 1)
                            dve.wait_ge(filled, mix_seq(i, u) + 1)
                            dve.tensor_tensor(x[:, s, u, :], ring[:, u % RING, :], x[:, s, u, :],
                                              ALU.add).then_inc(emptied, 1)
                        dve.wait_ge(emptied, mix_seq(i, SUB - 1) + 1)
                    if not norm:
                        return
                    for u in range(SUB):
                        last = dve.bn_stats(stats[:, u, :], x[:, s, u, :])
                    last.then_inc(stat_step, 1)
                    wait_alone(dve, stat_step, i + 1, dve_passed)
                    for u in range(SUB):
                        last = dve.bn_aggr(mv[:, u, :], stats[:, u, :])
                    last.then_inc(aggregated, 1)
                    dve.wait_ge(aggregated, i + 1)
                    dve.tensor_scalar_add(var[:], mv[:, :, 1], EPS).then_inc(var_ready, 1)
                    dve.wait_ge(rstd_ready, i + 1)
                    if at_least(i, 2):
                        dve.wait_ge(turned, (i - 1) * KC)
                    for u in range(SUB):
                        dve.tensor_scalar(xn[:, s, u, :], x[:, s, u, :], mv[:, u, 0:1], rstd[:, u:u + 1],
                                          ALU.subtract, ALU.mult).then_inc(normed, 1)

                def turning(i, b, s):
                    for c in range(KC):
                        dve.wait_ge(turned_out, i * KC + c + 1)
                        if c == 0 and at_least(i, 2):
                            if work:
                                dve.wait_ge(filled, work_seq(i - 2, len(work) - 1) + 1)
                            if keep_xt:
                                dve.wait_ge(xt_stored[s], b * 32)
                            dve.wait_ge(x_lo_done, (i - 1) * KC)
                        dve.tensor_copy(x_hi[:, s, c, :], xt[:, c, :]).then_inc(x_hi_done, 1)

                def working(i, b, s, half):
                    for n, (kind, k) in enumerate(halves[half]):
                        q = half * len(halves[0]) + n
                        dve.wait_ge(filled, work_seq(i, q) + 1)
                        bank = ring[:, q % RING, :]
                        if kind == "chan":
                            if k >= 4 or at_least(i, 1):
                                dve.wait_ge(lo_ready, i * n_chan + k - 3)
                            chans[k][1](dve, full[:, k % 4, :], bank, s).then_inc(emptied, 1)
                        else:
                            if k == 0 and at_least(i, 2):
                                dve.wait_ge(tok_stored[s], b * 16 * NG)
                            if k == 0 and isinstance(i, int) and i == 0 and small:
                                dve.wait_ge(small_loaded, 16 * len(small))
                            out = tok_out[:, s, k, :]
                            ins = (dve.tensor_tensor(out, bank, tok_bias[:], ALU.add) if toks[1] is not None
                                   else dve.tensor_copy(out, bank))
                            ins.then_inc(emptied, 1)

                schedule(dve, prepare, split, mixing, turning, working)

            @block.tensor
            def _(pe):
                def bank_free(seq, q, i):
                    if not (isinstance(seq, int) and seq < RING):
                        pe.wait_ge(emptied, seq - RING + 1)

                def prepare(numbers):
                    pass

                def split(i, b, s):
                    pass

                def mixing(i, b, s):
                    if not has_mix:
                        return
                    if isinstance(i, int) and i == 0:
                        pe.wait_ge(w_lo_done, n_mix_pieces)
                    pe.wait_ge(o_lo_done, (i + 1) * KC)
                    for u in range(SUB):
                        bank_free(mix_seq(i, u), u, i)
                        cols = slice(u * P, (u + 1) * P)
                        three(pe, ring[:, u % RING, :],
                                     [(o_hi[:, c, cols], o_lo[:, c, cols], ow_hi[:, c, :], ow_lo[:, c, :])
                                      for c in range(KC)], True, True).then_inc(filled, 1)

                def turning(i, b, s):
                    if norm:
                        pe.wait_ge(normed, (i + 1) * SUB)
                    else:
                        pe.wait_ge(x_loaded[s], (b + 1) * 16)
                    tokens = (xn if norm else x)[:, s]
                    for c in range(KC):
                        if c >= 2 or at_least(i, 1):
                            pe.wait_ge(turned_out, i * KC + c - 1)
                        for u in range(SUB):
                            last = pe.transpose(tr[:, c % 2, u * P:(u + 1) * P],
                                                tokens[:, u, c * P:(c + 1) * P], ident[:])
                        last.then_inc(turned, 1)

                def working(i, b, s, half):
                    if not work:
                        return
                    if half == 0:
                        pe.wait_ge(x_lo_done, (i + 1) * KC)
                    for n, (kind, k) in enumerate(halves[half]):
                        q = half * len(halves[0]) + n
                        bank_free(work_seq(i, q), q, i)
                        if isinstance(i, int) and i == 0:
                            used = chans[k][0] // KC if kind == "chan" else toks[0]
                            pe.wait_ge(w_lo_done, n_mix_pieces + (used + 1) * KC)
                        bank = ring[:, q % RING, :]
                        if kind == "chan":
                            w, m = divmod(chans[k][0], KC)
                            cols = slice(m * P, (m + 1) * P)
                            pairs = [(w_hi[:, w, c, cols], w_lo[:, w, c, cols], x_hi[:, s, c, :], x_lo[:, s, c, :])
                                     for c in range(KC)]
                        else:
                            cols = slice(k * P, (k + 1) * P)
                            pairs = [(x_hi[:, s, c, cols], x_lo[:, s, c, cols], w_hi[:, toks[0], c, :],
                                      w_lo[:, toks[0], c, :]) for c in range(KC)]
                        three(pe, bank, pairs, True, True).then_inc(filled, 1)

                schedule(pe, prepare, split, mixing, turning, working)
        sem.clear()


def attention_stage(nc, tag, ident, q_hi, q_lo, k_hi, k_lo, v, out, keep=None, mask_qk=None,
                    mask_kq=None, ident_bf=None):
    causal = keep is not None
    N = B * NG
    SETS = 3
    steps = [(h, t, max(0, t * P - h * TOK) if causal else 0) for h in range(HALVES)
             for t in range((h + 1) * TOK // P if causal else KT)]
    last_step = {h: max(n for n, st in enumerate(steps) if st[0] == h) for h in range(HALVES)}
    NS, NBLOCKS = len(steps), len(steps) * HG
    UNITS = HG * KT
    PR = 6
    LAG = 3
    TURN_BANK = 2
    TURN, TURN_HEAD = NS - LAG, 2
    pairs = list(range(0, NS, 2))
    summing = [[((i + 3 + c) // NS, i, c) for i in pairs for c in range(2) if (i + 3 + c) % NS == k]
               for k in range(NS)]
    NP = len(pairs)
    COPY, NORMALISE = 3, 4
    after_half = lambda k, lag: [(h, (last_step[h] + lag) // NS) for h in range(HALVES)
                                 if (last_step[h] + lag) % NS == k]
    CH = TOK // 4
    assert SETS * NS % PR == 0 and NBLOCKS % 2 == 0
    START = TURN * HG + TURN_HEAD
    free = []
    for at in range(NBLOCKS):
        k, j = divmod((START + at) % NBLOCKS, HG)
        free.append(150 + TOK - steps[k][2] if j in (0, 2) else 0)
    place, acc = [], 0.0
    unit_size = [0.3 + ((u % KT) + 1 if causal else KT) for u in range(UNITS)]
    for u in range(UNITS):
        x, at = acc / sum(unit_size) * sum(free), 0
        while x >= free[at]:
            x -= free[at]
            at += 1
        place.append(START + at - NBLOCKS)
        acc += unit_size[u]
    if causal:
        bank_of = [(0, 1, 2, 3, 0, 2, 0, 2)[u % KT] for u in range(UNITS)]
        reach = [(2, 3, 3, 4, 3, 2, 2, 2)[u % KT] for u in range(UNITS)]
    else:
        bank_of, reach = [u % 2 * 2 for u in range(UNITS)], [2] * UNITS
    next_units = [[[u for u in range(UNITS) if place[u] == k * HG + j] for j in range(HG)] for k in range(NS)]
    later_units = [[[u for u in range(UNITS) if place[u] + NBLOCKS == k * HG + j] for j in range(HG)]
                   for k in range(NS)]
    early_units = [u for u in range(UNITS) if place[u] < 0]

    with ExitStack() as ctx:
        sb = lambda name, shape, dt=F32: ctx.enter_context(nc.sbuf_tensor(tag + name, shape, dt))
        sem = Semaphores(nc, ctx, tag)
        qs = [sb(f"qs{p}", [P, HG, S], F32R) for p in range(SETS)]
        ks = [sb(f"ks{p}", [P, HG, S], F32R) for p in range(SETS)]
        vs = [sb(f"vs{p}", [P, KT, P]) for p in range(SETS)]
        probs = sb("probs", [P, PR, HG, TOK])
        ones = sb("ones", [P, DH])
        neg_max = sb("neg_max", [P, UNITS])
        max_hi = sb("max_hi", [UNITS, P], F32R)
        max_lo = sb("max_lo", [UNITS, P], F32R)
        sums = sb("sums", [P, HALVES, TOK])
        outs = sb("outs", [P, HALVES, TOK])
        nat = ctx.enter_context(nc.psum_tensor(tag + "nat", [P, 4, 512], F32))
        st_ps = ctx.enter_context(nc.psum_tensor(tag + "st", [P, 2, 512], F32))
        pv_ps = ctx.enter_context(nc.psum_tensor(tag + "pv", [P, 512], F32))
        sum_ps = ctx.enter_context(nc.psum_tensor(tag + "sum", [P, 512], F32))

        consts_set, ones_set, sp_passed = sem("consts_set"), sem("ones_set"), sem("sp_passed")
        paired = sem("paired")
        loaded = [sem(f"loaded{p}") for p in range(SETS)]
        rows_loaded = [sem(f"rows_loaded{p}") for p in range(SETS)]
        nat_ready, maxed, max_turned, max_split = sem("nat_ready"), sem("maxed"), sem("max_turned"), sem("max_split")
        st_ready, exped, weighed, summed = sem("st_ready"), sem("exped"), sem("weighed"), sem("summed")
        set0_made = sem("set0_made")
        sums_copied, outs_copied, inverted, normalised = (sem("sums_copied"), sem("outs_copied"), sem("inverted"),
                                                          sem("normalised"))
        out_stored = [sem(f"out_stored{h}") for h in range(HALVES)]
        LOADS = 7
        CONSTS = 4 * (SETS - 1)

        def schedule(eng, body):
            body(0, 0, 0)
            with eng.Fori(0, (N - 4) // SETS) as j:
                body(j * 3 + 1, j, 1)
                body(j * 3 + 2, j, 2)
                body(j * 3 + 3, j + 1, 0)
            for n in range(N - 3, N):
                body(n, n // SETS, n % SETS)

        def after(n, m, p):
            return (n + 1, m, p + 1) if p < SETS - 1 else (n + 1, m + 1, 0)

        def is_last(n):
            return isinstance(n, int) and n == N - 1

        with nc.Block() as block:
            @block.sync
            def _(sp):
                def load(n, m, p):
                    if at_least(n, SETS):
                        wait_alone(sp, weighed, (n - 2) * NS, sp_passed)
                    heads = "(h r) t -> r h t"
                    for row, part in ((0, q_hi), (1, q_hi), (2, q_lo)):
                        sp.dma_start(qs[p][row * DH:(row + 1) * DH].bitcast(F32),
                                     part[n].rearrange(heads, r=DH)).then_inc(loaded[p], 16)
                    for row, part in ((0, k_hi), (1, k_lo), (2, k_hi)):
                        sp.dma_start(ks[p][row * DH:(row + 1) * DH].bitcast(F32),
                                     part[n].rearrange(heads, r=DH)).then_inc(loaded[p], 16)
                    sp.dma_start(vs[p][:], v[n].rearrange("k p c -> p k c")).then_inc(loaded[p], 16)

                def rows(n, m, p):
                    wait_alone(sp, max_split, (n + 1) * 2, sp_passed)
                    for row, part in ((MAX_HI_ROW, max_hi), (MAX_LO_ROW, max_lo)):
                        sp.dma_start(qs[p][row:row + 1].bitcast(F32), part[:].bitcast(F32)).then_inc(rows_loaded[p], 16)

                def store(n, h):
                    wait_alone(sp, normalised, (n * HALVES + h + 1) * 4, sp_passed)
                    sp.dma_start(out[n][:, h * TOK:(h + 1) * TOK], outs[:, h, :]).then_inc(out_stored[h], 16)

                for n in range(2):
                    load(n, 0, n)
                sp.wait_ge(set0_made, 4)
                rows(0, 0, 0)
                sp.wait_ge(consts_set, CONSTS)

                def body(n, m, p):
                    if not (isinstance(n, int) and n >= N - 2):
                        load(*after(*after(n, m, p)))
                    if at_least(n, 1):
                        store(n - 1, 1)
                    if not is_last(n):
                        rows(*after(n, m, p))
                    store(n, 0)
                schedule(sp, body)
                store(N - 1, 1)
                for h in range(HALVES):
                    sp.wait_ge(out_stored[h], 16 * N)

            @block.gpsimd
            def _(pool):
                pool.memset(ones[:], 1.0).then_inc(ones_set, 1)
                pool.wait_ge(ones_set, 1)
                for p in range(1, SETS):
                    pool.memset(ks[p][AUG:ROWS].bitcast(F32), 1.0).then_inc(consts_set, 1)
                    pool.memset(qs[p][AUG:ROWS].bitcast(F32), 0.0).then_inc(consts_set, 1)
                pool.wait_ge(consts_set, 2 * (SETS - 1))

                def body(n, m, p):
                    for k in pairs:
                        first = steps[k + 1][2]
                        pool.wait_ge(exped, n * NBLOCKS + (k + 2) * HG)
                        pool.wait_ge(weighed, n * NS + k + 1)
                        for j in range(HG):
                            here, there = (probs[:, (p * NS + i) % PR, j, first:TOK] for i in (k, k + 1))
                            last = pool.tensor_tensor(here, here, there, ALU.add)
                        last.then_inc(paired, 1)
                schedule(pool, body)

            @block.vector
            def _(dve):
                def mask_rows(p, made):
                    if causal:
                        row = keep[AUG:AUG + 1, :].unsqueeze(1).to_broadcast([1, HG, S])
                        dve.tensor_copy(qs[p][AUG:AUG + 1], row).then_inc(made, 1)
                        dve.tensor_scalar(ks[p][AUG:AUG + 1], row, -NEG, NEG, ALU.mult, ALU.add).then_inc(made, 1)
                    else:
                        dve.memset(ks[p][AUG:AUG + 1].bitcast(F32), 0.0).then_inc(made, 2)

                dve.memset(ks[0][AUG:ROWS].bitcast(F32), 1.0).then_inc(set0_made, 1)
                dve.memset(qs[0][AUG:ROWS].bitcast(F32), 0.0).then_inc(set0_made, 1)
                dve.wait_ge(set0_made, 2)
                mask_rows(0, set0_made)

                def maximum(n, u):
                    keys = ((u % KT) + 1) * P if causal else S
                    banks = 2 if keys > 512 else 1
                    dve.wait_ge(nat_ready, n * UNITS + u + 1)
                    if u == 0 and at_least(n, 1):
                        dve.wait_ge(max_turned, n)
                    dve.tensor_reduce(neg_max[:, u:u + 1], nat[:, bank_of[u]:bank_of[u] + banks, 0:keys // banks], AX.XY,
                                      ALU.max, negate=True).then_inc(maxed, 1)

                def split_max(n, before=None):
                    dve.wait_ge(max_turned, n + 1)
                    if before is not None:
                        dve.wait_ge(rows_loaded[before[2]], (before[1] + 1) * 32)
                    turned = nat[0:UNITS, TURN_BANK, 0:P]
                    dve.tensor_copy(max_hi[:], turned).then_inc(max_split, 1)
                    dve.wait_ge(max_split, n * 2 + 1)
                    dve.tensor_tensor(max_lo[:], turned, max_hi[:].bitcast(F32), ALU.subtract).then_inc(max_split, 1)

                def normalise(n, h, c):
                    cols = slice(c * CH, (c + 1) * CH)
                    done = (n * HALVES + h) * 4 + c
                    if c == 0:
                        dve.wait_ge(sums_copied, n * HALVES + h + 1)
                        dve.wait_ge(outs_copied, n * HALVES + h + 1)
                    dve.reciprocal(sums[:, h, cols], sums[:, h, cols]).then_inc(inverted, 1)
                    dve.wait_ge(inverted, done + 1)
                    dve.tensor_tensor(outs[:, h, cols], outs[:, h, cols], sums[:, h, cols],
                                      ALU.mult).then_inc(normalised, 1)

                for u in range(UNITS):
                    maximum(0, u)
                split_max(0)
                dve.wait_ge(consts_set, 2 * (SETS - 1))
                for p in range(1, SETS):
                    mask_rows(p, consts_set)
                for u in early_units:
                    maximum(1, u)

                def body(n, m, p):
                    nn = after(n, m, p)
                    for k, (h, t, _) in enumerate(steps):
                        for j in range(HG):
                            if k == TURN and j == TURN_HEAD and not is_last(n):
                                split_max(nn[0], (n, m, p))
                            if not is_last(n):
                                for u in next_units[k][j]:
                                    maximum(n + 1, u)
                            if not (isinstance(n, int) and n >= N - 2):
                                for u in later_units[k][j]:
                                    maximum(n + 2, u)
                            if j == HG // 2:
                                for c in range(4):
                                    for half, back in after_half(k, NORMALISE + c):
                                        if at_least(n, back):
                                            normalise(n - back, half, c)
                        if k == last_step[h]:
                            dve.wait_ge(weighed, n * NS + k + 1)
                            if at_least(n, 1):
                                dve.wait_ge(out_stored[h], n * 16)
                            dve.tensor_copy(outs[:, h, :], pv_ps[:]).then_inc(outs_copied, 1)
                schedule(dve, body)
                for c in range(4):
                    normalise(N - 1, 1, c)

            @block.scalar
            def _(act):
                def exponentials(n, p, k):
                    first = steps[k][2]
                    for j in range(HG):
                        blk = k * HG + j
                        act.wait_ge(st_ready, n * NBLOCKS + blk + 1)
                        if j == 0 and k >= PR:
                            act.wait_ge(summed, n * NS + (k - PR) // 2 * 2 + 2)
                        elif j == 0 and at_least(n, 1):
                            act.wait_ge(summed, (n - 1) * NS + (k - PR + NS) // 2 * 2 + 2)
                        act.activation(probs[:, (p * NS + k) % PR, j, first:TOK], st_ps[:, blk % 2, first:TOK],
                                       ACT.Exp).then_inc(exped, 1)

                def copy_sums(n, h):
                    act.wait_ge(summed, n * NS + last_step[h] + 1)
                    if at_least(n, 1):
                        act.wait_ge(normalised, ((n - 1) * HALVES + h + 1) * 4)
                    act.copy(sums[:, h, :], sum_ps[:]).then_inc(sums_copied, 1)

                exponentials(0, 0, 0)

                def body(n, m, p):
                    nn = after(n, m, p)
                    for k, (h, t, _) in enumerate(steps):
                        if k + 1 < NS:
                            exponentials(n, p, k + 1)
                        elif not is_last(n):
                            exponentials(nn[0], nn[2], 0)
                        for half, back in after_half(k, COPY):
                            if at_least(n, back):
                                copy_sums(n - back, half)
                schedule(act, body)
                copy_sums(N - 1, HALVES - 1)

            @block.tensor
            def _(pe):
                def max_scores(n, m, p, u):
                    j, t = divmod(u, KT)
                    keys = (t + 1) * P if causal else S
                    banks = 2 if keys > 512 else 1
                    width = keys // banks
                    rows = AUG + 1 if causal else AUG
                    if u == 0:
                        pe.wait_ge(loaded[p], (m + 1) * LOADS * 16)
                        if at_least(n, 1):
                            pe.wait_ge(max_turned, n)
                    if bank_of[u] == TURN_BANK and u <= TURN_BANK and at_least(n, 1):
                        pe.wait_ge(max_split, n * 2)
                    if u >= reach[u] or at_least(n, 1):
                        pe.wait_ge(maxed, n * UNITS + u + 1 - reach[u])
                    for bank in range(banks):
                        cols = max(width, 256)
                        diagonal = causal and bank == banks - 1
                        last = pe.matmul(nat[:, bank_of[u] + bank, 0:cols], qs[p][0:rows, j, t * P:(t + 1) * P],
                                         ks[p][0:rows, j, bank * width:bank * width + cols], start=True,
                                         stop=not diagonal)
                        if diagonal:
                            last = pe.matmul(nat[:, bank_of[u] + bank, width - P:width], ident_bf[:], mask_qk[:],
                                             start=False, stop=True)
                    last.then_inc(nat_ready, 1)

                def turn_max(n):
                    pe.wait_ge(maxed, (n + 1) * UNITS)
                    pe.transpose(nat[0:UNITS, TURN_BANK, 0:P], neg_max[:], ident[:]).then_inc(max_turned, 1)

                def scores(n, m, p, k, j):
                    h, t, first = steps[k]
                    blk = k * HG + j
                    if k == 0 and j == 0:
                        pe.wait_ge(rows_loaded[p], (m + 1) * 32)
                    if blk >= 2 or at_least(n, 1):
                        pe.wait_ge(exped, n * NBLOCKS + blk - 1)
                    lo = min(first, TOK - 256)
                    diagonal = causal and t * P >= h * TOK
                    last = pe.matmul(st_ps[:, blk % 2, lo:TOK], ks[p][0:ROWS, j, t * P:(t + 1) * P],
                                     qs[p][0:ROWS, j, h * TOK + lo:(h + 1) * TOK], start=True,
                                     stop=not diagonal)
                    if diagonal:
                        last = pe.matmul(st_ps[:, blk % 2, first:first + P], ident_bf[:], mask_kq[:],
                                         start=False, stop=True)
                    last.then_inc(st_ready, 1)

                def weigh(n, p, k):
                    h, t, first = steps[k]
                    pe.wait_ge(exped, n * NBLOCKS + (k + 1) * HG)
                    if t == 0 and (h or at_least(n, 1)):
                        pe.wait_ge(outs_copied, n * HALVES + h)
                    for j in range(HG):
                        last = pe.matmul(pv_ps[j * DH:(j + 1) * DH, first:TOK], vs[p][:, t, j * DH:(j + 1) * DH],
                                         probs[:, (p * NS + k) % PR, j, first:TOK],
                                         start=(t == 0), stop=(k == last_step[h]), skip_group_check=True)
                    last.then_inc(weighed, 1)

                def sum_up(n, p, i, c):
                    h, t, first = steps[i]
                    if c == 0:
                        pe.wait_ge(paired, n * NP + i // 2 + 1)
                        if t == 0 and (h or at_least(n, 1)):
                            pe.wait_ge(sums_copied, n * HALVES + h)
                    mid = (first + TOK) // 2
                    cols = slice(first, mid) if c == 0 else slice(mid, TOK)
                    for j in range(HG):
                        last = pe.matmul(sum_ps[j * DH:(j + 1) * DH, cols], ones[:],
                                         probs[:, (p * NS + i) % PR, j, cols], start=(t == 0 and c == 0),
                                         stop=(i + 1 == last_step[h]), skip_group_check=True)
                    last.then_inc(summed, 1)

                pe.wait_ge(set0_made, 4)
                for u in range(UNITS):
                    max_scores(0, 0, 0, u)
                turn_max(0)
                pe.wait_ge(ones_set, 1)
                pe.wait_ge(consts_set, CONSTS)
                for u in early_units:
                    max_scores(1, 0, 1, u)
                for j in range(HG):
                    scores(0, 0, 0, 0, j)

                def body(n, m, p):
                    nn = after(n, m, p)
                    for k in range(NS):
                        following = (n, m, p, k + 1) if k + 1 < NS else None if is_last(n) else (*nn, 0)
                        for j in range(HG):
                            if following:
                                scores(*following, j)
                            if k == TURN and j == TURN_HEAD and not is_last(n):
                                turn_max(nn[0])
                            if not is_last(n):
                                for u in next_units[k][j]:
                                    max_scores(*nn, u)
                            if not (isinstance(n, int) and n >= N - 2):
                                for u in later_units[k][j]:
                                    max_scores(*after(*nn), u)
                            if j == 1:
                                weigh(n, p, k)
                            if j == HG - 1:
                                for back, i, c in summing[k]:
                                    if at_least(n, back):
                                        sum_up(n - back, p - back, i, c)
                schedule(pe, body)
                for k in range(NS):
                    for back, i, c in summing[k]:
                        if back:
                            sum_up(N - 1, (N - 1) % SETS, i, c)
        sem.clear()


def mlp_stage(nc, xt_hi, xt_lo, x_src, w1, b1, w2, b2, out):
    NC = FF // P
    LAG, RING = 2, 4
    with ExitStack() as ctx:
        sb = lambda name, shape, dt=F32: ctx.enter_context(nc.sbuf_tensor("m_" + name, shape, dt))
        sem = Semaphores(nc, ctx, "m_")
        w1_hi = sb("w1_hi", [P, NC, KC, P], F32R)
        w1_lo = sb("w1_lo", [P, NC, KC, P], F32R)
        w2_hi = sb("w2_hi", [P, NC, D], F32R)
        w2_lo = sb("w2_lo", [P, NC, D], F32R)
        raw = sb("raw", [P, 4, D])
        x_hi = sb("x_hi", [P, KC, TOK], F32R)
        x_lo = sb("x_lo", [P, KC, TOK], F32R)
        x = sb("x", [P, SUB, D])
        b1_sb = sb("b1", [P, NC])
        b2_sb = sb("b2", [P, D])
        hid = sb("hid", [P, RING, TOK])
        hid_hi = sb("hid_hi", [P, RING, TOK], F32R)
        hid_lo = sb("hid_lo", [P, RING, TOK], F32R)
        h_ps = ctx.enter_context(nc.psum_tensor("m_h_ps", [P, RING, 512], F32))
        o_ps = ctx.enter_context(nc.psum_tensor("m_o_ps", [P, SUB, 512], F32))
        sp_passed = sem("sp_passed")
        raw_loaded = [sem(f"raw_loaded{k}") for k in range(4)]
        small_loaded, w_hi_done, w_lo_done = sem("small_loaded"), sem("w_hi_done"), sem("w_lo_done")
        xt_loaded, x_loaded, biased = sem("xt_loaded"), sem("x_loaded"), sem("biased")
        h_filled, relu_done, hid_hi_done, hid_lo_done = (sem("h_filled"), sem("relu_done"), sem("hid_hi_done"),
                                                         sem("hid_lo_done"))
        multiplied, summed, stored = sem("multiplied"), sem("summed"), sem("stored")
        pieces = []
        for c in range(NC):
            pieces.append((w1.rearrange("(k p) f -> p k f", p=P)[:, :, c * P:(c + 1) * P],
                           w1_hi[:, c].rearrange("p k f -> p (k f)"), w1_lo[:, c].rearrange("p k f -> p (k f)")))
            pieces.append((w2[c * P:(c + 1) * P, :], w2_hi[:, c, :], w2_lo[:, c, :]))
        AHEAD = 3

        with nc.Block() as block:
            @block.sync
            def _(sp):
                def load(u):
                    if u >= 4:
                        sp.wait_ge(w_lo_done, u - 3)
                    dst = raw[:, u % 4, :]
                    if u % 2 == 0:
                        dst = dst.rearrange("p (k f) -> p k f", k=KC)
                    sp.dma_start(dst, pieces[u][0]).then_inc(raw_loaded[u % 4], 16)

                def load_xt(i, b, s):
                    if at_least(i, 1):
                        wait_alone(sp, h_filled, i * NC, sp_passed)
                    sp.dma_start(x_hi[:].bitcast(F32), xt_hi[b, s]).then_inc(xt_loaded, 16)
                    sp.dma_start(x_lo[:].bitcast(F32), xt_lo[b, s]).then_inc(xt_loaded, 16)

                def load_x(i, b, s):
                    if at_least(i, 1):
                        wait_alone(sp, stored, i * 16, sp_passed)
                    sp.dma_start(x[:], x_src[b, s]).then_inc(x_loaded, 16)

                def store(i, b, s):
                    wait_alone(sp, summed, (i + 1) * SUB, sp_passed)
                    sp.dma_start(out[b, s], x[:]).then_inc(stored, 16)

                load_xt(0, 0, 0)
                sp.dma_start(b1_sb[:], b1).then_inc(small_loaded, 16)
                for u in range(4):
                    load(u)
                sp.dma_start(b2_sb[:], b2.partition_broadcast(P)).then_inc(small_loaded, 16)
                load_x(0, 0, 0)
                for u in range(4, len(pieces)):
                    load(u)

                def body(i, b, s):
                    if isinstance(i, int) and i == TILES - 1:
                        return
                    load_xt(*nxt(i, b, s))
                    store(i, b, s)
                    load_x(*nxt(i, b, s))
                on_tiles(sp, body)
                store(TILES - 1, B - 1, 1)
                sp.wait_ge(stored, 16 * TILES)

            @block.scalar
            def _(act):
                def split(u):
                    act.wait_ge(raw_loaded[u % 4], 16 * (u // 4 + 1))
                    act.copy(pieces[u][1], raw[:, u % 4, :]).then_inc(w_hi_done, 1)

                for u in range(2 * AHEAD):
                    split(u)
                act.wait_ge(small_loaded, 32)

                def body(i, b, s):
                    for c in range(NC):
                        if isinstance(i, int) and i == 0 and c + AHEAD < NC:
                            split(2 * (c + AHEAD))
                            split(2 * (c + AHEAD) + 1)
                        act.wait_ge(h_filled, i * NC + c + 1)
                        if c >= RING or at_least(i, 1):
                            act.wait_ge(hid_lo_done, i * NC + c - RING + 1)
                        act.activation(hid[:, c % RING, :], h_ps[:, c % RING, :], ACT.Relu,
                                       bias=b1_sb[:, c:c + 1]).then_inc(relu_done, 1)
                on_tiles(act, body)

            @block.gpsimd
            def _(pool):
                def split(u):
                    pool.wait_ge(w_hi_done, u + 1)
                    pool.tensor_tensor(pieces[u][2], raw[:, u % 4, :], pieces[u][1].bitcast(F32),
                                       ALU.subtract).then_inc(w_lo_done, 1)

                for u in range(2 * AHEAD):
                    split(u)
                pool.wait_ge(small_loaded, 32)

                def body(i, b, s):
                    for c in range(NC):
                        if isinstance(i, int) and i == 0 and c + AHEAD < NC:
                            split(2 * (c + AHEAD))
                            split(2 * (c + AHEAD) + 1)
                        if 8 <= c < 8 + SUB:
                            u = c - 8
                            pool.wait_ge(x_loaded, (i + 1) * 16)
                            pool.tensor_tensor(x[:, u, :], x[:, u, :], b2_sb[:], ALU.add).then_inc(biased, 1)
                        pool.wait_ge(hid_hi_done, i * NC + c + 1)
                        if c >= RING or at_least(i, 1):
                            pool.wait_ge(multiplied, i * NC + c - RING + 1)
                        pool.tensor_tensor(hid_lo[:, c % RING, :], hid[:, c % RING, :],
                                           hid_hi[:, c % RING, :].bitcast(F32), ALU.subtract).then_inc(hid_lo_done, 1)
                on_tiles(pool, body)

            @block.vector
            def _(dve):
                def finish(i):
                    dve.wait_ge(multiplied, (i + 1) * NC)
                    dve.wait_ge(biased, (i + 1) * SUB)
                    for u in range(SUB):
                        dve.tensor_tensor(x[:, u, :], o_ps[:, u, :], x[:, u, :], ALU.add).then_inc(summed, 1)

                def body(i, b, s):
                    for c in range(NC):
                        dve.wait_ge(relu_done, i * NC + c + 1)
                        if c >= RING or at_least(i, 1):
                            dve.wait_ge(multiplied, i * NC + c - RING + 1)
                            dve.wait_ge(hid_lo_done, i * NC + c - RING + 1)
                        dve.tensor_copy(hid_hi[:, c % RING, :], hid[:, c % RING, :]).then_inc(hid_hi_done, 1)
                        if c == LAG - 1 and at_least(i, 1):
                            finish(i - 1)
                on_tiles(dve, body)
                finish(TILES - 1)

            @block.tensor
            def _(pe):
                def hidden(i, c):
                    if isinstance(i, int) and i == 0:
                        pe.wait_ge(w_lo_done, 2 * c + 1)
                    if c == 0:
                        pe.wait_ge(xt_loaded, (i + 1) * 32)
                    if c >= RING or at_least(i, 1):
                        pe.wait_ge(relu_done, i * NC + c - RING + 1)
                    three(pe, h_ps[:, c % RING, :],
                          [(w1_hi[:, c, k, :], w1_lo[:, c, k, :], x_hi[:, k, :], x_lo[:, k, :])
                           for k in range(KC)], True, True).then_inc(h_filled, 1)

                def multiply(i, c):
                    if isinstance(i, int) and i == 0:
                        pe.wait_ge(w_lo_done, 2 * c + 2)
                    pe.wait_ge(hid_lo_done, i * NC + c + 1)
                    if c == 0 and at_least(i, 1):
                        pe.wait_ge(summed, i * SUB)
                    for u in range(SUB):
                        cols = slice(u * P, (u + 1) * P)
                        last = three(pe, o_ps[:, u, :],
                                     [(hid_hi[:, c % RING, cols], hid_lo[:, c % RING, cols], w2_hi[:, c, :],
                                       w2_lo[:, c, :])], c == 0, c == NC - 1)
                    last.then_inc(multiplied, 1)

                def body(i, b, s):
                    for c in range(NC):
                        hidden(i, c)
                        if c >= LAG:
                            multiply(i, c - LAG)
                        elif at_least(i, 1):
                            multiply(i - 1, NC - LAG + c)
                on_tiles(pe, body)
                for c in range(NC - LAG, NC):
                    multiply(TILES - 1, c)
        sem.clear()


def layer(nc, a, y):
    def dram(name, shape):
        return nc.dram_tensor(name, shape, F32, kind="Internal").ap()

    def tokens(t):
        return t.rearrange("b (s u p) d -> b s p u d", s=HALVES, p=P)

    qk = {n: dram(n, [B, D, S]) for n in ("sq_hi", "sq_lo", "sk_hi", "sk_lo", "cq_hi", "cq_lo", "ck_hi", "ck_lo")}
    vals = {n: dram(n, [B, NG, KT, P, P]) for n in ("sv", "cv")}
    att = {n: dram(n, [B, D, S]) for n in ("s_att", "c_att")}
    x1, x2 = dram("x1", [B, S, D]), dram("x2", [B, S, D])
    xt_hi, xt_lo = dram("xt_hi", [B, HALVES, P, KC, TOK]), dram("xt_lo", [B, HALVES, P, KC, TOK])

    def chan_home(t, m):
        return t.rearrange("b (c p) (s t) -> c b s p t", p=P, s=HALVES)[m]

    def by_group(t):
        return t.rearrange("b (g p) t -> (b g) p t", p=P)

    def tok_home(t):
        return t.rearrange("b g (s u) p c -> b s g p u c", s=HALVES)

    def att_home(t):
        return t.rearrange("b (c p) (s t) -> b s p c t", p=P, s=HALVES)

    with ExitStack() as ctx:
        sb = lambda name, shape, dt=F32: ctx.enter_context(nc.sbuf_tensor(name, shape, dt))
        ident, ident_bf = sb("ident", [P, P]), sb("ident_bf", [P, P], BF16)
        mask_qk, mask_kq = sb("mask_qk", [P, P], BF16), sb("mask_kq", [P, P], BF16)
        keep = sb("keep", [P, S])
        q_bias, k_bias = sb("q_bias", [P, KC]), sb("k_bias", [P, KC])
        made, biases_loaded = (ctx.enter_context(nc.semaphore(n)) for n in ("made", "biases_loaded"))
        with nc.Block() as block:
            @block.gpsimd
            def _(pool):
                tiles = ((ident, 0.0, ALU.not_equal, 1.0, 1, -1), (ident_bf, 0.0, ALU.not_equal, 1.0, 1, -1),
                         (mask_qk, 0.0, ALU.is_ge, CAUSAL, 1, -1), (mask_kq, 0.0, ALU.is_ge, CAUSAL, -1, 1))
                for t, value, *_ in tiles:
                    pool.memset(t[:], value).then_inc(made, 1)
                pool.wait_ge(made, len(tiles))
                for t, _, op, fill, row, col in tiles:
                    pool.affine_select(out=t[:], in_=t[:], compare_op=op, fill=fill, base=0,
                                       pattern=[[col, P]], channel_multiplier=row).then_inc(made, 1)
                pool.wait_ge(made, 2 * len(tiles))

            @block.sync
            def _(sp):
                sp.dma_start(q_bias[:], a["ca_q_b"]).then_inc(biases_loaded, 16)
                sp.dma_start(k_bias[:], a["ca_k_b"]).then_inc(biases_loaded, 16)
                sp.wait_ge(biases_loaded, 32)

        router_stage(nc, keep, tokens(a["x"]), a["n1_g"], a["n1_b"], a["qkv_w"][:, D:2 * D], a["r_w1"],
                     a["r_b1"], a["r_w2"], a["r_b2"])

        self_scale, cross_scale = float(D) ** -0.5, float(DH) ** -0.5

        def self_q(dve, out, psum, s):
            return dve.scalar_tensor_tensor(out=out, in0=psum, scalar=self_scale, in1=keep[:, s * TOK:(s + 1) * TOK],
                                            op0=ALU.mult, op1=ALU.mult)

        def self_k(dve, out, psum, s):
            return dve.tensor_tensor(out, psum, keep[:, s * TOK:(s + 1) * TOK], ALU.mult)

        def cross_q(m):
            return lambda dve, out, psum, s: dve.tensor_scalar(out, psum, q_bias[:, m:m + 1], cross_scale,
                                                               ALU.add, ALU.mult)

        def cross_k(m):
            return lambda dve, out, psum, s: dve.tensor_scalar(out, psum, k_bias[:, m:m + 1], None, ALU.add)

        third = lambda w, n: w[:, n * D:(n + 1) * D]
        projection_stage(
            nc, "a_", ident, tokens(a["x"]), norm=(a["n1_g"], a["n1_b"]),
            weights=[third(a["qkv_w"], n) for n in range(3)],
            chans=[(m, self_q, chan_home(qk["sq_hi"], m), chan_home(qk["sq_lo"], m)) for m in range(KC)]
            + [(KC + m, self_k, chan_home(qk["sk_hi"], m), chan_home(qk["sk_lo"], m)) for m in range(KC)],
            toks=(2, None, tok_home(vals["sv"])))
        attention_stage(nc, "b_", ident, *(by_group(qk[n]) for n in ("sq_hi", "sq_lo", "sk_hi", "sk_lo")),
                        vals["sv"].rearrange("b g k p c -> (b g) k p c"), by_group(att["s_att"]),
                        keep, mask_qk, mask_kq, ident_bf)
        projection_stage(
            nc, "d_", ident, tokens(a["ctx"]), weights=[third(a["ca_in_w"], n) for n in (1, 2)],
            chans=[(m, cross_k(m), chan_home(qk["ck_hi"], m), chan_home(qk["ck_lo"], m)) for m in range(KC)],
            toks=(1, a["ca_v_b"], tok_home(vals["cv"])))
        projection_stage(
            nc, "c_", ident, tokens(a["x"]), mix=(att_home(att["s_att"]), a["sa_out_w"], a["sa_out_b"], tokens(x1)),
            norm=(a["n2_g"], a["n2_b"]), weights=[third(a["ca_in_w"], 0)],
            chans=[(m, cross_q(m), chan_home(qk["cq_hi"], m), chan_home(qk["cq_lo"], m)) for m in range(KC)])
        attention_stage(nc, "e_", ident, *(by_group(qk[n]) for n in ("cq_hi", "cq_lo", "ck_hi", "ck_lo")),
                        vals["cv"].rearrange("b g k p c -> (b g) k p c"), by_group(att["c_att"]))
        projection_stage(
            nc, "f_", ident, tokens(x1), mix=(att_home(att["c_att"]), a["ca_out_w"], a["ca_out_b"], tokens(x2)),
            norm=(a["n3_g"], a["n3_b"]), keep_xt=(xt_hi, xt_lo))
        mlp_stage(nc, xt_hi, xt_lo, tokens(x2), a["ff_w1"], a["ff_b1"], a["ff_w2"], a["ff_b2"], tokens(y))


def kernel(**inputs):
    import numpy as np
    from concourse import bacc
    from concourse.bass_utils import run_bass_kernel_spmd

    given = {n.removeprefix("L0_xattn_"): np.asarray(v) for n, v in inputs.items()}
    columns = lambda v: np.ascontiguousarray(v.reshape(-1, P).T)
    turned = lambda w: np.ascontiguousarray(w.T)
    ca_b = given["ca_in_b"]
    arrays = {
        "x": given["x"], "ctx": given["ctx_1024"],
        "qkv_w": turned(given["qkv_w"]), "sa_out_w": turned(given["sa_out_w"]), "sa_out_b": given["sa_out_b"],
        "r_w1": turned(given["r_w1"]), "r_b1": columns(given["r_b1"]), "r_w2": turned(given["r_w2"]),
        "r_b2": given["r_b2"],
        "ca_in_w": turned(given["ca_in_w"]), "ca_q_b": columns(ca_b[0:D]), "ca_k_b": columns(ca_b[D:2 * D]),
        "ca_v_b": np.ascontiguousarray(ca_b[2 * D:]), "ca_out_w": turned(given["ca_out_w"]),
        "ca_out_b": given["ca_out_b"],
        "ff_w1": turned(given["ff_w1"]), "ff_b1": columns(given["ff_b1"]), "ff_w2": turned(given["ff_w2"]),
        "ff_b2": given["ff_b2"],
        **{f"n{n}_{c}": columns(given[f"n{n}_{c}"]) for n in (1, 2, 3) for c in "gb"},
    }
    nc = bacc.Bacc("TRN2", target_bir_lowering=False, num_devices=1)
    feeds, aps = {}, {}
    for name, v in arrays.items():
        v = np.ascontiguousarray(v)
        feeds[f"in_{name}"] = v
        aps[name] = nc.dram_tensor(f"in_{name}", v.shape, mybir.dt.from_np(v.dtype), kind="ExternalInput").ap()
    y = nc.dram_tensor("out_y", (B, S, D), F32, kind="ExternalOutput").ap()
    layer(nc, aps, y)
    r = run_bass_kernel_spmd(nc, [feeds], core_ids=[0])
    return r.results[0]["out_y"]
```

```python
from contextlib import ExitStack

import concourse.bass as bass
from concourse import mybir

ALU = mybir.AluOpType
ACT = mybir.ActivationFunctionType
AX = mybir.AxisListType
F32 = mybir.dt.float32
F32R = mybir.dt.float32r
BF16 = mybir.dt.bfloat16

P = 128
B, S, D = 4, 1024, 512
H, DH = 16, 32
HG = P // DH
NG = H // HG
FF = 2048
BLOCK = 64
NBLK = S // BLOCK
TOK = 512
SUB = TOK // P
HALVES = S // TOK
TILES = B * HALVES
KC = D // P
KT = S // P
NEG = -1.0e9
CAUSAL = -1.0e30
EPS = 1e-5
AUG = 3 * DH
MASK_ROW, MAX_HI_ROW, MAX_LO_ROW = AUG, AUG + 1, AUG + 2
ROWS = AUG + 3


def on_tiles(eng, body, between=lambda tile: None):
    body(0, 0, 0)
    between(1)
    with eng.Fori(0, B - 2) as j:
        body(j * 2 + 1, j, 1)
        body(j * 2 + 2, j + 1, 0)
    for i in range(TILES - 3, TILES):
        between(i)
        body(i, i // HALVES, i % HALVES)


def nxt(i, b, s):
    return (i + 1, b, 1) if s == 0 else (i + 1, b + 1, 0)


def at_least(i, n):
    return i >= n if isinstance(i, int) else True


def wait_alone(eng, sem, value, passed):
    eng.wait_ge(sem, value)
    eng.sem_inc(passed, 1)


class Semaphores:

    def __init__(self, nc, ctx, tag):
        self.nc, self.ctx, self.tag, self.all = nc, ctx, tag, []

    def __call__(self, name):
        self.all.append(self.ctx.enter_context(self.nc.semaphore(self.tag + name)))
        return self.all[-1]

    def clear(self):
        numbers = sorted(s.num for s in self.all)
        starts = [n for n in numbers if n - 1 not in numbers]
        with self.nc.Block() as block:
            @block.sync
            def _(sp):
                for start in starts:
                    end = start
                    while end in numbers:
                        end += 1
                    sp.sem_clear(range(start, end))


def three(pe, out, pairs, start, stop):
    last = None
    for n, (wh, wl, xh, xl) in enumerate(pairs):
        for m, (w, x) in enumerate(((wh, xh), (wh, xl), (wl, xh))):
            last = pe.matmul(out, w, x, start=(start and n == 0 and m == 0),
                             stop=(stop and n == len(pairs) - 1 and m == 2))
    return last


class Router:

    def __init__(self, nc, keep, x_tiles, ln_g, ln_b, wk, r_w1, r_b1, r_w2, r_b2):
        self.nc, self.keep = nc, keep
        self.sources = (x_tiles, ln_g, ln_b, wk, r_w1, r_b1, r_w2, r_b2)

    def place(self, ctx, sem):
        sb = lambda name, shape, dt=F32: ctx.enter_context(self.nc.sbuf_tensor("r_" + name, shape, dt))
        self.x = sb("x", [P, HALVES * SUB, D])
        self.wk = sb("wk", [P, KC, D])
        self.w1 = sb("w1", [P, KC, P])
        self.w2 = sb("w2", [P, 1])
        self.w2_all = sb("w2_all", [P, P])
        self.gb = sb("gb", [P, 2, KC])
        self.b1 = sb("b1", [P, 1])
        self.b2 = sb("b2", [P, 1])
        self.stats = sb("stats", [P, KT, 6])
        self.mv = sb("mv", [P, KT, 2])
        self.var = sb("var", [P, KT])
        self.rstd = sb("rstd", [P, KT])
        self.power = sb("power", [P, KT])
        self.averager = sb("averager", [P, 2])
        self.means = sb("means", [P, KC, NBLK])
        self.key_means = sb("key_means", [P, KC, NBLK])
        self.hidden = sb("hidden", [P, NBLK])
        self.kept = sb("kept", [P, NBLK])
        ps = ctx.enter_context(self.nc.psum_tensor("r_ps", [P, 2, 512], F32))
        self.means_ps, self.keys_ps = ps[:, 0, 0:KC * NBLK], ps[:, 1, 0:KC * NBLK]
        self.hidden_ps, self.logits_ps = ps[:, 0, 256:256 + NBLK], ps[:, 1, 256:256 + NBLK]
        self.loaded_x, self.loaded_w, self.loaded_small = (sem("r_loaded_x"), sem("r_loaded_w"),
                                                           sem("r_loaded_small"))
        self.consts, self.v_step, self.aggregated = sem("r_consts"), sem("r_v_step"), sem("r_aggregated")
        self.rstd_ready, self.normed, self.meaned = sem("r_rstd_ready"), sem("r_normed"), sem("r_meaned")
        self.scaled, self.keyed, self.keys_copied = sem("r_scaled"), sem("r_keyed"), sem("r_keys_copied")
        self.hid_ready, self.relu_done, self.logits = sem("r_hid_ready"), sem("r_relu_done"), sem("r_logits")

    def load(self, sp):
        x_tiles, ln_g, ln_b, wk, r_w1, r_b1, r_w2, r_b2 = self.sources
        for s in range(HALVES):
            sp.dma_start(self.x[:, s * SUB:(s + 1) * SUB, :], x_tiles[0, s]).then_inc(self.loaded_x, 16)
        for dst, src in ((self.gb[:, 0, :], ln_g), (self.gb[:, 1, :], ln_b), (self.b1[:], r_b1),
                         (self.b2[:], r_b2.partition_broadcast(P)), (self.w2[:], r_w2)):
            sp.dma_start(dst, src).then_inc(self.loaded_small, 16)
        sp.dma_start(self.wk[:], wk.rearrange("(c p) n -> p c n", p=P)).then_inc(self.loaded_w, 16)
        sp.dma_start(self.w1[:], r_w1.rearrange("(c p) n -> p c n", p=P)).then_inc(self.loaded_w, 16)

    def constants(self, pool):
        pool.memset(self.averager[:], 0.0).then_inc(self.consts, 1)
        pool.memset(self.power[:], -0.5).then_inc(self.consts, 1)
        pool.wait_ge(self.consts, 2)
        for h in range(2):
            pool.memset(self.averager[h * BLOCK:(h + 1) * BLOCK, h:h + 1], 1.0 / BLOCK).then_inc(self.consts, 1)
        pool.wait_ge(self.consts, 4)

    def pool_step(self, pool, step):
        if step == 1:
            pool.wait_ge(self.v_step, 2)
            pool.tensor_tensor(self.rstd[:], self.var[:], self.power[:], ALU.pow).then_inc(self.rstd_ready, 1)

    def vector_step(self, dve, step):
        if step == 1:
            dve.wait_ge(self.loaded_x, 16 * HALVES)
            for t in range(KT):
                last = dve.bn_stats(self.stats[:, t, :], self.x[:, t, :])
            last.then_inc(self.v_step, 1)
            dve.wait_ge(self.v_step, 1)
            for t in range(KT):
                last = dve.bn_aggr(self.mv[:, t, :], self.stats[:, t, :])
            last.then_inc(self.aggregated, 1)
            dve.wait_ge(self.aggregated, 1)
            dve.tensor_scalar_add(self.var[:], self.mv[:, :, 1], EPS).then_inc(self.v_step, 1)
        elif step == TILES - 3:
            dve.wait_ge(self.rstd_ready, 1)
            for t in range(KT):
                last = dve.tensor_scalar(self.x[:, t, :], self.x[:, t, :], self.mv[:, t, 0:1],
                                         self.rstd[:, t:t + 1], ALU.subtract, ALU.mult)
            last.then_inc(self.normed, 1)
            dve.wait_ge(self.loaded_small, 16 * 5)
            dve.tensor_copy(self.w2_all[:], self.w2[:, 0:1].to_broadcast([P, P])).then_inc(self.v_step, 1)
        elif step == TILES - 1:
            dve.wait_ge(self.meaned, 1)
            for c in range(KC):
                last = dve.tensor_scalar(self.means[:, c, :], self.means_ps[:, c * NBLK:(c + 1) * NBLK],
                                         self.gb[:, 0, c:c + 1], self.gb[:, 1, c:c + 1], ALU.mult, ALU.add)
            last.then_inc(self.scaled, 1)
            dve.wait_ge(self.keyed, 1)
            dve.tensor_copy(self.key_means[:].rearrange("p c n -> p (c n)"), self.keys_ps).then_inc(self.keys_copied, 1)
            dve.wait_ge(self.hid_ready, 1)
            dve.tensor_scalar(self.hidden[:], self.hidden_ps, self.b1[:, 0:1], 0.0, ALU.add,
                              ALU.max).then_inc(self.relu_done, 1)
        elif step == TILES:
            dve.wait_ge(self.logits, 1)
            dve.tensor_scalar(self.kept[:], self.logits_ps, self.b2[:, 0:1], 0.0, ALU.add,
                              ALU.is_gt).then_inc(self.v_step, 1)
            dve.wait_ge(self.v_step, 4)
            dve.tensor_copy(self.keep[:].rearrange("p (n t) -> p n t", t=BLOCK),
                            self.kept[:].unsqueeze(2).to_broadcast([P, NBLK, BLOCK])).then_inc(self.v_step, 1)
            dve.wait_ge(self.v_step, 5)

    def tensor_step(self, pe, step):
        if step == TILES - 2:
            pe.wait_ge(self.consts, 4)
            pe.wait_ge(self.normed, 1)
            for t in range(KT):
                for c in range(KC):
                    last = pe.matmul(self.means_ps[:, c * NBLK + 2 * t:c * NBLK + 2 * t + 2],
                                     self.x[:, t, c * P:(c + 1) * P], self.averager[:], start=True, stop=True)
            last.then_inc(self.meaned, 1)
        elif step == TILES - 1:
            pe.wait_ge(self.loaded_w, 16 * 2)
            pe.wait_ge(self.scaled, 1)
            for m in range(KC):
                for c in range(KC):
                    last = pe.matmul(self.keys_ps[:, m * NBLK:(m + 1) * NBLK], self.wk[:, c, m * P:(m + 1) * P],
                                     self.means[:, c, :], start=(c == 0), stop=(c == KC - 1))
            last.then_inc(self.keyed, 1)
            pe.wait_ge(self.keys_copied, 1)
            for c in range(KC):
                last = pe.matmul(self.hidden_ps, self.w1[:, c, :], self.key_means[:, c, :],
                                 start=(c == 0), stop=(c == KC - 1))
            last.then_inc(self.hid_ready, 1)
        elif step == TILES:
            pe.wait_ge(self.v_step, 3)
            pe.wait_ge(self.relu_done, 1)
            pe.matmul(self.logits_ps, self.w2_all[:], self.hidden[:], start=True, stop=True).then_inc(self.logits, 1)


def projection_stage(nc, tag, ident, src, mix=None, norm=None, weights=(), chans=(), toks=None,
                     keep_xt=None, router=None):
    RING = 4
    has_mix = mix is not None
    n_mix, n_chan, n_tok = (SUB if has_mix else 0), len(chans), (SUB if toks else 0)
    per_tile = n_mix + n_chan + n_tok
    work = [("chan", k) for k in range(n_chan)] + [("tok", k) for k in range(n_tok)]
    assert n_chan % RING == 0 and n_tok % RING == 0

    def mix_seq(i, k):
        if isinstance(i, int) and i < 2:
            return i * n_mix + k
        return 2 * n_mix + (i - 2) * per_tile + k

    def work_seq(i, k):
        if isinstance(i, int) and i >= TILES - 2:
            return 2 * n_mix + (TILES - 2) * per_tile + (i - TILES + 2) * len(work) + k
        return 2 * n_mix + i * per_tile + n_mix + k

    with ExitStack() as ctx:
        sb = lambda name, shape, dt=F32: ctx.enter_context(nc.sbuf_tensor(tag + name, shape, dt))
        sem = Semaphores(nc, ctx, tag)
        n_w = len(weights)
        w_hi = sb("w_hi", [P, max(n_w, 1), KC, D], F32R) if n_w else None
        w_lo = sb("w_lo", [P, max(n_w, 1), KC, D], F32R) if n_w else None
        raw = sb("raw", [P, 4, D])
        x = sb("x", [P, 2, SUB, D])
        x_hi = sb("x_hi", [P, 2, KC, TOK], F32R)
        x_lo = sb("x_lo", [P, 2, KC, TOK], F32R)
        xt = sb("xt", [P, KC, TOK])
        tr = ctx.enter_context(nc.psum_tensor(tag + "tr", [P, 2, TOK], F32))
        ring = ctx.enter_context(nc.psum_tensor(tag + "ring", [P, RING, 512], F32))
        if norm:
            xn = sb("xn", [P, 2, SUB, D])
            stats = sb("stats", [P, SUB, 6])
            mv = sb("mv", [P, SUB, 2])
            var = sb("var", [P, SUB])
            rstd = sb("rstd", [P, SUB])
            power = sb("power", [P, SUB])
            gb = sb("gb", [P, 2, KC])
        if has_mix:
            o = sb("o", [P, 2, KC, TOK])
            o_hi = sb("o_hi", [P, 2, KC, TOK], F32R)
            o_lo = sb("o_lo", [P, 2, KC, TOK], F32R)
            o_bias = sb("o_bias", [P, D])
            ow_hi = sb("ow_hi", [P, KC, D], F32R)
            ow_lo = sb("ow_lo", [P, KC, D], F32R)
        if n_chan:
            full = sb("full", [P, 4, TOK])
            part_hi = sb("part_hi", [P, 4, TOK], F32R)
            part_lo = sb("part_lo", [P, 4, TOK], F32R)
        if toks:
            tok_out = sb("tok_out", [P, 2, SUB, D])
            tok_bias = sb("tok_bias", [P, D])

        sp_passed, dve_passed = sem("sp_passed"), sem("dve_passed")
        raw_loaded = [sem(f"raw_loaded{k}") for k in range(4)]
        w_hi_done, w_lo_done, small_loaded = sem("w_hi_done"), sem("w_lo_done"), sem("small_loaded")
        x_loaded = [sem(f"x_loaded{k}") for k in range(2)]
        o_loaded, o_hi_done, o_lo_done = [sem(f"o_loaded{k}") for k in range(2)], sem("o_hi_done"), sem("o_lo_done")
        biased, x_stored = sem("biased"), [sem(f"x_stored{k}") for k in range(2)]
        stat_step, aggregated, var_ready, rstd_ready, normed = (sem("stat_step"), sem("aggregated"),
                                                               sem("var_ready"), sem("rstd_ready"), sem("normed"))
        power_set, ow_lo_done = sem("power_set"), sem("ow_lo_done")
        turned, turned_out, x_hi_done, x_lo_done = sem("turned"), sem("turned_out"), sem("x_hi_done"), sem("x_lo_done")
        xt_stored = [sem(f"xt_stored{k}") for k in range(2)]
        filled, emptied = sem("filled"), sem("emptied")
        hi_ready, lo_ready = sem("hi_ready"), sem("lo_ready")
        hi_stored = [sem(f"hi_stored{k}") for k in range(4)]
        lo_stored = [sem(f"lo_stored{k}") for k in range(4)]
        tok_stored = [sem(f"tok_stored{k}") for k in range(2)]
        if router:
            router.place(ctx, sem)

        pieces = []
        if has_mix:
            pieces += [(mix[1][c * P:(c + 1) * P, :], ow_hi[:, c, :], ow_lo[:, c, :]) for c in range(KC)]
        n_mix_pieces = len(pieces)
        n_first = n_mix_pieces + (KC if n_w else 0)
        for n, w in enumerate(weights):
            pieces += [(w[c * P:(c + 1) * P, :], w_hi[:, n, c, :], w_lo[:, n, c, :]) for c in range(KC)]
        small = []
        if norm:
            small += [(gb[:, 0, :], norm[0]), (gb[:, 1, :], norm[1])]
        if has_mix:
            small += [(o_bias[:], mix[2].partition_broadcast(P))]
        if toks and toks[1] is not None:
            small += [(tok_bias[:], toks[1].partition_broadcast(P))]

        with nc.Block() as block:
            @block.sync
            def _(sp):
                def load_x(i, b, s):
                    if at_least(i, 2):
                        if norm:
                            wait_alone(sp, normed, (i - 1) * SUB, sp_passed)
                        else:
                            wait_alone(sp, turned, (i - 1) * KC, sp_passed)
                        if has_mix:
                            wait_alone(sp, x_stored[s], b * 16, sp_passed)
                    sp.dma_start(x[:, s], src[b, s]).then_inc(x_loaded[s], 16)

                def load_o(i, b, s):
                    if at_least(i, 2):
                        wait_alone(sp, o_lo_done, (i - 1) * KC, sp_passed)
                    sp.dma_start(o[:, s], mix[0][b, s]).then_inc(o_loaded[s], 16)

                def load_pieces(numbers):
                    for u in numbers:
                        if u - 4 >= n_mix_pieces:
                            sp.wait_ge(w_lo_done, u - 3 - n_mix_pieces)
                        elif u >= 4:
                            sp.wait_ge(ow_lo_done, u - 3)
                        sp.dma_start(raw[:, u % 4, :], pieces[u][0]).then_inc(raw_loaded[u % 4], 16)

                def store_x(i, b, s):
                    wait_alone(sp, emptied, mix_seq(i, SUB - 1) + 1, sp_passed)
                    sp.dma_start(mix[3][b, s], x[:, s]).then_inc(x_stored[s], 16)

                if has_mix:
                    load_o(0, 0, 0)
                    load_pieces(range(n_mix_pieces))
                load_x(0, 0, 0)
                for dst, row in small:
                    sp.dma_start(dst, row).then_inc(small_loaded, 16)
                load_pieces(range(n_mix_pieces, n_first))
                load_x(1, 0, 1)
                if has_mix:
                    load_o(1, 0, 1)
                    load_o(2, 1, 0)
                    store_x(0, 0, 0)
                load_pieces(range(n_first, len(pieces)))
                if has_mix:
                    store_x(1, 0, 1)
                load_x(2, 1, 0)
                if router:
                    router.load(sp)

                def body(i, b, s):
                    ahead = TILES - 1 - i if isinstance(i, int) else 3
                    if ahead >= 3:
                        three_on = nxt(i + 2, b + 1, s)
                        if has_mix:
                            load_o(*three_on)
                        load_x(*three_on)
                    if keep_xt:
                        wait_alone(sp, x_lo_done, (i + 1) * KC, sp_passed)
                        for part, home in ((x_hi, keep_xt[0]), (x_lo, keep_xt[1])):
                            sp.dma_start(home[b, s], part[:, s].bitcast(F32)).then_inc(xt_stored[s], 16)
                    if has_mix and ahead >= 2:
                        store_x(i + 2, b + 1, s)
                    for kind, k in work:
                        if kind == "chan":
                            c = i * n_chan + k
                            wait_alone(sp, hi_ready, c + 1, sp_passed)
                            sp.dma_start(chans[k][2][b, s], part_hi[:, k % 4, :].bitcast(F32)).then_inc(hi_stored[k % 4], 16)
                            wait_alone(sp, lo_ready, c + 1, sp_passed)
                            sp.dma_start(chans[k][3][b, s], part_lo[:, k % 4, :].bitcast(F32)).then_inc(lo_stored[k % 4], 16)
                        elif k == SUB - 1:
                            wait_alone(sp, emptied, work_seq(i, n_chan + k) + 1, sp_passed)
                            for g in range(NG):
                                sp.dma_start(toks[2][b, s, g], tok_out[:, s, :, g * P:(g + 1) * P]).then_inc(tok_stored[s], 16)

                on_tiles(sp, body)
                for s in range(2):
                    if has_mix:
                        sp.wait_ge(x_stored[s], 16 * TILES // 2)
                    if keep_xt:
                        sp.wait_ge(xt_stored[s], 32 * TILES // 2)
                    if toks:
                        sp.wait_ge(tok_stored[s], 16 * NG * TILES // 2)
                for k in range(4 if n_chan else 0):
                    sp.wait_ge(hi_stored[k], 16 * TILES * n_chan // 4)
                    sp.wait_ge(lo_stored[k], 16 * TILES * n_chan // 4)

            def schedule(eng, prepare, bias, split, mixing, norming, turning, working, routing=None):
                if has_mix:
                    split(0, 0, 0)
                    prepare(range(n_mix_pieces))
                    bias(0, 0, 0)
                    split(1, 0, 1)
                mixing(0, 0, 0)
                norming(0, 0, 0)
                prepare(range(n_mix_pieces, n_first))
                if has_mix:
                    bias(1, 0, 1)
                    split(2, 1, 0)
                mixing(1, 0, 1)
                for c in range(KC):
                    turning(0, 0, 0, c)
                norming(1, 0, 1)
                prepare(range(n_first, len(pieces)))
                between = lambda tile: routing(eng, tile) if router and routing else None

                def body(i, b, s):
                    ahead = TILES - 1 - i if isinstance(i, int) else 3
                    if has_mix and ahead >= 2:
                        bias(i + 2, b + 1, s)
                    if has_mix and ahead >= 3:
                        split(*nxt(i + 2, b + 1, s))
                    if ahead >= 2:
                        mixing(i + 2, b + 1, s)
                    for q in range(len(work) // 2):
                        working(i, b, s, q)
                    if ahead >= 2:
                        norming(i + 2, b + 1, s)
                    chunks = list(range(KC if ahead >= 1 else 0))
                    for q in range(len(work) // 2, len(work)):
                        for c in chunks[:2] if len(chunks) == KC else chunks[:1]:
                            turning(*nxt(i, b, s), chunks.pop(0))
                        working(i, b, s, q)
                    for c in chunks:
                        turning(*nxt(i, b, s), c)
                on_tiles(eng, body, between)
                between(TILES)

            @block.scalar
            def _(act):
                def prepare(numbers):
                    for u in numbers:
                        act.wait_ge(raw_loaded[u % 4], 16 * (u // 4 + 1))
                        act.copy(pieces[u][1], raw[:, u % 4, :]).then_inc(w_hi_done, 1)

                def split(i, b, s):
                    act.wait_ge(o_loaded[s], (b + 1) * 16)
                    if at_least(i, 2):
                        act.wait_ge(filled, mix_seq(i - 2, SUB - 1) + 1)
                    for c in range(KC):
                        act.copy(o_hi[:, s, c, :], o[:, s, c, :]).then_inc(o_hi_done, 1)

                def mixing(i, b, s):
                    pass

                bias = mixing

                norming = mixing

                def turning(i, b, s, c):
                    act.wait_ge(turned, i * KC + c + 1)
                    if at_least(i, 1):
                        act.wait_ge(x_lo_done, (i - 1) * KC + c + 1)
                    if norm:
                        if isinstance(i, int) and i == 0 and c == 0:
                            act.wait_ge(small_loaded, 16 * len(small))
                        act.activation(xt[:, c, :], tr[:, c % 2, :], ACT.Identity, bias=gb[:, 1, c:c + 1],
                                       scale=gb[:, 0, c:c + 1]).then_inc(turned_out, 1)
                    else:
                        act.copy(xt[:, c, :], tr[:, c % 2, :]).then_inc(turned_out, 1)

                def working(i, b, s, q):
                    kind, k = work[q]
                    if kind == "chan":
                        uses = i * (n_chan // 4) + k // 4
                        act.wait_ge(emptied, work_seq(i, k) + 1)
                        if k >= 4 or at_least(i, 1):
                            act.wait_ge(hi_stored[k % 4], uses * 16)
                            act.wait_ge(lo_ready, i * n_chan + k - 3)
                        act.copy(part_hi[:, k % 4, :], full[:, k % 4, :]).then_inc(hi_ready, 1)

                schedule(act, prepare, bias, split, mixing, norming, turning, working)

            @block.gpsimd
            def _(pool):
                if norm:
                    pool.memset(power[:], -0.5).then_inc(power_set, 1)
                    pool.wait_ge(power_set, 1)
                if router:
                    router.constants(pool)

                def prepare(numbers):
                    for u in numbers:
                        if u < n_mix_pieces:
                            continue
                        pool.wait_ge(w_hi_done, u + 1)
                        pool.tensor_tensor(pieces[u][2], raw[:, u % 4, :], pieces[u][1].bitcast(F32),
                                           ALU.subtract).then_inc(w_lo_done, 1)

                def split(i, b, s):
                    for c in range(KC):
                        pool.wait_ge(o_hi_done, i * KC + c + 1)
                        if at_least(i, 2) and c == 0:
                            pool.wait_ge(filled, mix_seq(i - 2, SUB - 1) + 1)
                        pool.tensor_tensor(o_lo[:, s, c, :], o[:, s, c, :], o_hi[:, s, c, :].bitcast(F32),
                                           ALU.subtract).then_inc(o_lo_done, 1)

                def bias(i, b, s):
                    pool.wait_ge(x_loaded[s], (b + 1) * 16)
                    if isinstance(i, int) and i == 0:
                        pool.wait_ge(small_loaded, 16 * len(small))
                    for u in range(SUB):
                        pool.tensor_tensor(x[:, s, u, :], x[:, s, u, :], o_bias[:], ALU.add).then_inc(biased, 1)

                def mixing(i, b, s):
                    if norm:
                        pool.wait_ge(var_ready, i + 1)
                        pool.tensor_tensor(rstd[:], var[:], power[:], ALU.pow).then_inc(rstd_ready, 1)

                def norming(i, b, s):
                    pass

                def turning(i, b, s, c):
                    pass

                def working(i, b, s, q):
                    kind, k = work[q]
                    if kind == "chan":
                        uses = i * (n_chan // 4) + k // 4
                        pool.wait_ge(hi_ready, i * n_chan + k + 1)
                        if k >= 4 or at_least(i, 1):
                            pool.wait_ge(lo_stored[k % 4], uses * 16)
                        pool.tensor_tensor(part_lo[:, k % 4, :], full[:, k % 4, :],
                                           part_hi[:, k % 4, :].bitcast(F32), ALU.subtract).then_inc(lo_ready, 1)

                schedule(pool, prepare, bias, split, mixing, norming, turning, working,
                         router.pool_step if router else None)

            @block.vector
            def _(dve):
                def prepare(numbers):
                    for u in numbers:
                        if u >= n_mix_pieces:
                            continue
                        dve.wait_ge(w_hi_done, u + 1)
                        dve.tensor_tensor(pieces[u][2], raw[:, u % 4, :], pieces[u][1].bitcast(F32),
                                          ALU.subtract).then_inc(ow_lo_done, 1)

                def split(i, b, s):
                    pass

                bias = split

                def mixing(i, b, s):
                    if not has_mix and not norm:
                        return
                    dve.wait_ge(x_loaded[s], (b + 1) * 16)
                    if has_mix:
                        for u in range(SUB):
                            dve.wait_ge(biased, i * SUB + u + 1)
                            dve.wait_ge(filled, mix_seq(i, u) + 1)
                            dve.tensor_tensor(x[:, s, u, :], ring[:, u % RING, :], x[:, s, u, :],
                                              ALU.add).then_inc(emptied, 1)
                        dve.wait_ge(emptied, mix_seq(i, SUB - 1) + 1)
                    if not norm:
                        return
                    for u in range(SUB):
                        last = dve.bn_stats(stats[:, u, :], x[:, s, u, :])
                    last.then_inc(stat_step, 1)
                    wait_alone(dve, stat_step, i + 1, dve_passed)
                    for u in range(SUB):
                        last = dve.bn_aggr(mv[:, u, :], stats[:, u, :])
                    last.then_inc(aggregated, 1)
                    dve.wait_ge(aggregated, i + 1)
                    dve.tensor_scalar_add(var[:], mv[:, :, 1], EPS).then_inc(var_ready, 1)

                def norming(i, b, s):
                    if not norm:
                        return
                    dve.wait_ge(rstd_ready, i + 1)
                    if at_least(i, 2):
                        dve.wait_ge(turned, (i - 1) * KC)
                    for u in range(SUB):
                        dve.tensor_scalar(xn[:, s, u, :], x[:, s, u, :], mv[:, u, 0:1], rstd[:, u:u + 1],
                                          ALU.subtract, ALU.mult).then_inc(normed, 1)

                def turning(i, b, s, c):
                    dve.wait_ge(turned_out, i * KC + c + 1)
                    if c == 0 and at_least(i, 2):
                        if work:
                            dve.wait_ge(filled, work_seq(i - 2, len(work) - 1) + 1)
                        if keep_xt:
                            dve.wait_ge(xt_stored[s], b * 32)
                    dve.tensor_copy(x_hi[:, s, c, :], xt[:, c, :]).then_inc(x_hi_done, 1)
                    dve.wait_ge(x_hi_done, i * KC + c + 1)
                    dve.tensor_tensor(x_lo[:, s, c, :], xt[:, c, :], x_hi[:, s, c, :].bitcast(F32),
                                      ALU.subtract).then_inc(x_lo_done, 1)

                def working(i, b, s, q):
                    kind, k = work[q]
                    dve.wait_ge(filled, work_seq(i, q) + 1)
                    bank = ring[:, q % RING, :]
                    if kind == "chan":
                        if k >= 4 or at_least(i, 1):
                            dve.wait_ge(lo_ready, i * n_chan + k - 3)
                        chans[k][1](dve, full[:, k % 4, :], bank, s).then_inc(emptied, 1)
                    else:
                        if k == 0 and at_least(i, 2):
                            dve.wait_ge(tok_stored[s], b * 16 * NG)
                        if k == 0 and isinstance(i, int) and i == 0 and small:
                            dve.wait_ge(small_loaded, 16 * len(small))
                        out = tok_out[:, s, k, :]
                        ins = (dve.tensor_tensor(out, bank, tok_bias[:], ALU.add) if toks[1] is not None
                               else dve.tensor_copy(out, bank))
                        ins.then_inc(emptied, 1)

                schedule(dve, prepare, bias, split, mixing, norming, turning, working,
                         router.vector_step if router else None)

            @block.tensor
            def _(pe):
                def bank_free(seq, q, i):
                    if not (isinstance(seq, int) and seq < RING):
                        pe.wait_ge(emptied, seq - RING + 1)

                def prepare(numbers):
                    pass

                def split(i, b, s):
                    pass

                bias = split

                def mixing(i, b, s):
                    if not has_mix:
                        return
                    if isinstance(i, int) and i == 0:
                        pe.wait_ge(ow_lo_done, n_mix_pieces)
                    pe.wait_ge(o_lo_done, (i + 1) * KC)
                    for u in range(SUB):
                        bank_free(mix_seq(i, u), u, i)
                        cols = slice(u * P, (u + 1) * P)
                        three(pe, ring[:, u % RING, :],
                                     [(o_hi[:, s, c, cols], o_lo[:, s, c, cols], ow_hi[:, c, :], ow_lo[:, c, :])
                                      for c in range(KC)], True, True).then_inc(filled, 1)

                def norming(i, b, s):
                    pass

                def turning(i, b, s, c):
                    if c == 0 and norm:
                        pe.wait_ge(normed, (i + 1) * SUB)
                    elif c == 0:
                        pe.wait_ge(x_loaded[s], (b + 1) * 16)
                    tokens = (xn if norm else x)[:, s]
                    if c >= 2 or at_least(i, 1):
                        pe.wait_ge(turned_out, i * KC + c - 1)
                    for u in range(SUB):
                        last = pe.transpose(tr[:, c % 2, u * P:(u + 1) * P],
                                            tokens[:, u, c * P:(c + 1) * P], ident[:])
                    last.then_inc(turned, 1)

                def working(i, b, s, q):
                    kind, k = work[q]
                    if q == 0:
                        pe.wait_ge(x_lo_done, (i + 1) * KC)
                    bank_free(work_seq(i, q), q, i)
                    if isinstance(i, int) and i == 0:
                        used = chans[k][0] // KC if kind == "chan" else toks[0]
                        pe.wait_ge(w_lo_done, (used + 1) * KC)
                    if kind == "chan":
                        w, m = divmod(chans[k][0], KC)
                        cols = slice(m * P, (m + 1) * P)
                        pairs = [(w_hi[:, w, c, cols], w_lo[:, w, c, cols], x_hi[:, s, c, :], x_lo[:, s, c, :])
                                 for c in range(KC)]
                    else:
                        cols = slice(k * P, (k + 1) * P)
                        pairs = [(x_hi[:, s, c, cols], x_lo[:, s, c, cols], w_hi[:, toks[0], c, :],
                                  w_lo[:, toks[0], c, :]) for c in range(KC)]
                    three(pe, ring[:, q % RING, :], pairs, True, True).then_inc(filled, 1)

                schedule(pe, prepare, bias, split, mixing, norming, turning, working,
                         router.tensor_step if router else None)
        sem.clear()


def attention_stage(nc, tag, ident, q_hi, q_lo, k_hi, k_lo, v, out, keep=None, mask_qk=None,
                    mask_kq=None, ident_bf=None):
    causal = keep is not None
    N = B * NG
    SETS = 3
    steps = [(h, t, max(0, t * P - h * TOK) if causal else 0) for h in range(HALVES)
             for t in range((h + 1) * TOK // P if causal else KT)]
    last_step = {h: max(n for n, st in enumerate(steps) if st[0] == h) for h in range(HALVES)}
    NS, NBLOCKS = len(steps), len(steps) * HG
    UNITS = HG * KT
    PR = 6 if causal else 8
    LAG = 3
    TURN_BANK = 2
    PE_TURN_HEAD = 2 if causal else 3
    TURN, TURN_HEAD = NS - LAG, 2
    if causal:
        groups = [(k, 2, 2, k + 3) for k in range(0, NS, 2)]
    else:
        assert KT == 8
        groups = [(h * KT + k, *g) for h in range(HALVES) for k, g in
                  ((0, (3, 3, h * KT + 4)), (3, (3, 3, h * KT + 7)), (6, (2, 2, h * KT + 10)))]
    summing = [[((at + c) // NS, g, c) for g, (_, _, parts, at) in enumerate(groups) for c in range(parts)
                if (at + c) % NS == k] for k in range(NS)]
    group_of = [next(g for g, (first, length, _, _) in enumerate(groups) if first <= k < first + length)
                for k in range(NS)]
    additions = lambda g: sum(length - 1 for _, length, _, _ in groups[:g + 1])
    parts_to = lambda g: sum(parts for _, _, parts, _ in groups[:g + 1])
    ADDITIONS, PARTS = additions(len(groups)), parts_to(len(groups))
    COPY = groups[-1][3] + groups[-1][2] - 1
    PIECES = 4 if causal else 8
    CH = TOK // PIECES
    copy_steps = [last_step[h] + COPY - (NS - 1) for h in range(HALVES)]
    norm_steps = []
    for h in range(HALVES):
        at, norm_steps_h = copy_steps[h] + 1, []
        for c in range(PIECES):
            at += at % NS == TURN
            norm_steps_h.append(at)
            at = min(at + 1, copy_steps[h] + 8)
        norm_steps.append(norm_steps_h)
    FIRST_LATE = norm_steps[0][-1] // NS
    assert SETS * NS % PR == 0 and NBLOCKS % 2 == 0
    START = TURN * HG + TURN_HEAD
    free = []
    for at in range(NBLOCKS):
        k, j = divmod((START + at) % NBLOCKS, HG)
        free.append(150 + TOK - steps[k][2] if j in (0, 2) else 0)
    place, acc = [], 0.0
    unit_size = [0.3 + ((u % KT) + 1 if causal else KT) for u in range(UNITS)]
    for u in range(UNITS):
        x, at = acc / sum(unit_size) * sum(free), 0
        while x >= free[at]:
            x -= free[at]
            at += 1
        place.append(START + at - NBLOCKS)
        acc += unit_size[u]
    if causal:
        bank_of = [(0, 1, 2, 3, 0, 2, 0, 2)[u % KT] for u in range(UNITS)]
        reach = [(2, 3, 3, 4, 3, 2, 2, 2)[u % KT] for u in range(UNITS)]
    else:
        bank_of, reach = [u % 2 * 2 for u in range(UNITS)], [2] * UNITS
    next_units = [[[u for u in range(UNITS) if place[u] == k * HG + j] for j in range(HG)] for k in range(NS)]
    later_units = [[[u for u in range(UNITS) if place[u] + NBLOCKS == k * HG + j] for j in range(HG)]
                   for k in range(NS)]
    early_units = [u for u in range(UNITS) if place[u] < 0]

    with ExitStack() as ctx:
        sb = lambda name, shape, dt=F32: ctx.enter_context(nc.sbuf_tensor(tag + name, shape, dt))
        sem = Semaphores(nc, ctx, tag)
        qs = [sb(f"qs{p}", [P, HG, S], F32R) for p in range(SETS)]
        ks = [sb(f"ks{p}", [P, HG, S], F32R) for p in range(SETS)]
        vs = [sb(f"vs{p}", [P, KT, P]) for p in range(SETS)]
        key_mask = sb("key_mask", [1, S], F32R) if causal else None
        probs = sb("probs", [P, PR, HG, TOK])
        ones = sb("ones", [P, DH])
        neg_max = sb("neg_max", [P, UNITS])
        max_hi = sb("max_hi", [UNITS, P], F32R)
        max_lo = sb("max_lo", [UNITS, P], F32R)
        sums = sb("sums", [P, HALVES, TOK])
        outs = sb("outs", [P, HALVES, TOK])
        nat = ctx.enter_context(nc.psum_tensor(tag + "nat", [P, 4, 512], F32))
        st_ps = ctx.enter_context(nc.psum_tensor(tag + "st", [P, 2, 512], F32))
        pv_ps = ctx.enter_context(nc.psum_tensor(tag + "pv", [P, 512], F32))
        sum_ps = ctx.enter_context(nc.psum_tensor(tag + "sum", [P, 512], F32))

        consts_set, ones_set, sp_passed = sem("consts_set"), sem("ones_set"), sem("sp_passed")
        added = sem("added")
        loaded = [sem(f"loaded{p}") for p in range(SETS)]
        rows_loaded = [sem(f"rows_loaded{p}") for p in range(SETS)]
        nat_ready, maxed, max_turned, max_split = sem("nat_ready"), sem("maxed"), sem("max_turned"), sem("max_split")
        st_ready, exped, weighed, summed = sem("st_ready"), sem("exped"), sem("weighed"), sem("summed")
        set0_made, key_mask_made = sem("set0_made"), sem("key_mask_made")
        head_loaded, v0_loaded = [sem(f"head_loaded{j}") for j in range(HG)], sem("v0_loaded")
        sums_copied, outs_copied, inverted, normalised = (sem("sums_copied"), sem("outs_copied"), sem("inverted"),
                                                          sem("normalised"))
        out_stored = [sem(f"out_stored{h}") for h in range(HALVES)]
        LOADS = 7
        FILLS, MASKS = 2, (32 if causal else 0)

        def schedule(eng, body):
            body(0, 0, 0)
            with eng.Fori(0, (N - 4) // SETS) as j:
                body(j * 3 + 1, j, 1)
                body(j * 3 + 2, j, 2)
                body(j * 3 + 3, j + 1, 0)
            for n in range(N - 3, N):
                body(n, n // SETS, n % SETS)

        def after(n, m, p):
            return (n + 1, m, p + 1) if p < SETS - 1 else (n + 1, m + 1, 0)

        def is_last(n):
            return isinstance(n, int) and n == N - 1

        with nc.Block() as block:
            @block.sync
            def _(sp):
                def load(n, m, p):
                    if at_least(n, SETS):
                        wait_alone(sp, weighed, (n - 2) * NS, sp_passed)
                    heads = "(h r) t -> r h t"
                    for row, part in ((0, q_hi), (1, q_hi), (2, q_lo)):
                        sp.dma_start(qs[p][row * DH:(row + 1) * DH].bitcast(F32),
                                     part[n].rearrange(heads, r=DH)).then_inc(loaded[p], 16)
                    for row, part in ((0, k_hi), (1, k_lo), (2, k_hi)):
                        sp.dma_start(ks[p][row * DH:(row + 1) * DH].bitcast(F32),
                                     part[n].rearrange(heads, r=DH)).then_inc(loaded[p], 16)
                    sp.dma_start(vs[p][:], v[n].rearrange("k p c -> p k c")).then_inc(loaded[p], 16)

                def rows(n, m, p):
                    wait_alone(sp, max_split, (n + 1) * 2, sp_passed)
                    for row, part in ((MAX_HI_ROW, max_hi), (MAX_LO_ROW, max_lo)):
                        sp.dma_start(qs[p][row:row + 1].bitcast(F32), part[:].bitcast(F32)).then_inc(rows_loaded[p], 16)

                def store(n, h):
                    wait_alone(sp, normalised, (n * HALVES + h + 1) * PIECES, sp_passed)
                    sp.dma_start(out[n][:, h * TOK:(h + 1) * TOK], outs[:, h, :]).then_inc(out_stored[h], 16)

                def mask_rows(p, made):
                    for dst, row in ((qs[p], keep[0:1, :]), (ks[p], key_mask[0:1, :].bitcast(F32))):
                        sp.dma_start(dst[AUG:AUG + 1].bitcast(F32),
                                     row.unsqueeze(1).to_broadcast([1, HG, S])).then_inc(made, 16)

                for j in range(HG):
                    head = slice(j * DH, (j + 1) * DH)
                    for row, part in ((0, q_hi), (1, q_hi), (2, q_lo)):
                        sp.dma_start(qs[0][row * DH:(row + 1) * DH, j].bitcast(F32),
                                     part[0][head, :]).then_inc(head_loaded[j], 16)
                    for row, part in ((0, k_hi), (1, k_lo), (2, k_hi)):
                        sp.dma_start(ks[0][row * DH:(row + 1) * DH, j].bitcast(F32),
                                     part[0][head, :]).then_inc(head_loaded[j], 16)
                    if j == 0 and causal:
                        sp.wait_ge(set0_made, FILLS)
                        sp.wait_ge(key_mask_made, 1)
                        mask_rows(0, set0_made)
                sp.dma_start(vs[0][:], v[0].rearrange("k p c -> p k c")).then_inc(v0_loaded, 16)
                load(1, 0, 1)
                if causal:
                    sp.wait_ge(consts_set, FILLS * (SETS - 1))
                    for p in range(1, SETS):
                        mask_rows(p, consts_set)
                rows(0, 0, 0)
                sp.wait_ge(consts_set, (FILLS + MASKS) * (SETS - 1))

                def body(n, m, p):
                    if not (isinstance(n, int) and n >= N - 2):
                        load(*after(*after(n, m, p)))
                    if at_least(n, 1):
                        if FIRST_LATE:
                            store(n - 1, 0)
                        store(n - 1, 1)
                    if not is_last(n):
                        rows(*after(n, m, p))
                    if not FIRST_LATE:
                        store(n, 0)
                schedule(sp, body)
                if FIRST_LATE:
                    store(N - 1, 0)
                store(N - 1, 1)
                for h in range(HALVES):
                    sp.wait_ge(out_stored[h], 16 * N)

            @block.gpsimd
            def _(pool):
                pool.memset(ones[:], 1.0).then_inc(ones_set, 1)
                pool.wait_ge(ones_set, 1)
                pool.memset(qs[0][AUG:ROWS].bitcast(F32), 0.0).then_inc(set0_made, 1)
                for p in range(1, SETS):
                    pool.memset(ks[p][AUG:ROWS].bitcast(F32), 1.0).then_inc(consts_set, 1)
                    pool.memset(qs[p][AUG:ROWS].bitcast(F32), 0.0).then_inc(consts_set, 1)
                pool.wait_ge(consts_set, FILLS * (SETS - 1))

                def body(n, m, p):
                    for g, (k, length, _, _) in enumerate(groups):
                        for more in range(1, length):
                            done = n * ADDITIONS + additions(g) - length + more
                            first = steps[k + more][2]
                            pool.wait_ge(exped, n * NBLOCKS + (k + more + 1) * HG)
                            if more == 1:
                                pool.wait_ge(weighed, n * NS + k + 1)
                            else:
                                pool.wait_ge(added, done)
                            for j in range(HG):
                                here, there = (probs[:, (p * NS + i) % PR, j, first:TOK] for i in (k, k + more))
                                last = pool.tensor_tensor(here, here, there, ALU.add)
                            last.then_inc(added, 1)
                schedule(pool, body)

            @block.vector
            def _(dve):
                dve.memset(ks[0][AUG:ROWS].bitcast(F32), 1.0).then_inc(set0_made, 1)
                if causal:
                    dve.tensor_scalar(key_mask[:], keep[0:1, :], -NEG, NEG, ALU.mult, ALU.add).then_inc(key_mask_made, 1)

                def copy_outs(n, h):
                    dve.wait_ge(weighed, n * NS + last_step[h] + 1)
                    if at_least(n, 1):
                        dve.wait_ge(out_stored[h], n * 16)
                    dve.tensor_copy(outs[:, h, :], pv_ps[:]).then_inc(outs_copied, 1)

                def maximum(n, u):
                    keys = ((u % KT) + 1) * P if causal else S
                    banks = 2 if keys > 512 else 1
                    dve.wait_ge(nat_ready, n * UNITS + u + 1)
                    if u == 0 and at_least(n, 1):
                        dve.wait_ge(max_turned, n)
                    dve.tensor_reduce(neg_max[:, u:u + 1], nat[:, bank_of[u]:bank_of[u] + banks, 0:keys // banks], AX.XY,
                                      ALU.max, negate=True).then_inc(maxed, 1)

                def split_max(n, before=None):
                    dve.wait_ge(max_turned, n + 1)
                    if before is not None:
                        dve.wait_ge(rows_loaded[before[2]], (before[1] + 1) * 32)
                    turned = nat[0:UNITS, TURN_BANK, 0:P]
                    dve.tensor_copy(max_hi[:], turned).then_inc(max_split, 1)
                    dve.wait_ge(max_split, n * 2 + 1)
                    dve.tensor_tensor(max_lo[:], turned, max_hi[:].bitcast(F32), ALU.subtract).then_inc(max_split, 1)

                def normalise(n, h, c):
                    cols = slice(c * CH, (c + 1) * CH)
                    done = (n * HALVES + h) * PIECES + c
                    if c == 0:
                        dve.wait_ge(sums_copied, n * HALVES + h + 1)
                        dve.wait_ge(outs_copied, n * HALVES + h + 1)
                    dve.reciprocal(sums[:, h, cols], sums[:, h, cols]).then_inc(inverted, 1)
                    dve.wait_ge(inverted, done + 1)
                    dve.tensor_tensor(outs[:, h, cols], outs[:, h, cols], sums[:, h, cols],
                                      ALU.mult).then_inc(normalised, 1)

                for u in range(UNITS):
                    maximum(0, u)
                split_max(0)
                for u in early_units:
                    maximum(1, u)

                def body(n, m, p):
                    nn = after(n, m, p)
                    for k, (h, t, _) in enumerate(steps):
                        for j in range(HG):
                            if k == last_step[h] and j == HG // 2:
                                copy_outs(n, h)
                            if k == TURN and j == TURN_HEAD and not is_last(n):
                                split_max(nn[0], (n, m, p))
                            if not is_last(n):
                                for u in next_units[k][j]:
                                    maximum(n + 1, u)
                            if not (isinstance(n, int) and n >= N - 2):
                                for u in later_units[k][j]:
                                    maximum(n + 2, u)
                            if j == HG // 2:
                                for half in reversed(range(HALVES)):
                                    for c, at in enumerate(norm_steps[half]):
                                        if at % NS == k and at_least(n, at // NS):
                                            normalise(n - at // NS, half, c)
                schedule(dve, body)
                for half in range(HALVES):
                    for c, at in enumerate(norm_steps[half]):
                        if at >= NS:
                            normalise(N - 1, half, c)

            @block.scalar
            def _(act):
                def exponentials(n, p, k):
                    first = steps[k][2]
                    for j in range(HG):
                        blk = k * HG + j
                        act.wait_ge(st_ready, n * NBLOCKS + blk + 1)
                        if j == 0 and k >= PR:
                            act.wait_ge(summed, n * PARTS + parts_to(group_of[k - PR]))
                        elif j == 0 and at_least(n, 1):
                            act.wait_ge(summed, (n - 1) * PARTS + parts_to(group_of[k - PR + NS]))
                        act.activation(probs[:, (p * NS + k) % PR, j, first:TOK], st_ps[:, blk % 2, first:TOK],
                                       ACT.Exp).then_inc(exped, 1)

                def copy_sums(n, h):
                    act.wait_ge(summed, n * PARTS + parts_to(group_of[last_step[h]]))
                    if at_least(n, 1):
                        act.wait_ge(normalised, ((n - 1) * HALVES + h + 1) * PIECES)
                    act.copy(sums[:, h, :], sum_ps[:]).then_inc(sums_copied, 1)

                exponentials(0, 0, 0)

                def body(n, m, p):
                    nn = after(n, m, p)
                    for k, (h, t, _) in enumerate(steps):
                        if k + 1 < NS:
                            exponentials(n, p, k + 1)
                        elif not is_last(n):
                            exponentials(nn[0], nn[2], 0)
                        for half, at in enumerate(copy_steps):
                            if at % NS == k and at_least(n, at // NS):
                                copy_sums(n - at // NS, half)
                schedule(act, body)
                copy_sums(N - 1, HALVES - 1)

            @block.tensor
            def _(pe):
                def max_scores(n, m, p, u):
                    j, t = divmod(u, KT)
                    keys = (t + 1) * P if causal else S
                    banks = 2 if keys > 512 else 1
                    width = keys // banks
                    rows = AUG + 1 if causal else AUG
                    if isinstance(n, int) and n == 0 and u % KT == 0:
                        pe.wait_ge(head_loaded[u // KT], 6 * 16)
                    if u == 0 and at_least(n, 1):
                        pe.wait_ge(loaded[p], (m if p == 0 else m + 1) * LOADS * 16)
                    if bank_of[u] == TURN_BANK and u <= TURN_BANK and at_least(n, 1):
                        pe.wait_ge(max_split, n * 2)
                    if u >= reach[u] or at_least(n, 1):
                        pe.wait_ge(maxed, n * UNITS + u + 1 - reach[u])
                    for bank in range(banks):
                        cols = max(width, 256)
                        diagonal = causal and bank == banks - 1
                        last = pe.matmul(nat[:, bank_of[u] + bank, 0:cols], qs[p][0:rows, j, t * P:(t + 1) * P],
                                         ks[p][0:rows, j, bank * width:bank * width + cols], start=True,
                                         stop=not diagonal)
                        if diagonal:
                            last = pe.matmul(nat[:, bank_of[u] + bank, width - P:width], ident_bf[:], mask_qk[:],
                                             start=False, stop=True)
                    last.then_inc(nat_ready, 1)

                def turn_max(n):
                    pe.wait_ge(maxed, (n + 1) * UNITS)
                    pe.transpose(nat[0:UNITS, TURN_BANK, 0:P], neg_max[:], ident[:]).then_inc(max_turned, 1)

                def scores(n, m, p, k, j):
                    h, t, first = steps[k]
                    blk = k * HG + j
                    if k == 0 and j == 0:
                        pe.wait_ge(rows_loaded[p], (m + 1) * 32)
                    if blk >= 2 or at_least(n, 1):
                        pe.wait_ge(exped, n * NBLOCKS + blk - 1)
                    lo = min(first, TOK - 256)
                    diagonal = causal and t * P >= h * TOK
                    last = pe.matmul(st_ps[:, blk % 2, lo:TOK], ks[p][0:ROWS, j, t * P:(t + 1) * P],
                                     qs[p][0:ROWS, j, h * TOK + lo:(h + 1) * TOK], start=True,
                                     stop=not diagonal)
                    if diagonal:
                        last = pe.matmul(st_ps[:, blk % 2, first:first + P], ident_bf[:], mask_kq[:],
                                         start=False, stop=True)
                    last.then_inc(st_ready, 1)

                def weigh(n, p, k):
                    h, t, first = steps[k]
                    pe.wait_ge(exped, n * NBLOCKS + (k + 1) * HG)
                    if t == 0 and (h or at_least(n, 1)):
                        pe.wait_ge(outs_copied, n * HALVES + h)
                    for j in range(HG):
                        last = pe.matmul(pv_ps[j * DH:(j + 1) * DH, first:TOK], vs[p][:, t, j * DH:(j + 1) * DH],
                                         probs[:, (p * NS + k) % PR, j, first:TOK],
                                         start=(t == 0), stop=(k == last_step[h]), skip_group_check=True)
                    last.then_inc(weighed, 1)

                def sum_up(n, p, g, c):
                    i, length, parts, _ = groups[g]
                    h, t, first = steps[i]
                    if c == 0:
                        pe.wait_ge(added, n * ADDITIONS + additions(g))
                        if t == 0 and (h or at_least(n, 1)):
                            pe.wait_ge(sums_copied, n * HALVES + h)
                    width = TOK - first
                    cols = slice(first + width * c // parts, first + width * (c + 1) // parts)
                    for j in range(HG):
                        last = pe.matmul(sum_ps[j * DH:(j + 1) * DH, cols], ones[:],
                                         probs[:, (p * NS + i) % PR, j, cols], start=(t == 0 and c == 0),
                                         stop=(i + length - 1 == last_step[h]), skip_group_check=True)
                    last.then_inc(summed, 1)

                if causal:
                    pe.wait_ge(set0_made, FILLS + MASKS)
                for u in range(UNITS):
                    max_scores(0, 0, 0, u)
                pe.wait_ge(set0_made, FILLS + MASKS)
                turn_max(0)
                pe.wait_ge(ones_set, 1)
                pe.wait_ge(v0_loaded, 16)
                pe.wait_ge(consts_set, (FILLS + MASKS) * (SETS - 1))
                for u in early_units:
                    max_scores(1, 0, 1, u)
                for j in range(HG):
                    scores(0, 0, 0, 0, j)

                def body(n, m, p):
                    nn = after(n, m, p)
                    for k in range(NS):
                        following = (n, m, p, k + 1) if k + 1 < NS else None if is_last(n) else (*nn, 0)
                        for j in range(HG):
                            if following:
                                scores(*following, j)
                            if k == TURN and j == PE_TURN_HEAD and not is_last(n):
                                turn_max(nn[0])
                            if not is_last(n):
                                for u in next_units[k][j]:
                                    max_scores(*nn, u)
                            if not (isinstance(n, int) and n >= N - 2):
                                for u in later_units[k][j]:
                                    max_scores(*after(*nn), u)
                            if j == 1:
                                weigh(n, p, k)
                            if j == HG - 1:
                                for back, g, c in summing[k]:
                                    if at_least(n, back):
                                        sum_up(n - back, p - back, g, c)
                schedule(pe, body)
                for k in range(NS):
                    for back, g, c in summing[k]:
                        if back:
                            sum_up(N - 1, (N - 1) % SETS, g, c)
        sem.clear()


def mlp_stage(nc, xt_hi, xt_lo, x_src, w1, b1, w2, b2, out):
    NC = FF // P
    LAG, RING = 2, 4
    with ExitStack() as ctx:
        sb = lambda name, shape, dt=F32: ctx.enter_context(nc.sbuf_tensor("m_" + name, shape, dt))
        sem = Semaphores(nc, ctx, "m_")
        w1_hi = sb("w1_hi", [P, NC, KC, P], F32R)
        w1_lo = sb("w1_lo", [P, NC, KC, P], F32R)
        w2_hi = sb("w2_hi", [P, NC, D], F32R)
        w2_lo = sb("w2_lo", [P, NC, D], F32R)
        raw = sb("raw", [P, 4, D])
        x_hi = sb("x_hi", [P, KC, TOK], F32R)
        x_lo = sb("x_lo", [P, KC, TOK], F32R)
        x = sb("x", [P, SUB, D])
        b1_sb = sb("b1", [P, NC])
        b2_sb = sb("b2", [P, D])
        hid = sb("hid", [P, RING, TOK])
        hid_hi = sb("hid_hi", [P, RING, TOK], F32R)
        hid_lo = sb("hid_lo", [P, RING, TOK], F32R)
        h_ps = ctx.enter_context(nc.psum_tensor("m_h_ps", [P, RING, 512], F32))
        o_ps = ctx.enter_context(nc.psum_tensor("m_o_ps", [P, SUB, 512], F32))
        sp_passed = sem("sp_passed")
        raw_loaded = [sem(f"raw_loaded{k}") for k in range(4)]
        small_loaded, w_hi_done, w_lo_done = sem("small_loaded"), sem("w_hi_done"), sem("w_lo_done")
        xt_loaded, x_loaded, biased = sem("xt_loaded"), sem("x_loaded"), sem("biased")
        h_filled, relu_done, hid_hi_done, hid_lo_done = (sem("h_filled"), sem("relu_done"), sem("hid_hi_done"),
                                                         sem("hid_lo_done"))
        multiplied, summed, stored = sem("multiplied"), sem("summed"), sem("stored")
        pieces = []
        for c in range(NC):
            pieces.append((w1.rearrange("(k p) f -> p k f", p=P)[:, :, c * P:(c + 1) * P],
                           w1_hi[:, c].rearrange("p k f -> p (k f)"), w1_lo[:, c].rearrange("p k f -> p (k f)")))
            pieces.append((w2[c * P:(c + 1) * P, :], w2_hi[:, c, :], w2_lo[:, c, :]))
        AHEAD = 3

        with nc.Block() as block:
            @block.sync
            def _(sp):
                def load(u):
                    if u >= 4:
                        sp.wait_ge(w_lo_done, u - 3)
                    dst = raw[:, u % 4, :]
                    if u % 2 == 0:
                        dst = dst.rearrange("p (k f) -> p k f", k=KC)
                    sp.dma_start(dst, pieces[u][0]).then_inc(raw_loaded[u % 4], 16)

                def load_xt(i, b, s):
                    if at_least(i, 1):
                        wait_alone(sp, h_filled, i * NC, sp_passed)
                    sp.dma_start(x_hi[:].bitcast(F32), xt_hi[b, s]).then_inc(xt_loaded, 16)
                    sp.dma_start(x_lo[:].bitcast(F32), xt_lo[b, s]).then_inc(xt_loaded, 16)

                def load_x(i, b, s):
                    if at_least(i, 1):
                        wait_alone(sp, stored, i * 16, sp_passed)
                    sp.dma_start(x[:], x_src[b, s]).then_inc(x_loaded, 16)

                def store(i, b, s):
                    wait_alone(sp, summed, (i + 1) * SUB, sp_passed)
                    sp.dma_start(out[b, s], x[:]).then_inc(stored, 16)

                load(0)
                load_xt(0, 0, 0)
                sp.dma_start(b1_sb[:], b1).then_inc(small_loaded, 16)
                for u in range(1, 4):
                    load(u)
                sp.dma_start(b2_sb[:], b2.partition_broadcast(P)).then_inc(small_loaded, 16)
                load_x(0, 0, 0)
                for u in range(4, len(pieces)):
                    load(u)

                def body(i, b, s):
                    if isinstance(i, int) and i == TILES - 1:
                        return
                    load_xt(*nxt(i, b, s))
                    store(i, b, s)
                    load_x(*nxt(i, b, s))
                on_tiles(sp, body)
                store(TILES - 1, B - 1, 1)
                sp.wait_ge(stored, 16 * TILES)

            @block.scalar
            def _(act):
                def split(u):
                    act.wait_ge(raw_loaded[u % 4], 16 * (u // 4 + 1))
                    act.copy(pieces[u][1], raw[:, u % 4, :]).then_inc(w_hi_done, 1)

                for u in range(2 * AHEAD):
                    split(u)
                act.wait_ge(small_loaded, 32)

                def body(i, b, s):
                    for c in range(NC):
                        if isinstance(i, int) and i == 0 and c + AHEAD < NC:
                            split(2 * (c + AHEAD))
                            split(2 * (c + AHEAD) + 1)
                        act.wait_ge(h_filled, i * NC + c + 1)
                        if c >= RING or at_least(i, 1):
                            act.wait_ge(hid_lo_done, i * NC + c - RING + 1)
                        act.activation(hid[:, c % RING, :], h_ps[:, c % RING, :], ACT.Relu,
                                       bias=b1_sb[:, c:c + 1]).then_inc(relu_done, 1)
                on_tiles(act, body)

            @block.gpsimd
            def _(pool):
                def split(u):
                    pool.wait_ge(w_hi_done, u + 1)
                    pool.tensor_tensor(pieces[u][2], raw[:, u % 4, :], pieces[u][1].bitcast(F32),
                                       ALU.subtract).then_inc(w_lo_done, 1)

                for u in range(2 * AHEAD):
                    split(u)
                pool.wait_ge(small_loaded, 32)

                def body(i, b, s):
                    for c in range(NC):
                        if isinstance(i, int) and i == 0 and c + AHEAD < NC:
                            split(2 * (c + AHEAD))
                            split(2 * (c + AHEAD) + 1)
                        if 8 <= c < 8 + SUB:
                            u = c - 8
                            pool.wait_ge(x_loaded, (i + 1) * 16)
                            pool.tensor_tensor(x[:, u, :], x[:, u, :], b2_sb[:], ALU.add).then_inc(biased, 1)
                        pool.wait_ge(hid_hi_done, i * NC + c + 1)
                        if c >= RING or at_least(i, 1):
                            pool.wait_ge(multiplied, i * NC + c - RING + 1)
                        pool.tensor_tensor(hid_lo[:, c % RING, :], hid[:, c % RING, :],
                                           hid_hi[:, c % RING, :].bitcast(F32), ALU.subtract).then_inc(hid_lo_done, 1)
                on_tiles(pool, body)

            @block.vector
            def _(dve):
                def finish(i):
                    dve.wait_ge(multiplied, (i + 1) * NC)
                    dve.wait_ge(biased, (i + 1) * SUB)
                    for u in range(SUB):
                        dve.tensor_tensor(x[:, u, :], o_ps[:, u, :], x[:, u, :], ALU.add).then_inc(summed, 1)

                def body(i, b, s):
                    if at_least(i, 1):
                        finish(i - 1)
                    for c in range(NC):
                        dve.wait_ge(relu_done, i * NC + c + 1)
                        if c >= RING or at_least(i, 1):
                            dve.wait_ge(multiplied, i * NC + c - RING + 1)
                            dve.wait_ge(hid_lo_done, i * NC + c - RING + 1)
                        dve.tensor_copy(hid_hi[:, c % RING, :], hid[:, c % RING, :]).then_inc(hid_hi_done, 1)
                on_tiles(dve, body)
                finish(TILES - 1)

            @block.tensor
            def _(pe):
                def hidden(i, c):
                    if isinstance(i, int) and i == 0:
                        pe.wait_ge(w_lo_done, 2 * c + 1)
                    if c == 0:
                        pe.wait_ge(xt_loaded, (i + 1) * 32)
                    if c >= RING or at_least(i, 1):
                        pe.wait_ge(relu_done, i * NC + c - RING + 1)
                    three(pe, h_ps[:, c % RING, :],
                          [(w1_hi[:, c, k, :], w1_lo[:, c, k, :], x_hi[:, k, :], x_lo[:, k, :])
                           for k in range(KC)], True, True).then_inc(h_filled, 1)

                def multiply(i, c):
                    if isinstance(i, int) and i == 0:
                        pe.wait_ge(w_lo_done, 2 * c + 2)
                    pe.wait_ge(hid_lo_done, i * NC + c + 1)
                    if c == 0 and at_least(i, 1):
                        pe.wait_ge(summed, i * SUB)
                    for u in range(SUB):
                        cols = slice(u * P, (u + 1) * P)
                        last = three(pe, o_ps[:, u, :],
                                     [(hid_hi[:, c % RING, cols], hid_lo[:, c % RING, cols], w2_hi[:, c, :],
                                       w2_lo[:, c, :])], c == 0, c == NC - 1)
                    last.then_inc(multiplied, 1)

                def body(i, b, s):
                    for c in range(NC):
                        hidden(i, c)
                        if c >= LAG:
                            multiply(i, c - LAG)
                    for c in range(NC - LAG, NC):
                        multiply(i, c)
                on_tiles(pe, body)
        sem.clear()


def layer(nc, a, y):
    def dram(name, shape):
        return nc.dram_tensor(name, shape, F32, kind="Internal").ap()

    def tokens(t):
        return t.rearrange("b (s u p) d -> b s p u d", s=HALVES, p=P)

    qk = {n: dram(n, [B, D, S]) for n in ("sq_hi", "sq_lo", "sk_hi", "sk_lo", "cq_hi", "cq_lo", "ck_hi", "ck_lo")}
    vals = {n: dram(n, [B, NG, KT, P, P]) for n in ("sv", "cv")}
    att = {n: dram(n, [B, D, S]) for n in ("s_att", "c_att")}
    x1, x2 = dram("x1", [B, S, D]), dram("x2", [B, S, D])
    xt_hi, xt_lo = dram("xt_hi", [B, HALVES, P, KC, TOK]), dram("xt_lo", [B, HALVES, P, KC, TOK])

    def chan_home(t, m):
        return t.rearrange("b (c p) (s t) -> c b s p t", p=P, s=HALVES)[m]

    def by_group(t):
        return t.rearrange("b (g p) t -> (b g) p t", p=P)

    def tok_home(t):
        return t.rearrange("b g (s u) p c -> b s g p u c", s=HALVES)

    def att_home(t):
        return t.rearrange("b (c p) (s t) -> b s p c t", p=P, s=HALVES)

    with ExitStack() as ctx:
        sb = lambda name, shape, dt=F32: ctx.enter_context(nc.sbuf_tensor(name, shape, dt))
        ident, ident_bf = sb("ident", [P, P]), sb("ident_bf", [P, P], BF16)
        mask_qk, mask_kq = sb("mask_qk", [P, P], BF16), sb("mask_kq", [P, P], BF16)
        keep = sb("keep", [P, S])
        q_bias, k_bias = sb("q_bias", [P, KC]), sb("k_bias", [P, KC])
        made, biases_loaded = (ctx.enter_context(nc.semaphore(n)) for n in ("made", "biases_loaded"))
        with nc.Block() as block:
            @block.gpsimd
            def _(pool):
                tiles = ((ident, 0.0, ALU.not_equal, 1.0, 1, -1), (ident_bf, 0.0, ALU.not_equal, 1.0, 1, -1),
                         (mask_qk, 0.0, ALU.is_ge, CAUSAL, 1, -1), (mask_kq, 0.0, ALU.is_ge, CAUSAL, -1, 1))
                for t, value, *_ in tiles:
                    pool.memset(t[:], value).then_inc(made, 1)
                pool.wait_ge(made, len(tiles))
                for t, _, op, fill, row, col in tiles:
                    pool.affine_select(out=t[:], in_=t[:], compare_op=op, fill=fill, base=0,
                                       pattern=[[col, P]], channel_multiplier=row).then_inc(made, 1)
                pool.wait_ge(made, 2 * len(tiles))

            @block.sync
            def _(sp):
                sp.dma_start(q_bias[:], a["ca_q_b"]).then_inc(biases_loaded, 16)
                sp.dma_start(k_bias[:], a["ca_k_b"]).then_inc(biases_loaded, 16)
                sp.wait_ge(biases_loaded, 32)

        router = Router(nc, keep, tokens(a["x"]), a["n1_g"], a["n1_b"], a["qkv_w"][:, D:2 * D], a["r_w1"],
                        a["r_b1"], a["r_w2"], a["r_b2"])

        self_scale, cross_scale = float(D) ** -0.5, float(DH) ** -0.5

        def self_q(dve, out, psum, s):
            return dve.scalar_tensor_tensor(out=out, in0=psum, scalar=self_scale, in1=keep[:, s * TOK:(s + 1) * TOK],
                                            op0=ALU.mult, op1=ALU.mult)

        def self_k(dve, out, psum, s):
            return dve.tensor_tensor(out, psum, keep[:, s * TOK:(s + 1) * TOK], ALU.mult)

        def cross_q(m):
            return lambda dve, out, psum, s: dve.tensor_scalar(out, psum, q_bias[:, m:m + 1], cross_scale,
                                                               ALU.add, ALU.mult)

        def cross_k(m):
            return lambda dve, out, psum, s: dve.tensor_scalar(out, psum, k_bias[:, m:m + 1], None, ALU.add)

        third = lambda w, n: w[:, n * D:(n + 1) * D]
        projection_stage(
            nc, "d_", ident, tokens(a["ctx"]), weights=[third(a["ca_in_w"], n) for n in (1, 2)],
            chans=[(m, cross_k(m), chan_home(qk["ck_hi"], m), chan_home(qk["ck_lo"], m)) for m in range(KC)],
            toks=(1, a["ca_v_b"], tok_home(vals["cv"])), router=router)
        projection_stage(
            nc, "a_", ident, tokens(a["x"]), norm=(a["n1_g"], a["n1_b"]),
            weights=[third(a["qkv_w"], n) for n in range(3)],
            chans=[(m, self_q, chan_home(qk["sq_hi"], m), chan_home(qk["sq_lo"], m)) for m in range(KC)]
            + [(KC + m, self_k, chan_home(qk["sk_hi"], m), chan_home(qk["sk_lo"], m)) for m in range(KC)],
            toks=(2, None, tok_home(vals["sv"])))
        attention_stage(nc, "b_", ident, *(by_group(qk[n]) for n in ("sq_hi", "sq_lo", "sk_hi", "sk_lo")),
                        vals["sv"].rearrange("b g k p c -> (b g) k p c"), by_group(att["s_att"]),
                        keep, mask_qk, mask_kq, ident_bf)
        projection_stage(
            nc, "c_", ident, tokens(a["x"]), mix=(att_home(att["s_att"]), a["sa_out_w"], a["sa_out_b"], tokens(x1)),
            norm=(a["n2_g"], a["n2_b"]), weights=[third(a["ca_in_w"], 0)],
            chans=[(m, cross_q(m), chan_home(qk["cq_hi"], m), chan_home(qk["cq_lo"], m)) for m in range(KC)])
        attention_stage(nc, "e_", ident, *(by_group(qk[n]) for n in ("cq_hi", "cq_lo", "ck_hi", "ck_lo")),
                        vals["cv"].rearrange("b g k p c -> (b g) k p c"), by_group(att["c_att"]))
        projection_stage(
            nc, "f_", ident, tokens(x1), mix=(att_home(att["c_att"]), a["ca_out_w"], a["ca_out_b"], tokens(x2)),
            norm=(a["n3_g"], a["n3_b"]), keep_xt=(xt_hi, xt_lo))
        mlp_stage(nc, xt_hi, xt_lo, tokens(x2), a["ff_w1"], a["ff_b1"], a["ff_w2"], a["ff_b2"], tokens(y))


def kernel(**inputs):
    import numpy as np
    from concourse import bacc
    from concourse.bass_utils import run_bass_kernel_spmd

    given = {n.removeprefix("L0_xattn_"): np.asarray(v) for n, v in inputs.items()}
    columns = lambda v: np.ascontiguousarray(v.reshape(-1, P).T)
    turned = lambda w: np.ascontiguousarray(w.T)
    ca_b = given["ca_in_b"]
    arrays = {
        "x": given["x"], "ctx": given["ctx_1024"],
        "qkv_w": turned(given["qkv_w"]), "sa_out_w": turned(given["sa_out_w"]), "sa_out_b": given["sa_out_b"],
        "r_w1": turned(given["r_w1"]), "r_b1": columns(given["r_b1"]), "r_w2": turned(given["r_w2"]),
        "r_b2": given["r_b2"],
        "ca_in_w": turned(given["ca_in_w"]), "ca_q_b": columns(ca_b[0:D]), "ca_k_b": columns(ca_b[D:2 * D]),
        "ca_v_b": np.ascontiguousarray(ca_b[2 * D:]), "ca_out_w": turned(given["ca_out_w"]),
        "ca_out_b": given["ca_out_b"],
        "ff_w1": turned(given["ff_w1"]), "ff_b1": columns(given["ff_b1"]), "ff_w2": turned(given["ff_w2"]),
        "ff_b2": given["ff_b2"],
        **{f"n{n}_{c}": columns(given[f"n{n}_{c}"]) for n in (1, 2, 3) for c in "gb"},
    }
    nc = bacc.Bacc("TRN2", target_bir_lowering=False, num_devices=1)
    feeds, aps = {}, {}
    for name, v in arrays.items():
        v = np.ascontiguousarray(v)
        feeds[f"in_{name}"] = v
        aps[name] = nc.dram_tensor(f"in_{name}", v.shape, mybir.dt.from_np(v.dtype), kind="ExternalInput").ap()
    y = nc.dram_tensor("out_y", (B, S, D), F32, kind="ExternalOutput").ap()
    layer(nc, aps, y)
    r = run_bass_kernel_spmd(nc, [feeds], core_ids=[0])
    return r.results[0]["out_y"]
```
